# Optimizing a Trainium2 kernel written in Bass

```python
import numpy as np
import jax
import jax.numpy as jnp

def _softmax(x, axis=-1):
    return jax.nn.softmax(x, axis=axis)

def _gelu(x):
    return jax.nn.gelu(x, approximate=True)

def _silu(x):
    return jax.nn.silu(x)

def _sigmoid(x):
    return jax.nn.sigmoid(x)

def _layernorm(x, axis=-1, eps=1e-05):
    m = jnp.mean(x, axis=axis, keepdims=True)
    v = jnp.var(x, axis=axis, keepdims=True)
    return (x - m) / jnp.sqrt(v + eps)

def _scatter_add(tgt, idx, src, axis=0):
    return tgt.at[idx].add(src)

def _segment_sum(src, seg, n):
    return jax.ops.segment_sum(src, seg, n)
kernel_name = 'mk_adaln_d2_jaxref_r8_82feea'

def setup_inputs(seed: int=0):
    np.random.seed(seed)
    _w = jnp.asarray

    def _L0_attn_setup():
        import math
        import jax, jax.numpy as jnp
        import numpy as np
        H = 16
        LAYER_POS = 12
        LAM_INIT = 0.8 - 0.6 * math.exp(-0.3 * (LAYER_POS - 1))
        LN_EPS = 1e-05

        def _heads(t, B, S, h, d):
            return t.reshape(B, S, h, d).transpose(0, 2, 1, 3)
        key = jax.random.key(seed)
        ks = jax.random.split(key, 12)
        B, S, E = (2, 256, 128)
        d = E // H
        w = 0.02
        return {'x': jax.random.normal(ks[0], (B, S, E), jnp.float32), 'Wq1': jax.random.normal(ks[1], (E, E), jnp.float32) * w, 'Wq2': jax.random.normal(ks[2], (E, E), jnp.float32) * w, 'Wk1': jax.random.normal(ks[3], (E, E), jnp.float32) * w, 'Wk2': jax.random.normal(ks[4], (E, E), jnp.float32) * w, 'Wv': jax.random.normal(ks[5], (E, 2 * E), jnp.float32) * w, 'Wo': jax.random.normal(ks[6], (2 * E, E), jnp.float32) * w, 'lq1': jax.random.normal(ks[7], (H, d), jnp.float32) * 0.1, 'lk1': jax.random.normal(ks[8], (H, d), jnp.float32) * 0.1, 'lq2': jax.random.normal(ks[9], (H, d), jnp.float32) * 0.1, 'lk2': jax.random.normal(ks[10], (H, d), jnp.float32) * 0.1}
    _L0_attn_in = _L0_attn_setup()

    def _L0_ffn_setup():
        import jax, jax.numpy as jnp
        import numpy as np
        B, S, D_MODEL, D_FF = (4, 256, 128, 512)

        def _quantum_transform(hidden, theta, w_real, w_imag):
            imag = w_imag * jnp.sin(theta + hidden * 0.1)
            quantum_phase = jnp.cos(theta) * w_real + jnp.sin(theta) * w_imag
            return hidden + quantum_phase * imag * 0.1
        key = jax.random.key(seed)
        ks = jax.random.split(key, 8)
        return {'x': jax.random.normal(ks[0], (B, S, D_MODEL), dtype=jnp.float32), 'W1': jax.random.normal(ks[1], (D_MODEL, D_FF), dtype=jnp.float32) * (1.0 / np.sqrt(D_MODEL)), 'b1': jnp.zeros((D_FF,), dtype=jnp.float32), 'quantum_phases': jax.random.normal(ks[2], (D_FF,), dtype=jnp.float32) * (2.0 * np.pi), 'quantum_weights_real': jax.random.normal(ks[3], (D_FF,), dtype=jnp.float32) * 0.1, 'quantum_weights_imag': jax.random.normal(ks[4], (D_FF,), dtype=jnp.float32) * 0.1, 'W2': jax.random.normal(ks[5], (D_FF, D_MODEL), dtype=jnp.float32) * (1.0 / np.sqrt(D_FF)), 'b2': jnp.zeros((D_MODEL,), dtype=jnp.float32)}
    _L0_ffn_in = _L0_ffn_setup()
    _L0_c = _w((lambda *s: np.random.randn(*s).astype(np.float32) * 0.05)(8, 128))
    _L0_wmod = _w((lambda *s: np.random.randn(*s).astype(np.float32) * 0.05)(128, 6 * 128) * 128 ** (-0.5))

    def _L1_attn_setup():
        import math
        import jax, jax.numpy as jnp
        import numpy as np
        B_SZ, L_SEQ, D_MODEL, N_STATE = (4, 512, 128, 16)
        DT_RANK = math.ceil(D_MODEL / 16)
        CONV_K = 3
        DT_MIN, DT_MAX = (0.001, 0.1)

        def _inverse_softplus(x):
            return x + jnp.log(1.0 - jnp.exp(-x))

        def _largest_factor_up_to(b, n):
            if n < 2:
                return n
            k = b
            while n % k != 0:
                k -= 1
            return k

        def _ssm_chunked_scan(x, A, Bc, Cc, dt):
            B, L, D = x.shape
            N = A.shape[-1]
            chunk = _largest_factor_up_to(int(math.sqrt(L)), L)
            nc = L // chunk
            r3 = lambda t, F: t.reshape(B, nc, chunk, F).transpose(1, 2, 0, 3)
            xc, dtc = (r3(x, D), r3(dt, D))
            bc, cc = (r3(Bc, N), r3(Cc, N))

            def assoc(lft, rgt):
                g_l, h_l = lft
                g_r, h_r = rgt
                return (g_l * g_r, g_r * h_l + h_r)

            def scan_chunk(carry, ch):
                g0, h0 = carry
                xk, bk, ck, dk = ch
                dA = jnp.exp(jnp.einsum('dn,lbd->lbdn', A, dk))
                dB = jnp.einsum('lbn,lbd,lbd->lbdn', bk, xk, dk)
                gs, hs = jax.lax.associative_scan(assoc, (dA, dB))
                hs = gs * h0 + hs
                yk = jnp.einsum('lbn,lbdn->lbd', ck, hs)
                return ((gs[-1:] * g0, hs[-1:]), yk)
            init = (jnp.ones((1, B, D, N), x.dtype), jnp.zeros((1, B, D, N), x.dtype))
            _, yc = jax.lax.scan(scan_chunk, init, (xc, bc, cc, dtc))
            return yc.transpose(2, 0, 1, 3).reshape(B, L, D)
        key = jax.random.key(seed)
        ks = jax.random.split(key, 6)
        x = jax.random.normal(ks[0], (B_SZ, L_SEQ, D_MODEL), dtype=jnp.float32)
        conv_w = jax.random.normal(ks[1], (CONV_K, D_MODEL), dtype=jnp.float32) / jnp.sqrt(3.0)
        W_bc = jax.random.normal(ks[2], (D_MODEL, 2 * N_STATE), dtype=jnp.float32) / jnp.sqrt(float(D_MODEL))
        b_bc = jnp.zeros((2 * N_STATE,), dtype=jnp.float32)
        W_dt = jax.random.normal(ks[3], (D_MODEL, DT_RANK), dtype=jnp.float32) / jnp.sqrt(float(D_MODEL))
        b_dt = jnp.zeros((DT_RANK,), dtype=jnp.float32)
        W_dtp = jax.random.normal(ks[4], (DT_RANK, D_MODEL), dtype=jnp.float32) / jnp.sqrt(float(DT_RANK))
        u0 = jax.random.uniform(ks[5], (D_MODEL,), dtype=jnp.float32, minval=DT_MIN, maxval=DT_MAX)
        b_dtp = _inverse_softplus(u0)
        A_log = jnp.log(jnp.tile(jnp.arange(1, N_STATE + 1, dtype=jnp.float32)[None, :], (D_MODEL, 1)))
        Dcoeff = jnp.ones((D_MODEL,), dtype=jnp.float32)
        return dict(x=x, conv_w=conv_w, W_bc=W_bc, b_bc=b_bc, W_dt=W_dt, b_dt=b_dt, W_dtp=W_dtp, b_dtp=b_dtp, A_log=A_log, Dcoeff=Dcoeff)
    _L1_attn_in = _L1_attn_setup()

    def _L1_ffn_setup():
        import jax, jax.numpy as jnp
        import numpy as np
        TOP_K = 8
        key = jax.random.key(seed)
        ks = jax.random.split(key, 6)
        B, S, D, F, E = (2, 128, 128, 64, 64)
        x = jax.random.normal(ks[0], (B, S, D), dtype=jnp.float32)
        centroids = jax.random.normal(ks[1], (E, D), dtype=jnp.float32) * 0.05
        expert_biases = jnp.zeros((E,), dtype=jnp.float32)
        Ws_up = jax.random.normal(ks[2], (D, F), dtype=jnp.float32) / np.sqrt(D)
        Ws_down = jax.random.normal(ks[3], (F, D), dtype=jnp.float32) / np.sqrt(F)
        W_up = jax.random.normal(ks[4], (E, D, F), dtype=jnp.float32) / np.sqrt(D)
        W_down = jax.random.normal(ks[5], (E, F, D), dtype=jnp.float32) / np.sqrt(F)
        return {'x': x, 'centroids': centroids, 'expert_biases': expert_biases, 'Ws_up': Ws_up, 'Ws_down': Ws_down, 'W_up': W_up, 'W_down': W_down}
    _L1_ffn_in = _L1_ffn_setup()
    _L1_c = _w((lambda *s: np.random.randn(*s).astype(np.float32) * 0.05)(8, 128))
    _L1_wmod = _w((lambda *s: np.random.randn(*s).astype(np.float32) * 0.05)(128, 6 * 128) * 128 ** (-0.5))
    _d = {'L0_attn_x': _L0_attn_in['x'], 'L0_attn_Wq1': _L0_attn_in['Wq1'], 'L0_attn_Wq2': _L0_attn_in['Wq2'], 'L0_attn_Wk1': _L0_attn_in['Wk1'], 'L0_attn_Wk2': _L0_attn_in['Wk2'], 'L0_attn_Wv': _L0_attn_in['Wv'], 'L0_attn_Wo': _L0_attn_in['Wo'], 'L0_attn_lq1': _L0_attn_in['lq1'], 'L0_attn_lk1': _L0_attn_in['lk1'], 'L0_attn_lq2': _L0_attn_in['lq2'], 'L0_attn_lk2': _L0_attn_in['lk2'], 'L0_ffn_W1': _L0_ffn_in['W1'], 'L0_ffn_b1': _L0_ffn_in['b1'], 'L0_ffn_quantum_phases': _L0_ffn_in['quantum_phases'], 'L0_ffn_quantum_weights_real': _L0_ffn_in['quantum_weights_real'], 'L0_ffn_quantum_weights_imag': _L0_ffn_in['quantum_weights_imag'], 'L0_ffn_W2': _L0_ffn_in['W2'], 'L0_ffn_b2': _L0_ffn_in['b2'], 'L0_c': _L0_c, 'L0_wmod': _L0_wmod, 'L1_attn_conv_w': _L1_attn_in['conv_w'], 'L1_attn_W_bc': _L1_attn_in['W_bc'], 'L1_attn_b_bc': _L1_attn_in['b_bc'], 'L1_attn_W_dt': _L1_attn_in['W_dt'], 'L1_attn_b_dt': _L1_attn_in['b_dt'], 'L1_attn_W_dtp': _L1_attn_in['W_dtp'], 'L1_attn_b_dtp': _L1_attn_in['b_dtp'], 'L1_attn_A_log': _L1_attn_in['A_log'], 'L1_attn_Dcoeff': _L1_attn_in['Dcoeff'], 'L1_ffn_centroids': _L1_ffn_in['centroids'], 'L1_ffn_expert_biases': _L1_ffn_in['expert_biases'], 'L1_ffn_Ws_up': _L1_ffn_in['Ws_up'], 'L1_ffn_Ws_down': _L1_ffn_in['Ws_down'], 'L1_ffn_W_up': _L1_ffn_in['W_up'], 'L1_ffn_W_down': _L1_ffn_in['W_down'], 'L1_c': _L1_c, 'L1_wmod': _L1_wmod}
    _x0 = _d['L0_attn_x']
    _d['L0_attn_x'] = jax.random.normal(jax.random.fold_in(jax.random.key(seed), 1), (8, 512, 128), dtype=_x0.dtype)
    del _x0
    return _d

def reference(L0_attn_x, L0_attn_Wq1, L0_attn_Wq2, L0_attn_Wk1, L0_attn_Wk2, L0_attn_Wv, L0_attn_Wo, L0_attn_lq1, L0_attn_lk1, L0_attn_lq2, L0_attn_lk2, L0_ffn_W1, L0_ffn_b1, L0_ffn_quantum_phases, L0_ffn_quantum_weights_real, L0_ffn_quantum_weights_imag, L0_ffn_W2, L0_ffn_b2, L0_c, L0_wmod, L1_attn_conv_w, L1_attn_W_bc, L1_attn_b_bc, L1_attn_W_dt, L1_attn_b_dt, L1_attn_W_dtp, L1_attn_b_dtp, L1_attn_A_log, L1_attn_Dcoeff, L1_ffn_centroids, L1_ffn_expert_biases, L1_ffn_Ws_up, L1_ffn_Ws_down, L1_ffn_W_up, L1_ffn_W_down, L1_c, L1_wmod):

    def _L0_attn_ref(x, Wq1, Wq2, Wk1, Wk2, Wv, Wo, lq1, lk1, lq2, lk2):
        import math
        import jax, jax.numpy as jnp
        import numpy as np
        H = 16
        LAYER_POS = 12
        LAM_INIT = 0.8 - 0.6 * math.exp(-0.3 * (LAYER_POS - 1))
        LN_EPS = 1e-05

        def _heads(t, B, S, h, d):
            return t.reshape(B, S, h, d).transpose(0, 2, 1, 3)
        B, S, E = x.shape
        d = E // H
        scale = 1.0 / math.sqrt(d)
        q1 = _heads(x @ Wq1, B, S, H, d)
        q2 = _heads(x @ Wq2, B, S, H, d)
        k1 = _heads(x @ Wk1, B, S, H, d)
        k2 = _heads(x @ Wk2, B, S, H, d)
        v = _heads(x @ Wv, B, S, H, 2 * d)
        causal = jnp.tril(jnp.ones((S, S), dtype=bool))
        neg_inf = jnp.float32(-jnp.inf)
        s1 = jnp.einsum('bhqd,bhkd->bhqk', q1, k1) * scale
        s2 = jnp.einsum('bhqd,bhkd->bhqk', q2, k2) * scale
        a1 = jax.nn.softmax(jnp.where(causal, s1, neg_inf), axis=-1)
        a2 = jax.nn.softmax(jnp.where(causal, s2, neg_inf), axis=-1)
        lam = jnp.exp(jnp.sum(lq1 * lk1, axis=-1)) - jnp.exp(jnp.sum(lq2 * lk2, axis=-1)) + LAM_INIT
        comb = a1 - lam[None, :, None, None] * a2
        out = jnp.einsum('bhqk,bhkv->bhqv', comb, v)
        mu = jnp.mean(out, axis=-1, keepdims=True)
        var = jnp.mean(jnp.square(out - mu), axis=-1, keepdims=True)
        normed = (out - mu) * jax.lax.rsqrt(var + LN_EPS)
        scaled = normed * (1.0 - LAM_INIT)
        merged = scaled.transpose(0, 2, 1, 3).reshape(B, S, 2 * E)
        return merged @ Wo

    def _L0_ffn_ref(x, W1, b1, quantum_phases, quantum_weights_real, quantum_weights_imag, W2, b2):
        import jax, jax.numpy as jnp
        import numpy as np
        B, S, D_MODEL, D_FF = (4, 256, 128, 512)

        def _quantum_transform(hidden, theta, w_real, w_imag):
            imag = w_imag * jnp.sin(theta + hidden * 0.1)
            quantum_phase = jnp.cos(theta) * w_real + jnp.sin(theta) * w_imag
            return hidden + quantum_phase * imag * 0.1
        hidden = jnp.einsum('bsd,df->bsf', x, W1) + b1
        q = _quantum_transform(hidden, quantum_phases, quantum_weights_real, quantum_weights_imag)
        act = jax.nn.relu(q)
        return jnp.einsum('bsf,fd->bsd', act, W2) + b2

    def _L1_attn_ref(x, conv_w, W_bc, b_bc, W_dt, b_dt, W_dtp, b_dtp, A_log, Dcoeff):
        import math
        import jax, jax.numpy as jnp
        import numpy as np
        B_SZ, L_SEQ, D_MODEL, N_STATE = (4, 512, 128, 16)
        DT_RANK = math.ceil(D_MODEL / 16)
        CONV_K = 3
        DT_MIN, DT_MAX = (0.001, 0.1)

        def _inverse_softplus(x):
            return x + jnp.log(1.0 - jnp.exp(-x))

        def _largest_factor_up_to(b, n):
            if n < 2:
                return n
            k = b
            while n % k != 0:
                k -= 1
            return k

        def _ssm_chunked_scan(x, A, Bc, Cc, dt):
            B, L, D = x.shape
            N = A.shape[-1]
            chunk = _largest_factor_up_to(int(math.sqrt(L)), L)
            nc = L // chunk
            r3 = lambda t, F: t.reshape(B, nc, chunk, F).transpose(1, 2, 0, 3)
            xc, dtc = (r3(x, D), r3(dt, D))
            bc, cc = (r3(Bc, N), r3(Cc, N))

            def assoc(lft, rgt):
                g_l, h_l = lft
                g_r, h_r = rgt
                return (g_l * g_r, g_r * h_l + h_r)

            def scan_chunk(carry, ch):
                g0, h0 = carry
                xk, bk, ck, dk = ch
                dA = jnp.exp(jnp.einsum('dn,lbd->lbdn', A, dk))
                dB = jnp.einsum('lbn,lbd,lbd->lbdn', bk, xk, dk)
                gs, hs = jax.lax.associative_scan(assoc, (dA, dB))
                hs = gs * h0 + hs
                yk = jnp.einsum('lbn,lbdn->lbd', ck, hs)
                return ((gs[-1:] * g0, hs[-1:]), yk)
            init = (jnp.ones((1, B, D, N), x.dtype), jnp.zeros((1, B, D, N), x.dtype))
            _, yc = jax.lax.scan(scan_chunk, init, (xc, bc, cc, dtc))
            return yc.transpose(2, 0, 1, 3).reshape(B, L, D)
        xp = jnp.pad(x, ((0, 0), (1, 1), (0, 0)))
        u = xp[:, :-2] * conv_w[0] + xp[:, 1:-1] * conv_w[1] + xp[:, 2:] * conv_w[2]
        u = jax.nn.silu(u)
        BC = u @ W_bc + b_bc
        Bcoeff, Ccoeff = jnp.split(BC, 2, axis=-1)
        A = -jnp.exp(A_log)
        dt = jax.nn.softplus((u @ W_dt + b_dt) @ W_dtp + b_dtp)
        y = _ssm_chunked_scan(x, A, Bcoeff, Ccoeff, dt)
        return y + x * Dcoeff

    def _L1_ffn_ref(x, centroids, expert_biases, Ws_up, Ws_down, W_up, W_down):
        import jax, jax.numpy as jnp
        import numpy as np
        TOP_K = 8
        B, S, D = x.shape
        E = centroids.shape[0]
        T = B * S
        xf = x.reshape(T, D)
        shared = jax.nn.silu(xf @ Ws_up) @ Ws_down
        aff = xf @ centroids.T
        biased = aff + expert_biases
        _, idx = jax.lax.top_k(biased, TOP_K)
        sel = jnp.take_along_axis(aff, idx, axis=1)
        w = jax.nn.sigmoid(sel)
        w = w / (jnp.sum(w, axis=-1, keepdims=True) + 1e-08)
        cw = jnp.zeros((T, E), dtype=x.dtype).at[jnp.arange(T)[:, None], idx].add(w)
        h = jax.nn.silu(jnp.einsum('td,edf->etf', xf, W_up))
        y = jnp.einsum('etf,efd->etd', h, W_down)
        routed = jnp.einsum('etd,te->td', y, cw)
        return (shared + routed).reshape(B, S, D)
    x = L0_attn_x
    mod = (_silu(L0_c) @ L0_wmod).reshape(L0_c.shape[0], 6, 1, -1)
    sa, ca, ga, sb, cb, gb = (mod[:, 0], mod[:, 1], mod[:, 2], mod[:, 3], mod[:, 4], mod[:, 5])
    ga = (2 * (ga >= 0) - 1) * jnp.maximum(jnp.abs(ga), 0.25)
    gb = (2 * (gb >= 0) - 1) * jnp.maximum(jnp.abs(gb), 0.25)
    h = _layernorm(x, axis=-1) * (1 + ca) + sa
    x = x + ga * _L0_attn_ref(h, L0_attn_Wq1, L0_attn_Wq2, L0_attn_Wk1, L0_attn_Wk2, L0_attn_Wv, L0_attn_Wo, L0_attn_lq1, L0_attn_lk1, L0_attn_lq2, L0_attn_lk2)
    h = _layernorm(x, axis=-1) * (1 + cb) + sb
    x = x + gb * _L0_ffn_ref(h, L0_ffn_W1, L0_ffn_b1, L0_ffn_quantum_phases, L0_ffn_quantum_weights_real, L0_ffn_quantum_weights_imag, L0_ffn_W2, L0_ffn_b2)
    mod = (_silu(L1_c) @ L1_wmod).reshape(L1_c.shape[0], 6, 1, -1)
    sa, ca, ga, sb, cb, gb = (mod[:, 0], mod[:, 1], mod[:, 2], mod[:, 3], mod[:, 4], mod[:, 5])
    ga = (2 * (ga >= 0) - 1) * jnp.maximum(jnp.abs(ga), 0.25)
    gb = (2 * (gb >= 0) - 1) * jnp.maximum(jnp.abs(gb), 0.25)
    h = _layernorm(x, axis=-1) * (1 + ca) + sa
    x = x + ga * _L1_attn_ref(h, L1_attn_conv_w, L1_attn_W_bc, L1_attn_b_bc, L1_attn_W_dt, L1_attn_b_dt, L1_attn_W_dtp, L1_attn_b_dtp, L1_attn_A_log, L1_attn_Dcoeff)
    h = _layernorm(x, axis=-1) * (1 + cb) + sb
    x = x + gb * _L1_ffn_ref(h, L1_ffn_centroids, L1_ffn_expert_biases, L1_ffn_Ws_up, L1_ffn_Ws_down, L1_ffn_W_up, L1_ffn_W_down)
    return x

_drawn_inputs = setup_inputs


def setup_inputs(seed=0):
    import zlib

    import numpy as np

    out = dict(_drawn_inputs(seed))
    spreads = {'L0_ffn_b1': (0.0, 0.419),
     'L0_ffn_b2': (0.0, 0.303),
     'L1_attn_b_bc': (0.0, 2.0),
     'L1_attn_b_dt': (0.0, 2.0),
     'L1_attn_Dcoeff': (1.0, 0.2),
     'L1_ffn_expert_biases': (0.0, 0.339)}
    factors = {'L0_attn_Wq1': 8.0,
     'L0_attn_Wq2': 8.0,
     'L0_attn_Wk1': 8.0,
     'L0_attn_Wk2': 8.0,
     'L0_attn_Wv': 3.922,
     'L0_attn_Wo': 3.939,
     'L0_attn_lq1': 8.0,
     'L0_attn_lk1': 8.0,
     'L0_attn_lq2': 8.0,
     'L0_attn_lk2': 8.0,
     'L0_ffn_quantum_phases': 48.618,
     'L0_ffn_quantum_weights_real': 64.0,
     'L0_ffn_quantum_weights_imag': 39.281,
     'L1_attn_b_dtp': 9.406,
     'L1_attn_conv_w': 3.296,
     'L1_attn_W_bc': 3.003,
     'L1_attn_W_dt': 5.299,
     'L1_attn_W_dtp': 3.404,
     'L1_attn_A_log': 5.775}
    for name, (base, spread) in spreads.items():
        noise = np.random.default_rng([zlib.crc32(name.encode()), seed]).standard_normal(out[name].shape)
        drawn = base * np.exp(spread * noise) if base else spread * noise
        out[name] = jnp.asarray(drawn.astype(out[name].dtype))
    for name, factor in factors.items():
        out[name] = (out[name] * factor).astype(out[name].dtype)
    return out
```

```python
import math
from contextlib import ExitStack

import numpy as np
import concourse.bass as bass
from concourse import mybir

F32 = mybir.dt.float32
BF16 = mybir.dt.bfloat16
FP16 = mybir.dt.float16
I32 = mybir.dt.int32
ALU = mybir.AluOpType
ACT = mybir.ActivationFunctionType
AX = mybir.AxisListType.X

B, S, D = 8, 512, 128
P = 128
TILES = S // P
H, HD = 16, 8
VD = 2 * HD
LAM_INIT = 0.8 - 0.6 * math.exp(-0.3 * 11)
EPS = 1e-5
FF = 512
N = 16
RANK = 8
E, EF, TOPK = 64, 64, 8
ET = E * EF // P

NEG = -3.0e38
INV_2PI = 1.0 / (2.0 * math.pi)
ROUND = 1.5 * 2.0 ** 23
TWO_PI_HI = 6.28125
TWO_PI_MID = float(np.float32(np.round((2 * math.pi - TWO_PI_HI) * 2.0 ** 21) / 2.0 ** 21))
TWO_PI_LO = 2 * math.pi - TWO_PI_HI - TWO_PI_MID
PI_BELOW = 3.1415925


class Chain:

    def __init__(self, eng, sem, base=0, passed=None):
        self.eng, self.sem, self.base, self.n, self.passed = eng, sem, base, 0, passed

    def link(self, ins):
        ins.then_inc(self.sem, 1)
        self.n += 1
        self.eng.wait_ge(self.sem, self.base + self.n)
        if self.passed is not None:
            self.eng.sem_inc(self.passed, 1)


def rsqrt_steps(dve, link, v, half, y, t):
    link(dve.tensor_scalar(t.bitcast(I32), v.bitcast(I32), 1, None, ALU.logical_shift_right))
    link(dve.tensor_scalar(y.bitcast(I32), t.bitcast(I32), -1.0, 1597463007.0, ALU.mult, ALU.add))
    link(dve.tensor_scalar(half, v, -0.5, None, ALU.mult))
    for _ in range(3):
        link(dve.tensor_tensor(t, y, y, ALU.mult))
        link(dve.tensor_tensor(t, t, half, ALU.mult))
        link(dve.scalar_tensor_tensor(y, t, 1.5, y, ALU.add, ALU.mult))


RSQRT_LINKS = 3 + 3 * 3


def build(nc, d, out):
    with ExitStack() as top:
        keep = shared_tiles(nc, top)
        setup(nc, d, keep)
        attention(nc, d, keep)
        ffn(nc, d, keep)
        scan(nc, d, keep)
        experts(nc, d, keep, out)


class Keep:
    pass


def shared_tiles(nc, ctx):
    k = Keep()

    def sb(name, shape, dt=F32):
        return ctx.enter_context(nc.sbuf_tensor(name, shape, dt))

    k.x = sb("x_tok", [P, B * TILES, D])
    k.ident = sb("ident", [P, P])
    k.identb = sb("identb", [P, P], BF16)
    k.ones = sb("ones", [P, P])
    k.mod = sb("mod", [P, 2, 6, B])
    k.gate_a0 = sb("gate_a0", [P, B, D])
    k.gate_b0 = sb("gate_b0", [P, B, D])
    k.neg_lam = sb("neg_lam", [P, H])
    k.stats = sb("stats", [P, B * TILES, 2])
    k.rstd = sb("rstd", [P, B * TILES])
    k.half = sb("half", [P, B * TILES])
    k.tmp = sb("rs_tmp", [P, B * TILES])
    k.bn = sb("bn", [P, B * TILES, 6])
    return k


def setup(nc, d, k):
    with ExitStack() as ctx:
        def sb(name, shape, dt=F32):
            return ctx.enter_context(nc.sbuf_tensor(name, shape, dt))

        def sem(name):
            return ctx.enter_context(nc.semaphore(name))

        c = sb("c", [B, 2, D])
        sc = sb("silu_c", [B, 2, D])
        cT = sb("silu_cT", [P, 2, B])
        cTb = sb("silu_cTb", [P, B, P])
        wmod = sb("wmod", [P, 2, 6 * D])
        lq = sb("lq", [1, 4, H * HD])
        lp = sb("lp", [1, 2, H * HD])
        ls = sb("ls", [1, 2, H])
        le = sb("le", [1, 2, H])
        lr = sb("lr", [1, H])
        gs = sb("gs", [P, 2, 2, 2, B])
        gsr = sb("gsr", [P, 2, B, D])
        psum_c = ctx.enter_context(nc.psum_tensor("psum_c", [P, 512], F32))
        psum_m = ctx.enter_context(nc.psum_tensor("psum_m", [P, 512], F32))
        psum_l = ctx.enter_context(nc.psum_tensor("psum_l", [P, 512], F32))
        psum_g = ctx.enter_context(nc.psum_tensor("psum_g", [P, 4, 512], F32))
        x_loaded, w_loaded = sem("x_loaded"), sem("w_loaded")
        consts = sem("setup_consts")
        silu_done, cT_psum, cT_ready, mod_psum, gate_psum = (
            sem("silu_done"), sem("cT_psum"), sem("cT_ready"), sem("mod_psum"), sem("gate_psum"))
        lp_ready, le_ready, lr_ready, lam_psum = sem("lp_ready"), sem("le_ready"), sem("lr_ready"), sem("lam_psum")
        dve_chain = sem("setup_dve")
        block = ctx.enter_context(nc.Block())

        @block.sync
        def _(sp):
            for l, name in enumerate(("L0_c", "L1_c")):
                sp.dma_start(c[:, l, :], d[name]).then_inc(w_loaded, 16)
            for l, name in enumerate(("L0_wmod", "L1_wmod")):
                sp.dma_start(wmod[:, l, :], d[name]).then_inc(w_loaded, 16)
            for j, name in enumerate(("lq1", "lk1", "lq2", "lk2")):
                sp.dma_start(lq[0:1, j, :], d["L0_attn_" + name].rearrange("(a h) d -> a (h d)", a=1)).then_inc(w_loaded, 16)
            sp.dma_start(k.x[:, :, :], d["L0_attn_x"].rearrange("b (i p) d -> p (b i) d", p=P)).then_inc(x_loaded, 16)

        @block.gpsimd
        def _(pool):
            pool.memset(k.ident[:, :], 0.0).then_inc(consts, 1)
            pool.memset(k.identb[:, :], 0.0).then_inc(consts, 1)
            pool.memset(k.ones[:, :], 1.0).then_inc(consts, 1)
            pool.wait_ge(consts, 3)
            for m in (k.ident, k.identb):
                pool.affine_select(out=m[:, :], in_=m[:, :], compare_op=ALU.not_equal, fill=1.0, base=0,
                                   pattern=[[-1, P]], channel_multiplier=1).then_inc(consts, 1)

        @block.scalar
        def _(act):
            act.wait_ge(w_loaded, 16 * 8)
            act.activation(sc[:, :, :], c[:, :, :], ACT.Silu).then_inc(silu_done, 1)
            act.wait_ge(lp_ready, 1)
            act.activation(le[0:1, :, :], ls[0:1, :, :], ACT.Exp).then_inc(le_ready, 1)

        @block.tensor
        def _(pe):
            pe.wait_ge(consts, 5)
            pe.wait_ge(silu_done, 1)
            for l in range(2):
                mm = pe.transpose(psum_c[:, 8 * l:8 * l + B], sc[:, l, :], k.ident[0:B, 0:B])
            mm.then_inc(cT_psum, 1)
            pe.wait_ge(cT_ready, 2)
            for l in range(2):
                for j in range(6):
                    at = (6 * l + j) * B
                    mm = pe.matmul(psum_m[:, at:at + B], wmod[:, l, j * D:(j + 1) * D], cT[:, l, :], start=True, stop=True)
            mm.then_inc(mod_psum, 1)
            for n, j in enumerate((2, 5)):
                for b in range(B):
                    mm = pe.matmul(psum_g[:, 2 * n + b // 4, (b % 4) * D:(b % 4 + 1) * D], cTb[:, b, :],
                                   wmod[:, 0, j * D:(j + 1) * D], start=True, stop=True)
            mm.then_inc(gate_psum, 1)
            pe.wait_ge(lr_ready, 1)
            pe.matmul(psum_l[:, 0:H], k.ones[0:1, :], lr[0:1, :], start=True, stop=True).then_inc(lam_psum, 1)

        @block.vector
        def _(dve):
            link = Chain(dve, dve_chain).link
            dve.wait_ge(w_loaded, 16 * 8)
            for j in range(2):
                link(dve.tensor_tensor(lp[0:1, j, :], lq[0:1, 2 * j, :], lq[0:1, 2 * j + 1, :], ALU.mult))
            dve.tensor_reduce(ls[0:1, :, :], lp[0:1, :, :].rearrange("a j (h d) -> a j h d", d=HD), AX, ALU.add).then_inc(lp_ready, 1)
            dve.wait_ge(cT_psum, 1)
            dve.tensor_copy(cT[:, :, :], psum_c[:, 0:2 * B].rearrange("p (l b) -> p l b", l=2)).then_inc(cT_ready, 1)
            dve.tensor_copy(cTb[:, :, :], psum_c[:, 0:B].unsqueeze(2).broadcast_to([P, B, P])).then_inc(cT_ready, 1)
            dve.wait_ge(le_ready, 1)
            dve.scalar_tensor_tensor(lr[0:1, :], le[0:1, 1, :], -LAM_INIT, le[0:1, 0, :], ALU.add, ALU.subtract).then_inc(lr_ready, 1)
            dve.wait_ge(mod_psum, 1)
            link(dve.tensor_copy(k.mod[:, :, :, :], psum_m[:, 0:12 * B].rearrange("p (l j b) -> p l j b", l=2, j=6)))
            for j in (1, 4):
                link(dve.tensor_scalar(k.mod[:, :, j, :], k.mod[:, :, j, :], 1.0, None, ALU.add))
            for n, j in enumerate((2, 5)):
                g = k.mod[:, :, j, :]
                link(dve.scalar_tensor_tensor(gs[:, 0, n, :, :], g, -1.0, g, ALU.mult, ALU.max))
                link(dve.tensor_scalar(gs[:, 0, n, :, :], gs[:, 0, n, :, :], 0.25, None, ALU.max))
                link(dve.tensor_scalar(gs[:, 1, n, :, :], g, 0.0, 2.0, ALU.is_ge, ALU.mult))
                link(dve.scalar_tensor_tensor(g, gs[:, 1, n, :, :], -1.0, gs[:, 0, n, :, :], ALU.add, ALU.mult))
            dve.wait_ge(gate_psum, 1)
            for n, gate in enumerate((k.gate_a0, k.gate_b0)):
                g = gate[:, :, :].rearrange("p b d -> p (b d)")
                s0, s1 = (gsr[:, j, :, :].rearrange("p b d -> p (b d)") for j in range(2))
                link(dve.tensor_copy(g, psum_g[:, 2 * n:2 * n + 2, :].rearrange("p b d -> p (b d)")))
                link(dve.scalar_tensor_tensor(s0, g, -1.0, g, ALU.mult, ALU.max))
                link(dve.tensor_scalar(s0, s0, 0.25, None, ALU.max))
                link(dve.tensor_scalar(s1, g, 0.0, 2.0, ALU.is_ge, ALU.mult))
                link(dve.scalar_tensor_tensor(g, s1, -1.0, s0, ALU.add, ALU.mult))
            dve.wait_ge(lam_psum, 1)
            link(dve.tensor_copy(k.neg_lam[:, :], psum_l[:, 0:H]))
            dve.wait_ge(x_loaded, 16)
            for t in range(B * TILES):
                last = dve.bn_stats(k.bn[:, t, :], k.x[:, t, :])
            link(last)
            for t in range(B * TILES):
                last = dve.bn_aggr(k.stats[:, t, :], k.bn[:, t, :])
            link(last)
            v = k.stats[:, :, 1]
            link(dve.tensor_scalar(v, v, EPS, None, ALU.add))
            link(dve.tensor_copy(k.half[:, :], v))
            rsqrt_steps(dve, link, k.half[:, :], k.bn[:, :, 0], k.rstd[:, :], k.tmp[:, :])


GROUPS = 8
MAPS = 4
SROWS = 6 * HD
NROWS = 3
KROWS = 96
UNITS = 10
SCALE = 1.0 / math.sqrt(HD)


def attention(nc, d, k):
    qk_dram = nc.dram_tensor("qk_parts", [B, 2, 3, D, 2, S], BF16).ap()
    neg_dram = nc.dram_tensor("neg_max", [B, GROUPS, 3, MAPS, S], BF16).ap()
    v_dram = nc.dram_tensor("v_ones", [B, GROUPS, S, 64], F32).ap()
    with ExitStack() as ctx:
        def sb(name, shape, dt=F32):
            return ctx.enter_context(nc.sbuf_tensor(name, shape, dt))

        def ps(name):
            return ctx.enter_context(nc.psum_tensor(name, [P, 512], F32))

        def sem(name):
            return ctx.enter_context(nc.semaphore(name))

        wqk = sb("wqk", [P, 4, D])
        wv = sb("wv", [P, H * VD])
        wo = sb("wo", [P, 2, D])
        causal = sb("causal", [P, P], BF16)
        xn = sb("xn", [P, D])
        hT = sb("hT", [P, P])
        parts = sb("parts", [P, 3, 4, P], BF16)
        res = sb("res", [P, 4, P])
        vst = sb("vst", [P, H, 32])
        q1, k1, q2, k2 = (sb(n, [KROWS, 2, MAPS, S], BF16) for n in ("q1s", "k1s", "q2s", "k2s"))
        vs = sb("vs", [P, 2, TILES, 2, 32])
        pT = sb("pT", [P, 2, UNITS, 512])
        bmax = sb("bmax", [P, 2 * H, 10])
        qmax = sb("qmax", [P, TILES, 2 * H])
        nparts = sb("nparts", [2 * H, 3, S], BF16)
        nres = sb("nres", [2 * H, S])
        o_sb = sb("o_sb", [P, 2, S])
        oT = sb("oT", [P, 2, TILES, 2 * H, VD + 1])
        rc = sb("rc", [P, H, 2])
        o1, o2 = sb("o1", [P, H, VD]), sb("o2", [P, H, VD])
        og, oc, sq = sb("og", [P, H, VD]), sb("oc", [P, H, VD]), sb("sq", [P, H, VD])
        msum, vsum, vhalf, orstd, otmp = (sb(n, [P, H]) for n in ("msum", "vsum", "vhalf", "orstd", "otmp"))
        merged = sb("merged", [P, H * VD])
        mT = sb("mT", [P, 2, P])
        gated = sb("gated", [P, D])
        p1b = [ps(f"p1b{i}") for i in range(2)]
        p2b = [ps(f"p2b{i}") for i in range(2)]
        ob, otb, prepb, postb = ps("ob"), ps("otb"), ps("prepb"), ps("postb")

        w_loaded, slots_set = sem("attn_w"), sem("slots_set")
        xn_ready, xnT_done, hT_ready, qk_done, hi_ready, res_ready, v_done, v_ready, split_ready = (
            sem(n) for n in ("xn_ready", "xnT_done", "hT_ready", "qk_done", "hi_ready", "res_ready", "v_done",
                             "v_ready", "split_ready"))
        mid_ready, passed = sem("mid_ready"), sem("passed")
        qkv_saved = sem("qkv_saved")
        first_loaded = [sem(f"first_loaded{s}") for s in range(2)]
        first_unit, first_read = sem("first_unit"), sem("first_read")
        second_loaded = [sem(f"second_loaded{s}") for s in range(2)]
        v_loaded = [sem(f"v_loaded{s}") for s in range(2)]
        second_unit, exp_done, masked, av_done, o_read, oT_done, oT_read = (
            sem(n) for n in ("second_unit", "exp_done", "masked", "av_done", "o_read", "oT_done", "oT_read"))
        qmax_ready, neg_psum, neg_read, neg_ready, neg_saved = (
            sem(n) for n in ("qmax_ready", "neg_psum", "neg_read", "neg_ready", "neg_saved"))
        rc_ready, og_ready, merged_ready, mT_done, mT_ready, wo_done, post_done = (
            sem(n) for n in ("rc_ready", "og_ready", "merged_ready", "mT_done", "mT_ready", "wo_done", "post_done"))
        pool_post, dve_post, dve_max = sem("pool_post"), sem("dve_post"), sem("dve_max")
        block = ctx.enter_context(nc.Block())

        CREDITS = {first_unit: 2 * UNITS, first_read: 2, second_unit: 2 * UNITS, exp_done: 2, av_done: 2, o_read: 1,
                   oT_done: 2, oT_read: 1, v_done: 1, v_ready: 1, qkv_saved: 16, split_ready: 1, neg_read: 2,
                   neg_saved: 16, merged_ready: 1, og_ready: 1, wo_done: 1, post_done: 1}
        W_LOADS = 6 * 16
        QKV_SAVES = 13 * 16
        FIRST_LOADS, SECOND_LOADS, NEG_SAVES = 12 * 16, 13 * 16, GROUPS * 16

        def rounds(eng, step, tail=None):
            for r0, r1 in ((-1, 0), (0, 1), (1, 2), (2, 7), (7, 8), (8, 9), (9, 10)):
                parts_on = dict(first=0 <= r0 < B, second=1 <= r0 <= B, post=r0 >= 2, prep=r0 + 1 < B)
                if r1 - r0 > 1:
                    with eng.Fori(r0, r1) as r:
                        with eng.Fori(0, TILES) as i:
                            step(r, i, **parts_on)
                        if tail and parts_on["first"]:
                            tail(r)
                else:
                    with eng.Fori(0, TILES) as i:
                        step(r0, i, **parts_on)
                    if tail and parts_on["first"]:
                        tail(r0)

        @block.sync
        def _(sp):
            for j, name in enumerate(("Wq1", "Wq2", "Wk1", "Wk2")):
                sp.dma_start(wqk[:, j, :], d["L0_attn_" + name]).then_inc(w_loaded, 16)
            sp.dma_start(wv[:, :], d["L0_attn_Wv"]).then_inc(w_loaded, 16)
            sp.dma_start(wo[:, :, :], d["L0_attn_Wo"].rearrange("(c p) n -> p c n", p=P)).then_inc(w_loaded, 16)
            sp.wait_ge(slots_set, 6)

            def stacks(q, kk, slot, b, g, done):
                for t, tile, order in ((0, q, (0, 0, 0, 1, 1, 2)), (1, kk, (0, 1, 2, 0, 1, 0))):
                    for n, part in enumerate(order):
                        src = qk_dram[b, t, part, bass.ds(g * 2 * HD, 2 * HD), :, :]
                        sp.dma_start(tile[n * HD:(n + 1) * HD, slot, :, :].rearrange("r (h j) t -> r h (j t)", h=2),
                                     src.rearrange("(h r) j t -> r h (j t)", h=2)).then_inc(done, 16)

            def step(r, i, first, second, post, prep):
                for a in range(2):
                    g = i * 2 + a
                    if first:
                        G = r * GROUPS + g
                        sp.wait_ge(qkv_saved, (r + 1) * TILES * QKV_SAVES + 16)
                        sp.wait_ge(first_unit, (G + 1) * UNITS)
                        stacks(q1, k1, a, r, g, first_loaded[a])
                    if second:
                        G = (r - 1) * GROUPS + g
                        sp.wait_ge(neg_saved, r * NEG_SAVES + 16)
                        sp.wait_ge(second_unit, (G + 1) * UNITS)
                        sp.dma_start(q2[SROWS:SROWS + NROWS, a, :, :].rearrange("p m t -> p (m t)"),
                                     neg_dram[r - 1, g, :, :, :].rearrange("s m t -> s (m t)")).then_inc(second_loaded[a], 16)
                        stacks(q2, k2, a, r - 1, g, second_loaded[a])
                        sp.wait_ge(av_done, G + 1)
                        sp.dma_start(vs[:, a, :, :, :].rearrange("p c h e -> p c (h e)"),
                                     v_dram[r - 1, g, :, :].rearrange("(c p) e -> p c e", p=P)).then_inc(v_loaded[a], 16)
                if prep:
                    T = (r + 1) * TILES + i
                    sp.wait_ge(split_ready, T + 2)
                    for t in range(2):
                        for j in range(2):
                            for s in range(3):
                                sp.dma_start(qk_dram[r + 1, t, s, :, j, bass.ds(i * P, P)], parts[:, s, 2 * t + j, :]).then_inc(qkv_saved, 16)
                    sp.wait_ge(v_ready, T + 2)
                    sp.dma_start(v_dram[r + 1, :, bass.ds(i * P, P), :].rearrange("g p e -> p g e"),
                                 vst[:, :, :].rearrange("p (g h) e -> p g (h e)", h=2)).then_inc(qkv_saved, 16)

            def tail(r):
                sp.wait_ge(neg_ready, r + 1)
                for g in range(GROUPS):
                    sp.dma_start(neg_dram[r, g, :, :, :].rearrange("s m t -> m s t"),
                                 nparts[g * MAPS:(g + 1) * MAPS, :, :]).then_inc(neg_saved, 16)

            rounds(sp, step, tail)
            sp.wait_ge(post_done, B * TILES + 1)

        @block.gpsimd
        def _(pool):
            pool.memset(q1[:, :, :, :], 0.0).then_inc(slots_set, 1)
            pool.memset(q2[:, :, :, :], 0.0).then_inc(slots_set, 1)
            pool.memset(k1[:, :, :, :], 1.0).then_inc(slots_set, 1)
            pool.memset(k2[:, :, :, :], 1.0).then_inc(slots_set, 1)
            pool.memset(causal[:, :], 0.0).then_inc(pool_post, 1)
            pool.wait_ge(pool_post, 1)
            pool.affine_select(out=causal[:, :], in_=causal[:, :], compare_op=ALU.is_ge, fill=NEG, base=0,
                               pattern=[[-1, P]], channel_multiplier=1).then_inc(slots_set, 1)
            pool.memset(vst[:, :, :], 1.0).then_inc(slots_set, 1)
            for s, n in CREDITS.items():
                pool.sem_inc(s, n)

            def keep_causal(G, a):
                pool.wait_ge(exp_done, G * UNITS + UNITS + 2)
                pool.sem_inc(passed, 1)
                for block_ap, n in ((pT[:, a, :, 0:P], UNITS), (pT[:, a, 1:8:2, 384:512], 4), (pT[:, a, 8:10, 256:384], 2)):
                    pool.affine_select(out=block_ap, in_=block_ap, compare_op=ALU.is_ge, fill=0.0, base=0,
                                       pattern=[[0, n], [1, P]], channel_multiplier=-1).then_inc(masked, 1)

            def step(r, i, first, second, post, prep):
                if post:
                    T = (r - 2) * TILES + i
                    par = r % 2
                    o = oT[:, par, i, :, 0:VD].rearrange("p (h j) e -> p h j e", j=2)
                    pool.wait_ge(rc_ready, T + 1)
                    pool.wait_ge(merged_ready, T + 1)
                    pool.tensor_tensor(o1[:, :, :], o[:, :, 0, :], rc[:, :, 0].unsqueeze(2).broadcast_to([P, H, VD]), ALU.mult).then_inc(pool_post, 1)
                    pool.tensor_tensor(o2[:, :, :], o[:, :, 1, :], rc[:, :, 1].unsqueeze(2).broadcast_to([P, H, VD]), ALU.mult).then_inc(pool_post, 1)
                    pool.wait_ge(pool_post, T * 2 + 3)
                    pool.tensor_tensor(og[:, :, :], o1[:, :, :], o2[:, :, :], ALU.add).then_inc(og_ready, 1)
                if second:
                    keep_causal((r - 1) * GROUPS + i * 2, 0)
                if prep:
                    T = (r + 1) * TILES + i
                    pool.wait_ge(res_ready, T + 1)
                    pool.wait_ge(qkv_saved, T * QKV_SAVES + 16)
                    pool.sem_inc(passed, 1)
                    pool.tensor_copy(parts[:, 1, :, :], res[:, :, :]).then_inc(mid_ready, 1)
                    pool.wait_ge(mid_ready, T + 1)
                    pool.tensor_tensor(parts[:, 2, :, :], res[:, :, :], parts[:, 1, :, :], ALU.subtract).then_inc(split_ready, 1)
                if second:
                    keep_causal((r - 1) * GROUPS + i * 2 + 1, 1)

            rounds(pool, step)

        @block.scalar
        def _(act):
            act.wait_ge(slots_set, 6)

            def exps(G, a):
                act.wait_ge(av_done, G + 1)
                for u in range(UNITS):
                    act.wait_ge(second_unit, G * UNITS + u + 1 + 2 * UNITS)
                    act.activation(pT[:, a, u, :], p2b[u % 2][:, :], ACT.Exp, scale=SCALE).then_inc(exp_done, 1)

            def take_o(G, a):
                act.wait_ge(av_done, G + 3)
                act.wait_ge(oT_done, G + 1)
                act.activation(o_sb[:, a, :], ob[:, :], ACT.Copy).then_inc(o_read, 1)

            def take_oT(r, i, G, a):
                act.wait_ge(oT_done, G + 3)
                to = oT[:, (r + 1) % 2, :, bass.ds(i * 2 * MAPS + a * MAPS, MAPS), :]
                act.activation(to, otb[:, :].rearrange("p (c m e) -> p c m e", c=TILES, m=MAPS)[:, :, :, 0:VD + 1],
                               ACT.Copy).then_inc(oT_read, 1)

            def step(r, i, first, second, post, prep):
                G = (r - 1) * GROUPS + i * 2
                if second:
                    exps(G, 0)
                if prep:
                    T = (r + 1) * TILES + i
                    act.wait_ge(xnT_done, T + 1)
                    act.wait_ge(v_done, T + 1)
                    act.activation(hT[:, :], prepb[:, 0:P], ACT.Identity, scale=k.mod[:, 0, 1, bass.ds(r + 1, 1)], bias=k.mod[:, 0, 0, bass.ds(r + 1, 1)]).then_inc(hT_ready, 1)
                    act.wait_ge(qk_done, T + 1)
                    act.wait_ge(qkv_saved, T * QKV_SAVES + 16)
                    act.activation(parts[:, 0, :, :], prepb[:, :].rearrange("p (j t) -> p j t", j=4), ACT.Copy).then_inc(hi_ready, 1)
                    act.wait_ge(v_done, T + 2)
                    act.activation(vst[:, :, 0:VD], prepb[:, 0:H * VD].rearrange("p (h e) -> p h e", h=H), ACT.Copy).then_inc(v_ready, 1)
                if second:
                    take_o(G, 0)
                    exps(G + 1, 1)
                    if post:
                        act.wait_ge(og_ready, (r - 2) * TILES + 1)
                    take_oT(r, i, G, 0)
                if post:
                    T = (r - 2) * TILES + i
                    act.wait_ge(mT_done, T + 1)
                    act.wait_ge(wo_done, T + 1)
                    act.activation(mT[:, :, :], postb[:, 0:2 * P].rearrange("p (c t) -> p c t", c=2), ACT.Copy).then_inc(mT_ready, 1)
                if second:
                    take_o(G + 1, 1)
                    take_oT(r, i, G + 1, 1)

            rounds(act, step)

        @block.tensor
        def _(pe):
            pe.wait_ge(w_loaded, W_LOADS)
            pe.wait_ge(slots_set, 6)

            def first_unit_of(G, a, u):
                bank = p1b[u % 2]
                pe.wait_ge(first_read, G * UNITS + u + 1)
                blocks = {0: [(u, 3, 0)], 1: [(u - 4, 2, 0), (u - 4, 0, 3)],
                          2: [(2 * u - 16, 1, 0), (2 * u - 15, 1, 2)]}[u // 4]
                for m, c, at in blocks:
                    pe.matmul(bank[:, at * P:(at + c + 1) * P], q1[:, a, m, c * P:(c + 1) * P], k1[:, a, m, 0:(c + 1) * P],
                              start=True, stop=False, skip_group_check=True)
                    mm = pe.matmul(bank[:, (at + c) * P:(at + c + 1) * P], k.identb[:, :], causal[:, :],
                                   start=False, stop=True, skip_group_check=True)
                mm.then_inc(first_unit, 1)

            def second_unit_of(G, a, u):
                bank = p2b[u % 2]
                pe.wait_ge(exp_done, G * UNITS + u + 1)
                if u < 8:
                    m = u // 2
                    blocks = [(m, 0, 0)] if u % 2 == 0 else [(m, 1, 0), (m, 3, 384)]
                else:
                    blocks = [(2 * u - 16, 2, 0), (2 * u - 15, 2, 256)]
                for m, c, at in blocks:
                    n = S - c * P
                    mm = pe.matmul(bank[:, at:at + n], k2[:, a, m, c * P:(c + 1) * P], q2[:, a, m, c * P:S],
                                   start=True, stop=True, skip_group_check=True)
                mm.then_inc(second_unit, 1)

            def units(r, i, a, first, second):
                g = i * 2 + a
                if first:
                    G1 = r * GROUPS + g
                    pe.wait_ge(first_loaded[a], (r * TILES + i + 1) * FIRST_LOADS)
                if second:
                    G2 = (r - 1) * GROUPS + g
                    pe.wait_ge(second_loaded[a], ((r - 1) * TILES + i + 1) * SECOND_LOADS)
                for u in range(UNITS):
                    if second:
                        second_unit_of(G2, a, u)
                    if first:
                        first_unit_of(G1, a, u)

            def product(r, i, a):
                G = (r - 1) * GROUPS + i * 2 + a
                pe.wait_ge(masked, 3 * G + 3)
                pe.wait_ge(v_loaded[a], ((r - 1) * TILES + i + 1) * 16)
                pe.wait_ge(o_read, G + 1)
                for c in range(TILES):
                    for m in range(MAPS):
                        u, at = {0: (2 * m, 0), 1: (2 * m + 1, 0), 2: (8 + m // 2, 256 * (m % 2)), 3: (2 * m + 1, 384)}[c]
                        n = S - c * P
                        mm = pe.matmul(ob[32 * m:32 * m + 32, c * P:S], vs[:, a, c, m // 2, :], pT[:, a, u, at:at + n],
                                       start=(c == 0), stop=(c == TILES - 1), skip_group_check=True)
                mm.then_inc(av_done, 1)

            def turn_o(r, i, a):
                G = (r - 1) * GROUPS + i * 2 + a
                pe.wait_ge(o_read, G + 2)
                pe.wait_ge(oT_read, G + 1)
                for c in range(TILES):
                    mm = pe.transpose(otb[:, c * P:(c + 1) * P], o_sb[:, a, c * P:(c + 1) * P], k.ident[:, :])
                mm.then_inc(oT_done, 1)

            def step(r, i, first, second, post, prep):
                if first or second:
                    units(r, i, 0, first, second)
                if prep:
                    T = (r + 1) * TILES + i
                    pe.wait_ge(xn_ready, T + 1)
                    pe.wait_ge(v_ready, T + 1)
                    pe.wait_ge(neg_read, r + 2)
                    pe.transpose(prepb[:, 0:P], xn[:, :], k.ident[:, :]).then_inc(xnT_done, 1)
                    pe.wait_ge(hT_ready, T + 1)
                    for j in range(4):
                        mm = pe.matmul(prepb[:, j * P:(j + 1) * P], wqk[:, j, :], hT[:, :], start=True, stop=True)
                    mm.then_inc(qk_done, 1)
                    pe.wait_ge(hi_ready, T + 1)
                    pe.wait_ge(res_ready, T + 1)
                    pe.matmul(prepb[:, 0:H * VD], hT[:, :], wv[:, :], start=True, stop=True).then_inc(v_done, 1)
                if second:
                    product(r, i, 0)
                if first or second:
                    units(r, i, 1, first, second)
                if second:
                    turn_o(r, i, 0)
                if post:
                    T = (r - 2) * TILES + i
                    pe.wait_ge(merged_ready, T + 2)
                    pe.wait_ge(post_done, T + 1)
                    for c in range(2):
                        mm = pe.transpose(postb[:, c * P:(c + 1) * P], merged[:, c * P:(c + 1) * P], k.ident[:, :])
                    mm.then_inc(mT_done, 1)
                    pe.wait_ge(mT_ready, T + 1)
                    for c in range(2):
                        mm = pe.matmul(postb[:, 2 * P:3 * P], mT[:, c, :], wo[:, c, :], start=(c == 0), stop=(c == 1))
                    mm.then_inc(wo_done, 1)
                if second:
                    product(r, i, 1)
                    turn_o(r, i, 1)

            def tail(r):
                pe.wait_ge(qmax_ready, r + 1)
                pe.wait_ge(v_ready, (min(r + 2, B) if isinstance(r, int) else r + 2) * TILES + 1)
                for c in range(TILES):
                    mm = pe.transpose(prepb[0:2 * H, c * P:(c + 1) * P], qmax[:, c, :], k.ident[:, :])
                mm.then_inc(neg_psum, 1)

            rounds(pe, step, tail)

        @block.vector
        def _(dve):
            def maxima(r, i, a):
                G = r * GROUPS + i * 2 + a
                m0 = i * 2 * MAPS + a * MAPS
                for u in range(UNITS):
                    dve.wait_ge(first_unit, G * UNITS + u + 1 + 2 * UNITS)
                    bank = p1b[u % 2][:, :]
                    if u < 8:
                        to = bmax[:, m0 + u % 4, 4 * (u // 4):4 * (u // 4) + 4]
                        src = bank.rearrange("p (c t) -> p c t", c=4)
                    else:
                        to = bmax[:, bass.ds(m0 + 2 * (u - 8), 2), 8:10]
                        src = bank.rearrange("p (m c t) -> p m c t", m=2, c=2)
                    dve.tensor_reduce(to, src, AX, ALU.max).then_inc(first_read, 1)

            def step(r, i, first, second, post, prep):
                if post:
                    T = (r - 2) * TILES + i
                    par = r % 2
                    dve.wait_ge(oT_read, (r - 1) * GROUPS + 1)
                    sums = oT[:, par, i, :, VD].rearrange("p (h j) -> p h j", j=2)
                    chain = Chain(dve, dve_post, T * POST_LINKS)
                    link = chain.link
                    link(dve.reciprocal(rc[:, :, :], sums))
                    dve.tensor_tensor(rc[:, :, 1], rc[:, :, 1], k.neg_lam[:, :], ALU.mult).then_inc(rc_ready, 1)
                if prep:
                    T = (r + 1) * TILES + i
                    dve.wait_ge(v_done, T + 1)
                    dve.tensor_scalar(xn[:, :], k.x[:, (r + 1) * TILES + i, :], k.stats[:, (r + 1) * TILES + i, 0:1],
                                      k.rstd[:, bass.ds((r + 1) * TILES + i, 1)], ALU.subtract, ALU.mult).then_inc(xn_ready, 1)
                if first:
                    maxima(r, i, 0)
                if prep:
                    dve.wait_ge(hi_ready, T + 1)
                    dve.wait_ge(split_ready, T + 1)
                    dve.tensor_tensor(res[:, :, :], prepb[:, :].rearrange("p (j t) -> p j t", j=4), parts[:, 0, :, :],
                                      ALU.subtract).then_inc(res_ready, 1)
                if post:
                    T = (r - 2) * TILES + i
                    dve.wait_ge(og_ready, T + 2)
                    bc = lambda t: t[:, :].unsqueeze(2).broadcast_to([P, H, VD])
                    link(dve.tensor_reduce(msum[:, :], og[:, :, :], AX, ALU.add))
                    link(dve.scalar_tensor_tensor(oc[:, :, :], bc(msum), -1.0 / VD, og[:, :, :], ALU.mult, ALU.add))
                    link(dve.tensor_tensor(sq[:, :, :], oc[:, :, :], oc[:, :, :], ALU.mult))
                    link(dve.tensor_reduce(vsum[:, :], sq[:, :, :], AX, ALU.add))
                    link(dve.tensor_scalar(vsum[:, :], vsum[:, :], 1.0 / VD, EPS, ALU.mult, ALU.add))
                    rsqrt_steps(dve, link, vsum[:, :], vhalf[:, :], orstd[:, :], otmp[:, :])
                    assert chain.n == POST_LINKS - 1
                    dve.wait_ge(wo_done, T + 1)
                    dve.scalar_tensor_tensor(merged[:, :].rearrange("p (h e) -> p h e", h=H), oc[:, :, :], 1.0 - LAM_INIT, bc(orstd),
                                             ALU.mult, ALU.mult).then_inc(merged_ready, 1)
                if first:
                    maxima(r, i, 1)
                if post:
                    dve.wait_ge(wo_done, T + 2)
                    link(dve.tensor_tensor(gated[:, :], postb[:, 2 * P:3 * P], k.gate_a0[:, r - 2, :], ALU.mult))
                    x = k.x[:, (r - 2) * TILES + i, :]
                    dve.tensor_tensor(x, x, gated[:, :], ALU.add).then_inc(post_done, 1)

            def tail(r):
                chain = Chain(dve, dve_max, r * MAX_LINKS)
                link = chain.link
                dve.wait_ge(first_read, (r + 1) * GROUPS * UNITS + 2)
                for c, lo, n in ((3, 0, 4), (2, 4, 3), (0, 7, 1), (1, 8, 2)):
                    ins = dve.tensor_reduce(qmax[:, c, :], bmax[:, :, lo:lo + n], AX, ALU.max)
                ins.then_inc(qmax_ready, 1)
                dve.wait_ge(neg_psum, r + 1)
                dve.wait_ge(neg_saved, r * NEG_SAVES + 16)
                src = prepb[0:2 * H, :]
                link(dve.tensor_scalar(nparts[:, 0, :], src, -1.0, None, ALU.mult))
                dve.scalar_tensor_tensor(nres[:, :], src, -1.0, nparts[:, 0, :], ALU.mult, ALU.subtract).then_inc(neg_read, 1)
                dve.wait_ge(neg_read, r + 3)
                link(dve.tensor_copy(nparts[:, 1, :], nres[:, :]))
                dve.tensor_tensor(nparts[:, 2, :], nres[:, :], nparts[:, 1, :], ALU.subtract).then_inc(neg_ready, 1)
                assert chain.n == MAX_LINKS

            rounds(dve, step, tail)


POST_LINKS = 1 + 5 + RSQRT_LINKS + 1
MAX_LINKS = 2


def token_stats(dve, link, k):
    for t in range(B * TILES):
        last = dve.bn_stats(k.bn[:, t, :], k.x[:, t, :])
    link(last)
    for t in range(B * TILES):
        last = dve.bn_aggr(k.stats[:, t, :], k.bn[:, t, :])
    link(last)
    link(dve.tensor_scalar(k.bn[:, :, 1], k.stats[:, :, 1], EPS, None, ALU.add))
    rsqrt_steps(dve, link, k.bn[:, :, 1], k.half[:, :], k.rstd[:, :], k.tmp[:, :])


def normalize(dve, k, xn, tile):
    return dve.tensor_scalar(xn, k.x[:, tile, :], k.stats[:, tile, 0:1], k.rstd[:, bass.ds(tile, 1)], ALU.subtract, ALU.mult)


def ffn(nc, d, k):
    FT = FF // P
    with ExitStack() as ctx:
        def sb(name, shape, dt=F32):
            return ctx.enter_context(nc.sbuf_tensor(name, shape, dt))

        def ps(name):
            return ctx.enter_context(nc.psum_tensor(name, [P, 512], F32))

        def sem(name):
            return ctx.enter_context(nc.semaphore(name))

        w1 = sb("w1", [P, FF])
        w2 = sb("w2", [P, FT, D])
        b2 = sb("b2", [P, D])
        col = sb("col", [P, 4, FT])
        th = sb("th", [P, 8, FT])
        coef = sb("coef", [P, FT])
        xn = sb("f_xn", [P, 2, TILES, D])
        hT = sb("f_hT", [P, 2, S])
        hid = sb("hid", [P, 2, FT, S])
        arg = sb("arg", [P, 2, FT, S])
        turns = sb("turns", [P, 2, FT, S])
        gated = sb("f_gated", [P, 2, TILES, D])
        tpb = [ps(f"tpb{a}") for a in range(2)]
        upb = [ps(f"upb{a}") for a in range(2)]
        outb = [ps(f"outb{a}") for a in range(2)]
        loaded, angle, th_sin, ready = sem("ffn_loaded"), sem("angle"), sem("th_sin"), sem("ffn_credits")
        xn_ready, xT_done, hT_ready, up_done, hid_ready, arg_ready, sin_ready, act_ready, out_done, x_ready = (
            sem(n) for n in ("f_xn_ready", "f_xT_done", "f_hT_ready", "up_done", "hid_ready", "arg_ready", "sin_ready",
                             "act_ready", "out_done", "f_x_ready"))
        dve_setup, dve_chain = sem("ffn_dve_setup"), sem("ffn_dve")
        block = ctx.enter_context(nc.Block())
        CREDITS = {hT_ready: 2, hid_ready: 2, out_done: 2, x_ready: 2}
        LOADS = 7 * 16

        @block.sync
        def _(sp):
            for s, n in CREDITS.items():
                sp.sem_inc(s, n)
            sp.dma_start(w1[:, :], d["L0_ffn_W1"]).then_inc(loaded, 16)
            for n, name in enumerate(("b1", "quantum_phases", "quantum_weights_real", "quantum_weights_imag")):
              with nc.allow_non_contiguous_dma("one value of each hidden unit"):
                sp.dma_start(col[:, n, :], d["L0_ffn_" + name].rearrange("(j p) -> p j", p=P)).then_inc(loaded, 16)
            sp.dma_start(w2[:, :, :], d["L0_ffn_W2"].rearrange("(j p) n -> p j n", p=P)).then_inc(loaded, 16)
            sp.dma_start(b2[:, :], d["L0_ffn_b2"].partition_broadcast(P)).then_inc(loaded, 16)
            sp.wait_ge(x_ready, B + 2)

        def reduce_angle(eng, link, out, angle_, n):
            link(eng.tensor_scalar(n, angle_, INV_2PI, ROUND, ALU.mult, ALU.add))
            link(eng.tensor_scalar(n, n, ROUND, None, ALU.subtract))
            link(eng.scalar_tensor_tensor(out, n, -TWO_PI_HI, angle_, ALU.mult, ALU.add))
            link(eng.scalar_tensor_tensor(out, n, -TWO_PI_MID, out, ALU.mult, ALU.add))
            link(eng.scalar_tensor_tensor(out, n, -TWO_PI_LO, out, ALU.mult, ALU.add))
            return eng.tensor_scalar(out, out, PI_BELOW, -PI_BELOW, ALU.min, ALU.max)

        @block.tensor
        def _(pe):
            pe.wait_ge(loaded, LOADS)
            with pe.Fori(0, B // 2) as it:
                for a in range(2):
                    T = it * 2 + a
                    pe.wait_ge(xn_ready, T + 1)
                    pe.wait_ge(hT_ready, T + 1)
                    for c in range(TILES):
                        mm = pe.transpose(tpb[a][:, c * P:(c + 1) * P], xn[:, a, c, :], k.ident[:, :])
                    mm.then_inc(xT_done, 1)
                for a in range(2):
                    T = it * 2 + a
                    pe.wait_ge(hT_ready, T + 3)
                    for j in range(FT):
                        pe.wait_ge(hid_ready, T * FT + j + 1)
                        pe.matmul(upb[j % 2][:, :], w1[:, j * P:(j + 1) * P], hT[:, a, :], start=True, stop=True).then_inc(up_done, 1)
                for a in range(2):
                    T = it * 2 + a
                    pe.wait_ge(x_ready, T + 1)
                    pe.matmul(outb[a][:, :].rearrange("p (c n) -> p c n", c=TILES), k.ident[:, :],
                              b2[:, :].unsqueeze(1).broadcast_to([P, TILES, D]), start=True, stop=False, skip_group_check=True)
                    pe.wait_ge(act_ready, T + 1)
                    for j in range(FT):
                        for c in range(TILES):
                            mm = pe.matmul(outb[a][:, c * P:(c + 1) * P], hid[:, a, j, c * P:(c + 1) * P], w2[:, j, :],
                                           start=False, stop=(j == FT - 1), skip_group_check=True)
                    mm.then_inc(out_done, 1)

        @block.scalar
        def _(act):
            act.wait_ge(angle, 1)
            act.activation(th[:, 6:8, :], th[:, 4:6, :], ACT.Sin).then_inc(th_sin, 1)
            act.wait_ge(loaded, LOADS)
            with act.Fori(0, B // 2) as it:
                for a in range(2):
                    T = it * 2 + a
                    act.wait_ge(xT_done, T + 1)
                    act.activation(hT[:, a, :], tpb[a][:, :], ACT.Identity, scale=k.mod[:, 0, 4, bass.ds(T, 1)],
                                   bias=k.mod[:, 0, 3, bass.ds(T, 1)]).then_inc(hT_ready, 1)
                for a in range(2):
                    T = it * 2 + a
                    act.wait_ge(out_done, T + 1)
                    for j in range(FT):
                        act.wait_ge(up_done, T * FT + j + 1)
                        act.activation(hid[:, a, j, :], upb[j % 2][:, :], ACT.Identity, bias=col[:, 0, j:j + 1]).then_inc(hid_ready, 1)
                for a in range(2):
                    T = it * 2 + a
                    act.wait_ge(arg_ready, T + 1)
                    act.activation(turns[:, a, :, :], arg[:, a, :, :], ACT.Sin).then_inc(sin_ready, 1)

        @block.vector
        def _(dve):
            link = Chain(dve, dve_setup).link
            token_stats(dve, link, k)
            dve.wait_ge(loaded, LOADS)
            theta = col[:, 1, :]
            link(reduce_angle(dve, link, th[:, 4, :], theta, th[:, 0, :]))
            link(dve.scalar_tensor_tensor(th[:, 1, :], th[:, 4, :], -1.0, th[:, 4, :], ALU.mult, ALU.max))
            dve.tensor_scalar(th[:, 5, :], th[:, 1, :], -1.0, math.pi / 2, ALU.mult, ALU.add).then_inc(angle, 1)
            dve.wait_ge(th_sin, 1)
            link(dve.tensor_tensor(th[:, 2, :], th[:, 7, :], col[:, 2, :], ALU.mult))
            link(dve.tensor_tensor(th[:, 3, :], th[:, 6, :], col[:, 3, :], ALU.mult))
            link(dve.tensor_tensor(th[:, 2, :], th[:, 2, :], th[:, 3, :], ALU.add))
            link(dve.scalar_tensor_tensor(coef[:, :], th[:, 2, :], 0.1, col[:, 3, :], ALU.mult, ALU.mult))
            LINKS = 2 * 8
            with dve.Fori(0, B // 2) as it:
                chain = Chain(dve, dve_chain, it * LINKS)
                link = chain.link
                for a in range(2):
                    T = it * 2 + a
                    for c in range(TILES):
                        ins = normalize(dve, k, xn[:, a, c, :], T * TILES + c)
                    ins.then_inc(xn_ready, 1)
                for a in range(2):
                    T = it * 2 + a
                    for j in range(FT):
                        dve.wait_ge(hid_ready, T * FT + j + 3)
                        ins = dve.tensor_scalar(arg[:, a, j, :], hid[:, a, j, :], 0.1, col[:, 1, j:j + 1], ALU.mult, ALU.add)
                    link(ins)
                    flat = lambda t: t[:, a, :, :].rearrange("p j t -> p (j t)")
                    reduce_angle(dve, link, flat(arg), flat(arg), flat(turns)).then_inc(arg_ready, 1)
                for a in range(2):
                    T = it * 2 + a
                    dve.wait_ge(sin_ready, T + 1)
                    for j in range(FT):
                        ins = dve.scalar_tensor_tensor(hid[:, a, j, :], turns[:, a, j, :], coef[:, j:j + 1], hid[:, a, j, :], ALU.mult, ALU.add)
                    link(ins)
                    dve.tensor_scalar(flat_of(hid, a), flat_of(hid, a), 0.0, None, ALU.max).then_inc(act_ready, 1)
                for a in range(2):
                    T = it * 2 + a
                    dve.wait_ge(out_done, T + 3)
                    link(dve.tensor_tensor(gated[:, a, :, :], outb[a][:, :].rearrange("p (c n) -> p c n", c=TILES),
                                           k.gate_b0[:, bass.ds(T, 1), :].broadcast_to([P, TILES, D]), ALU.mult))
                    x = k.x[:, bass.ds(T * TILES, TILES), :]
                    dve.tensor_tensor(x, x, gated[:, a, :, :], ALU.add).then_inc(x_ready, 1)
                assert chain.n == LINKS, chain.n


def flat_of(t, a):
    return t[:, a, :, :].rearrange("p j t -> p (j t)")


LOG1P = (1.0, -0.49999892711639404, 0.33329710364341736, -0.24951615929603577, 0.1966327428817749, -0.1526966691017151,
         0.10543623566627502, -0.05637361481785774, 0.019542528316378593, -0.0031760570127516985)


def scan(nc, d, k):
    BC = 2 * N
    with ExitStack() as ctx:
        def sb(name, shape, dt=F32):
            return ctx.enter_context(nc.sbuf_tensor(name, shape, dt))

        def ps(name):
            return ctx.enter_context(nc.psum_tensor(name, [P, 512], F32))

        def sem(name):
            return ctx.enter_context(nc.semaphore(name))

        conv_w = sb("conv_w", [P, 3])
        wbc = sb("wbc", [P, 3, BC])
        bbc = sb("bbc", [3 * BC, 1])
        wdt = sb("wdt", [P, RANK])
        bdt = sb("bdt", [RANK, 1])
        wdtp = sb("wdtp", [RANK, D])
        bdtp = sb("bdtp", [P, 1])
        nA = sb("nA", [P, N])
        dco = sb("dco", [P, 1])
        sel = sb("sel", [3 * BC, BC, P], BF16)
        xn = sb("s_xn", [P, TILES, D])
        hT = sb("s_hT", [P, 2, S + 2])
        u = sb("u", [P, S])
        us = sb("us", [P, S])
        bc = sb("bc", [3 * BC, S])
        bcp = sb("bcp", [3 * BC, 2, S], BF16)
        t1 = sb("t1", [RANK, S])
        zb, na, ee, pl = (sb(n, [P, S]) for n in ("zb", "na", "ee", "pl"))
        dt = sb("dt", [P, 2, S])
        dtx = sb("dtx", [P, 2, S])
        dA = sb("dA", [P, 4, S])
        dBx = sb("dBx", [P, 2, S])
        hs = sb("hs", [P, 2, S])
        ch = sb("ch", [P, 4, S])
        yT = sb("yT", [P, S])
        yg = sb("yg", [P, S])
        preb, pre2 = ps("s_preb"), ps("s_pre2")
        bb = [ps(f"bb{i}") for i in range(2)]
        cb = [ps(f"cb{i}") for i in range(2)]
        yb = ps("yb")
        postb = ps("s_postb")
        loaded, sel_ready, consts, nA_ready = sem("s_loaded"), sem("sel_ready"), sem("s_consts"), sem("nA_ready")
        xn_ready, xT_done, hT_ready, u_ready, us_ready, bc_psum, bc_ready, dtr_psum, t1_ready, z_psum, zb_ready, na_ready, ee_ready, log_ready, dt_ready, parts_ready = (
            sem("s_" + n) for n in ("xn_ready", "xT_done", "hT_ready", "u_ready", "us_ready", "bc_psum", "bc_ready", "dtr_psum",
                                    "t1_ready", "z_psum", "zb_ready", "na_ready", "ee_ready", "log_ready", "dt_ready", "parts_ready"))
        state_bc, dA_ready, dBx_ready, scan_done, ch_ready, y_acc, yT_ready, yg_ready, out_done, x_ready = (
            sem("s_" + n) for n in ("state_bc", "dA_ready", "dBx_ready", "scan_done", "ch_ready", "y_acc", "yT_ready", "yg_ready",
                                    "out_done", "x_ready"))
        dve_setup, dve_pre, dve_main, pool_log = sem("s_dve_setup"), sem("s_dve_pre"), sem("s_dve_main"), sem("s_pool_log")
        passed, act_passed = sem("s_passed"), sem("s_act_passed")
        block = ctx.enter_context(nc.Block())
        CREDITS = {x_ready: 1, y_acc: 4, ch_ready: 2, yg_ready: 1, zb_ready: 1, parts_ready: 1, yT_ready: 1,
                   scan_done: 4, dt_ready: 1, log_ready: 1}
        LOADS = (3 + 3 + 6) * 16
        LOG_LINKS = 2 * (len(LOG1P) - 2) + 1

        def rounds(eng, step):
            step(-1, pre=True, main=False)
            with eng.Fori(0, B - 1) as r:
                step(r, pre=True, main=True)
            step(B - 1, pre=False, main=True)

        @block.sync
        def _(sp):
            a = "L1_attn_"
            for j in range(3):
                sp.dma_start(wbc[:, j, :], d[a + "W_bc"]).then_inc(loaded, 16)
                sp.dma_start(bbc[j * BC:(j + 1) * BC, :], d[a + "b_bc"].unsqueeze(1)).then_inc(loaded, 16)
            with nc.allow_non_contiguous_dma("three values of each feature"):
                sp.dma_start(conv_w[:, :], d[a + "conv_w"].rearrange("c p -> p c")).then_inc(loaded, 16)
            sp.dma_start(wdt[:, :], d[a + "W_dt"]).then_inc(loaded, 16)
            sp.dma_start(bdt[:, :], d[a + "b_dt"].unsqueeze(1)).then_inc(loaded, 16)
            sp.dma_start(wdtp[:, :], d[a + "W_dtp"]).then_inc(loaded, 16)
            sp.dma_start(bdtp[:, :], d[a + "b_dtp"].unsqueeze(1)).then_inc(loaded, 16)
            sp.dma_start(dco[:, :], d[a + "Dcoeff"].unsqueeze(1)).then_inc(loaded, 16)
            sp.dma_start(nA[:, :], d[a + "A_log"]).then_inc(nA_ready, 16)
            sp.wait_ge(x_ready, B + 1)

        @block.gpsimd
        def _(pool):
            for s, n in CREDITS.items():
                pool.sem_inc(s, n)
            pool.memset(sel[:, :, :], 0.0).then_inc(consts, 1)
            pool.memset(hT[:, :, :], 0.0).then_inc(consts, 1)
            pool.wait_ge(consts, 2)
            for j in range(3):
                pool.affine_select(out=sel[:, :, :], in_=sel[:, :, :], compare_op=ALU.not_equal, fill=1.0, base=-j * BC,
                                   pattern=[[-1, BC], [0, P]], channel_multiplier=1).then_inc(sel_ready, 1)
                pool.wait_ge(sel_ready, j + 1)

            def step(r, pre, main):
                if pre:
                    b = r + 1
                    pool.wait_ge(ee_ready, b + 1)
                    pool.wait_ge(dt_ready, b + 1)
                    pool.sem_inc(passed, 1)
                    chain = Chain(pool, pool_log, b * LOG_LINKS, passed)
                    link = chain.link
                    p, e = pl[:, :], ee[:, :]
                    link(pool.tensor_scalar(p, e, LOG1P[-1], LOG1P[-2], ALU.mult, ALU.add))
                    for c in LOG1P[-3::-1]:
                        link(pool.tensor_tensor(p, p, e, ALU.mult))
                        link(pool.tensor_scalar(p, p, 1.0, c, ALU.mult, ALU.add))
                    pool.tensor_tensor(p, p, e, ALU.mult).then_inc(log_ready, 1)
                    assert chain.n == LOG_LINKS, chain.n

            rounds(pool, step)

        @block.tensor
        def _(pe):
            pe.wait_ge(loaded, LOADS)
            pe.wait_ge(sel_ready, 3)

            def step(r, pre, main):
                b = r + 1

                def pre_turn():
                    pe.wait_ge(xn_ready, b + 1)
                    pe.wait_ge(zb_ready, b + 1)
                    for c in range(TILES):
                        mm = pe.transpose(preb[:, c * P:(c + 1) * P], xn[:, c, :], k.ident[:, :])
                    mm.then_inc(xT_done, 1)

                def pre_bc():
                    pe.wait_ge(us_ready, b + 1)
                    pe.matmul(preb[0:3 * BC, :], wbc[:, :, :].rearrange("p j n -> p (j n)"), us[:, :], start=True, stop=True).then_inc(bc_psum, 1)
                    pe.matmul(pre2[0:RANK, :], wdt[:, :], us[:, :], start=True, stop=True).then_inc(dtr_psum, 1)

                def pre_z():
                    pe.wait_ge(t1_ready, b + 1)
                    pe.wait_ge(bc_ready, 2 * b + 2)
                    pe.matmul(preb[:, :], wdtp[:, :], t1[:, :], start=True, stop=True).then_inc(z_psum, 1)

                if not main:
                    pre_turn(), pre_bc(), pre_z()
                    return
                par = r % 2
                pe.wait_ge(parts_ready, r + 2)
                for n in range(N + 2):
                    if n < N:
                        pe.wait_ge(ch_ready, r * N + n + 1)
                        pe.matmul(bb[n % 2][:, :], sel[:, n, :], bcp[:, par, :], start=True, stop=True)
                        pe.matmul(cb[n % 2][:, :], sel[:, N + n, :], bcp[:, par, :], start=True, stop=True).then_inc(state_bc, 1)
                    if n >= 2:
                        q = r * N + n - 2
                        pe.wait_ge(ch_ready, q + 3)
                        if n == 2:
                            pe.wait_ge(yT_ready, r + 1)
                        mm = pe.matmul(yb[:, :], k.ident[:, :], ch[:, (n - 2) % 4, :],
                                       start=(n == 2), stop=(n == N + 1), skip_group_check=True)
                        mm.then_inc(y_acc, 1)
                    if pre and n == 2:
                        pre_turn()
                    if pre and n == 6:
                        pre_bc()
                    if pre and n == 8:
                        pre_z()
                pe.wait_ge(yg_ready, r + 2)
                pe.wait_ge(x_ready, r + 1)
                for c in range(TILES):
                    mm = pe.transpose(postb[:, c * P:(c + 1) * P], yg[:, c * P:(c + 1) * P], k.ident[:, :])
                mm.then_inc(out_done, 1)

            rounds(pe, step)

        @block.scalar
        def _(act):
            act.wait_ge(nA_ready, 16)
            act.activation(nA[:, :], nA[:, :], ACT.Exp).then_inc(nA_ready, 1)
            act.wait_ge(nA_ready, 17)
            act.activation(nA[:, :], nA[:, :], ACT.Copy, scale=-1.0).then_inc(nA_ready, 1)
            act.wait_ge(nA_ready, 18)
            act.wait_ge(loaded, LOADS)
            act.wait_ge(consts, 2)

            def step(r, pre, main):
                b = r + 1
                bpar = b % 2

                def pre_h():
                    act.wait_ge(xT_done, b + 1)
                    act.activation(hT[:, bpar, 1:S + 1], preb[:, :], ACT.Identity, scale=k.mod[:, 1, 1, bass.ds(b, 1)],
                                   bias=k.mod[:, 1, 0, bass.ds(b, 1)]).then_inc(hT_ready, 1)

                def pre_silu():
                    act.wait_ge(u_ready, b + 1)
                    act.activation(us[:, :], u[:, :], ACT.Silu).then_inc(us_ready, 1)

                def pre_bc():
                    act.wait_ge(bc_psum, b + 1)
                    act.wait_ge(parts_ready, b + 1)
                    act.activation(bc[:, :], preb[0:3 * BC, :], ACT.Identity, bias=bbc[:, 0:1]).then_inc(bc_ready, 1)
                    act.activation(bcp[:, bpar, :], preb[0:3 * BC, :], ACT.Identity, bias=bbc[:, 0:1]).then_inc(bc_ready, 1)
                    act.wait_ge(dtr_psum, b + 1)
                    act.activation(t1[:, :], pre2[0:RANK, :], ACT.Identity, bias=bdt[:, 0:1]).then_inc(t1_ready, 1)

                def pre_z():
                    act.wait_ge(z_psum, b + 1)
                    act.wait_ge(dt_ready, b + 1)
                    act.activation(zb[:, :], preb[:, :], ACT.Identity, bias=bdtp[:, 0:1]).then_inc(zb_ready, 1)

                def pre_exp():
                    act.wait_ge(na_ready, b + 1)
                    act.wait_ge(log_ready, b + 1)
                    act.activation(ee[:, :], na[:, :], ACT.Exp).then_inc(ee_ready, 1)

                if not main:
                    pre_h(), pre_silu(), pre_bc(), pre_z(), pre_exp()
                    return
                par = r % 2
                act.wait_ge(dt_ready, r + 2)
                for n in range(N):
                    q = r * N + n
                    act.wait_ge(scan_done, q + 1)
                    act.sem_inc(act_passed, 1)
                    act.activation(dA[:, n % 4, :], dt[:, par, :], ACT.Exp, scale=nA[:, n:n + 1]).then_inc(dA_ready, 1)
                    if pre:
                        for at, f in ((2, pre_h), (4, pre_silu), (6, pre_bc), (8, pre_z), (9, pre_exp)):
                            if n == at:
                                f()
                act.wait_ge(yT_ready, r + 2)
                act.wait_ge(x_ready, r + 1)
                act.activation(yg[:, :], yT[:, :], ACT.Copy, scale=k.mod[:, 1, 2, bass.ds(r, 1)]).then_inc(yg_ready, 1)

            rounds(act, step)

        @block.vector
        def _(dve):
            link = Chain(dve, dve_setup).link
            token_stats(dve, link, k)
            dve.wait_ge(loaded, LOADS)
            PRE_LINKS, MAIN_LINKS = 5, 1

            def step(r, pre, main):
                b = r + 1
                bpar = b % 2
                if pre:
                    plink = Chain(dve, dve_pre, b * PRE_LINKS).link

                def pre_norm():
                    for c in range(TILES):
                        ins = normalize(dve, k, xn[:, c, :], b * TILES + c)
                    ins.then_inc(xn_ready, 1)

                def pre_conv():
                    dve.wait_ge(hT_ready, b + 1)
                    plink(dve.tensor_scalar(u[:, :], hT[:, bpar, 0:S], conv_w[:, 0:1], None, ALU.mult))
                    plink(dve.scalar_tensor_tensor(u[:, :], hT[:, bpar, 1:S + 1], conv_w[:, 1:2], u[:, :], ALU.mult, ALU.add))
                    dve.scalar_tensor_tensor(u[:, :], hT[:, bpar, 2:S + 2], conv_w[:, 2:3], u[:, :], ALU.mult, ALU.add).then_inc(u_ready, 1)

                def pre_parts():
                    dve.wait_ge(bc_ready, 2 * b + 2)
                    plink(dve.tensor_tensor(bc[:, :], bc[:, :], bcp[:, bpar, :], ALU.subtract))
                    dve.tensor_copy(bcp[BC:2 * BC, bpar, :], bc[BC:2 * BC, :])
                    plink(dve.tensor_copy(bcp[2 * BC:3 * BC, bpar, :], bc[2 * BC:3 * BC, :]))
                    lo = bcp[2 * BC:3 * BC, bpar, :]
                    dve.tensor_tensor(lo, bc[2 * BC:3 * BC, :], lo, ALU.subtract).then_inc(parts_ready, 1)

                def pre_abs():
                    dve.wait_ge(zb_ready, b + 2)
                    dve.scalar_tensor_tensor(na[:, :], zb[:, :], -1.0, zb[:, :], ALU.mult, ALU.min).then_inc(na_ready, 1)

                def pre_dt():
                    dve.wait_ge(log_ready, b + 2)
                    plink(dve.scalar_tensor_tensor(dt[:, bpar, :], zb[:, :], 0.0, pl[:, :], ALU.max, ALU.add))
                    dve.tensor_tensor(dtx[:, bpar, :], dt[:, bpar, :], hT[:, bpar, 1:S + 1], ALU.mult).then_inc(dt_ready, 1)

                if not main:
                    pre_norm(), pre_conv(), pre_parts(), pre_abs(), pre_dt()
                    return
                par = r % 2
                dve.wait_ge(dt_ready, r + 2)
                for n in range(N):
                    q = r * N + n
                    dve.wait_ge(state_bc, q + 1)
                    dve.tensor_tensor(dBx[:, n % 2, :], dtx[:, par, :], bb[n % 2][:, :], ALU.mult).then_inc(dBx_ready, 1)
                    dve.wait_ge(dA_ready, q + 1)
                    dve.wait_ge(dBx_ready, q + 1)
                    dve.tensor_tensor_scan(hs[:, n % 2, :], dA[:, n % 4, :], dBx[:, n % 2, :], 0.0, ALU.mult, ALU.add).then_inc(scan_done, 1)
                    dve.wait_ge(scan_done, q + 5)
                    dve.wait_ge(y_acc, q + 1)
                    dve.tensor_tensor(ch[:, n % 4, :], hs[:, n % 2, :], cb[n % 2][:, :], ALU.mult).then_inc(ch_ready, 1)
                    if pre:
                        for at, f in ((0, pre_norm), (3, pre_conv), (7, pre_parts), (8, pre_abs), (15, pre_dt)):
                            if n == at:
                                f()
                dve.wait_ge(y_acc, (r + 1) * N + 4)
                dve.wait_ge(yg_ready, r + 1)
                dve.scalar_tensor_tensor(yT[:, :], hT[:, par, 1:S + 1], dco[:, 0:1], yb[:, :], ALU.mult, ALU.add).then_inc(yT_ready, 1)
                dve.wait_ge(out_done, r + 1)
                x = k.x[:, bass.ds(r * TILES, TILES), :]
                dve.tensor_tensor(x, x, postb[:, :].rearrange("p (c n) -> p c n", c=TILES), ALU.add).then_inc(x_ready, 1)

            rounds(dve, step)


def experts(nc, d, k, out):
    SLOTS = ET + 1
    LOW = 2.0 ** 11
    with ExitStack() as ctx:
        def sb(name, shape, dt=F32):
            return ctx.enter_context(nc.sbuf_tensor(name, shape, dt))

        def ps(name):
            return ctx.enter_context(nc.psum_tensor(name, [P, 512], F32))

        def sem(name):
            return ctx.enter_context(nc.semaphore(name))

        w_up = sb("w_up", [P, E, EF])
        w_down = sb("w_down", [P, ET, D])
        ws_up = sb("ws_up", [P, EF])
        ws_down = sb("ws_down", [EF, D])
        cent = sb("cent", [E, D])
        centT = sb("centT", [P, E])
        ebias = sb("ebias", [P, E])
        sel = sb("sel_e", [P, ET, P], FP16)
        xn = sb("e_xn", [P, TILES, D])
        hT = sb("e_hT", [P, 2, S])
        hTr = sb("e_hTr", [P, S])
        biased = sb("biased", [P, TILES, E])
        rest = sb("rest", [P, TILES, E])
        top = sb("top", [P, TILES, TOPK])
        sig = sb("sig", [P, TILES, E])
        wsum = sb("wsum", [P, TILES])
        cw = sb("cw", [P, TILES, 2, E])
        parts = sb("cw_parts", [P, 2, S], FP16)
        low = sb("cw_low", [P, S])
        act_u = sb("act_u", [P, 2, S])
        hid = sb("e_hid", [P, 4, S])
        yg = sb("e_yg", [P, S])
        ub = [ps(f"ub{i}") for i in range(2)]
        cb = [ps(f"e_cb{i}") for i in range(2)]
        yb, preb, routeb, postb = ps("e_yb"), ps("e_preb"), ps("routeb"), ps("e_postb")
        up_loaded, loaded, consts = sem("up_loaded"), sem("e_loaded"), sem("e_consts")
        cent_psum, cent_ready = sem("cent_psum"), sem("cent_ready")
        xn_ready, xT_done, hT_ready, aff_done, sig_ready, cw_ready, cwT_done, high_ready, low_read, parts_ready = (
            sem("e_" + n) for n in ("xn_ready", "xT_done", "hT_ready", "aff_done", "sig_ready", "cw_ready", "cwT_done",
                                    "high_ready", "low_read", "parts_ready"))
        biased_ready, top_ready = sem("biased_ready"), sem("top_ready")
        u_done, c_done, silu_ready, hid_ready, down_done, yg_ready, turned, x_ready = (
            sem("e_" + n) for n in ("u_done", "c_done", "silu_ready", "hid_ready", "down_done", "yg_ready", "turned", "x_ready"))
        stored, passed = sem("stored"), sem("e_passed")
        dve_setup, dve_pre = sem("e_dve_setup"), sem("e_dve_pre")
        block = ctx.enter_context(nc.Block())
        CREDITS = {silu_ready: 2, hid_ready: 2, down_done: 4, yg_ready: 1, turned: 1, x_ready: 1, parts_ready: 2, low_read: 1,
                   biased_ready: 1, top_ready: 1, aff_done: 1, cwT_done: 1}
        LOADS = 5 * 16
        PRE_LINKS = 7

        def rounds(eng, step):
            step(-1, pre=True, main=False, post=False)
            step(0, pre=True, main=True, post=False)
            with eng.Fori(1, B - 1) as r:
                step(r, pre=True, main=True, post=True)
            step(B - 1, pre=False, main=True, post=True)
            step(B, pre=False, main=False, post=True)

        @block.sync
        def _(sp):
            f = "L1_ffn_"
            sp.dma_start(cent[:, :], d[f + "centroids"]).then_inc(loaded, 16)
            sp.dma_start(ebias[:, :], d[f + "expert_biases"].partition_broadcast(P)).then_inc(loaded, 16)
            sp.dma_start(ws_up[:, :], d[f + "Ws_up"]).then_inc(loaded, 16)
            sp.dma_start(ws_down[:, :], d[f + "Ws_down"]).then_inc(loaded, 16)
            sp.dma_start(w_up[:, :, :], d[f + "W_up"].rearrange("e d f -> d e f")).then_inc(up_loaded, 16)
            sp.dma_start(w_down[:, :, :], d[f + "W_down"].rearrange("(t a) f d -> (a f) t d", a=2)).then_inc(loaded, 16)
            with sp.Fori(0, B) as r:
                sp.wait_ge(x_ready, r + 2)
                sp.dma_start(out[r, :, :].rearrange("(i p) d -> p i d", p=P), k.x[:, bass.ds(r * TILES, TILES), :]).then_inc(stored, 16)
            sp.wait_ge(stored, B * 16)

        @block.gpsimd
        def _(pool):
            for s, n in CREDITS.items():
                pool.sem_inc(s, n)
            pool.memset(sel[:, :, :], 0.0).then_inc(consts, 1)
            pool.wait_ge(consts, 1)
            for a in range(2):
                for base, fill in ((0, 1.0), (E, 1.0 / LOW)):
                    view = sel[:, :, a * EF:(a + 1) * EF]
                    pool.affine_select(out=view, in_=view, compare_op=ALU.not_equal, fill=fill, base=-base - a,
                                       pattern=[[-2, ET], [0, EF]], channel_multiplier=1).then_inc(consts, 1)
                    pool.wait_ge(consts, 2 + 2 * a + (1 if base else 0))

        @block.tensor
        def _(pe):
            pe.wait_ge(loaded, LOADS)
            pe.wait_ge(up_loaded, 16)
            pe.wait_ge(consts, 5)
            pe.transpose(preb[:, 0:E], cent[:, :], k.ident[0:E, 0:E]).then_inc(cent_psum, 1)
            pe.wait_ge(cent_ready, 1)

            def step(r, pre, main, post):
                b = r + 1

                def pre_turn():
                    pe.wait_ge(xn_ready, b + 1)
                    pe.wait_ge(low_read, b + 1)
                    for c in range(TILES):
                        mm = pe.transpose(preb[:, c * P:(c + 1) * P], xn[:, c, :], k.ident[:, :])
                    mm.then_inc(xT_done, 1)

                def route():
                    pe.wait_ge(hT_ready, 2 * b + 2)
                    pe.wait_ge(sig_ready, b) if main else None
                    pe.wait_ge(biased_ready, b + 1)
                    for c in range(TILES):
                        mm = pe.matmul(routeb[:, c * E:(c + 1) * E], hTr[:, c * P:(c + 1) * P], centT[:, :], start=True, stop=True)
                    mm.then_inc(aff_done, 1)

                def turn_weights():
                    pe.wait_ge(cw_ready, b + 1)
                    for c in range(TILES):
                        mm = pe.transpose(preb[:, c * P:(c + 1) * P], cw[:, c, :, :].rearrange("p a e -> p (a e)"), k.ident[:, :])
                    mm.then_inc(cwT_done, 1)

                def down(T):
                    q = r * SLOTS + T
                    pe.wait_ge(hid_ready, q + 3)
                    if T == 0:
                        pe.wait_ge(yg_ready, r + 1)
                    rows = P if T < ET else EF
                    w = w_down[:, T, :] if T < ET else ws_down[:, :]
                    pe.matmul(yb[:, :], w, hid[0:rows, T % 4, :], start=(T == 0), stop=(T == ET)).then_inc(down_done, 1)

                def turn_back():
                    pe.wait_ge(yg_ready, r + 1)
                    pe.wait_ge(x_ready, r)
                    for c in range(TILES):
                        mm = pe.transpose(postb[:, c * P:(c + 1) * P], yg[:, c * P:(c + 1) * P], k.ident[:, :])
                    mm.then_inc(turned, 1)

                if main:
                    pe.wait_ge(parts_ready, r + 3)
                    for T in range(SLOTS):
                        q = r * SLOTS + T
                        fresh = 2 if T == 0 else 1
                        pe.wait_ge(silu_ready, q + fresh)
                        pe.sem_inc(passed, 1)
                        if T < ET:
                            pe.matmul(ub[T % 2][:, :], w_up[:, 2 * T:2 * T + 2, :].rearrange("p a f -> p (a f)"), hT[:, r % 2, :],
                                      start=True, stop=True).then_inc(u_done, 1)
                            pe.wait_ge(hid_ready, q + fresh)
                            pe.matmul(cb[T % 2][:, :], sel[:, T, :], parts[:, r % 2, :], start=True, stop=True).then_inc(c_done, 1)
                        else:
                            pe.matmul(ub[T % 2][0:EF, :], ws_up[:, :], hT[:, r % 2, :], start=True, stop=True).then_inc(u_done, 1)
                        if T >= 2:
                            down(T - 2)
                        if post and T == 2:
                            turn_back()
                        if pre:
                            for at, f in ((4, pre_turn), (8, route), (20, turn_weights)):
                                if T == at:
                                    f()
                    down(SLOTS - 2)
                    down(SLOTS - 1)
                elif pre:
                    pre_turn(), route(), turn_weights()
                else:
                    turn_back()

            rounds(pe, step)

        @block.scalar
        def _(act):
            act.wait_ge(cent_psum, 1)
            act.activation(centT[:, :], preb[:, 0:E], ACT.Copy).then_inc(cent_ready, 1)
            act.wait_ge(cent_ready, 1)

            def step(r, pre, main, post):
                b = r + 1

                def pre_h():
                    act.wait_ge(xT_done, b + 1)
                    act.wait_ge(aff_done, b + 1)
                    for to in (hT[:, b % 2, :], hTr[:, :]):
                        act.activation(to, preb[:, :], ACT.Identity, scale=k.mod[:, 1, 4, bass.ds(b, 1)],
                                       bias=k.mod[:, 1, 3, bass.ds(b, 1)]).then_inc(hT_ready, 1)

                def sigmoid():
                    act.wait_ge(cw_ready, b) if main else None
                    act.wait_ge(biased_ready, b + 2)
                    act.activation(sig[:, :, :].rearrange("p c e -> p (c e)"), routeb[:, 0:TILES * E], ACT.Sigmoid).then_inc(sig_ready, 1)

                def high():
                    act.wait_ge(cwT_done, b + 2)
                    act.wait_ge(parts_ready, b + 2)
                    act.activation(parts[:, b % 2, :], preb[:, :], ACT.Copy).then_inc(high_ready, 1)

                if main:
                    for T in range(SLOTS):
                        q = r * SLOTS + T
                        act.wait_ge(u_done, q + 1)
                        act.wait_ge(hid_ready, q + (2 if T == 0 else 1))
                        rows = P if T < ET else EF
                        act.activation(act_u[0:rows, T % 2, :], ub[T % 2][0:rows, :], ACT.Silu).then_inc(silu_ready, 1)
                        if pre:
                            for at, f in ((5, pre_h), (9, sigmoid), (21, high)):
                                if T == at:
                                    f()
                    act.wait_ge(down_done, (r + 1) * SLOTS + 4)
                    act.wait_ge(turned, r + 1)
                    act.activation(yg[:, :], yb[:, :], ACT.Copy, scale=k.mod[:, 1, 5, bass.ds(r, 1)]).then_inc(yg_ready, 1)
                elif pre:
                    pre_h(), sigmoid(), high()

            rounds(act, step)

        @block.vector
        def _(dve):
            link = Chain(dve, dve_setup).link
            token_stats(dve, link, k)
            dve.wait_ge(loaded, LOADS)

            def step(r, pre, main, post):
                b = r + 1

                def pre_norm():
                    for c in range(TILES):
                        ins = normalize(dve, k, xn[:, c, :], b * TILES + c)
                    ins.then_inc(xn_ready, 1)

                def weights():
                    dve.wait_ge(aff_done, b + 2)
                    dve.wait_ge(cwT_done, b + 1)
                    chain = Chain(dve, dve_pre, b * PRE_LINKS)
                    link = chain.link
                    dve.tensor_tensor(biased[:, :, :], routeb[:, 0:TILES * E].rearrange("p (c e) -> p c e", c=TILES),
                                      ebias[:, :].unsqueeze(1).broadcast_to([P, TILES, E]), ALU.add).then_inc(biased_ready, 1)
                    dve.wait_ge(loaded, LOADS)
                    dve.wait_ge(biased_ready, b + 2)
                    for c in range(TILES):
                        ins = dve.max(top[:, c, :], biased[:, c, :])
                    ins.then_inc(top_ready, 1)
                    dve.wait_ge(loaded, LOADS)
                    dve.wait_ge(top_ready, b + 2)
                    for c in range(TILES):
                        ins = dve.match_replace(rest[:, c, :], top[:, c, :], biased[:, c, :], NEG)
                    link(ins)
                    link(dve.tensor_tensor(rest[:, :, :], rest[:, :, :], biased[:, :, :], ALU.not_equal))
                    dve.wait_ge(sig_ready, b + 1)
                    link(dve.tensor_tensor(rest[:, :, :], rest[:, :, :], sig[:, :, :], ALU.mult))
                    link(dve.tensor_reduce(wsum[:, :], rest[:, :, :], AX, ALU.add))
                    link(dve.tensor_scalar(wsum[:, :], wsum[:, :], 1e-8, None, ALU.add))
                    link(dve.reciprocal(wsum[:, :], wsum[:, :]))
                    link(dve.tensor_tensor(rest[:, :, :], rest[:, :, :], wsum[:, :].unsqueeze(2).broadcast_to([P, TILES, E]), ALU.mult))
                    dve.tensor_copy(cw[:, :, :, :], rest[:, :, :].unsqueeze(2).broadcast_to([P, TILES, 2, E])).then_inc(cw_ready, 1)
                    assert chain.n == PRE_LINKS

                def split():
                    dve.wait_ge(high_ready, b + 1)
                    lo = parts[E:2 * E, b % 2, :]
                    dve.tensor_tensor(low[E:2 * E, :], preb[E:2 * E, :], lo, ALU.subtract).then_inc(low_read, 1)
                    dve.wait_ge(low_read, b + 2)
                    dve.tensor_scalar(lo, low[E:2 * E, :], LOW, None, ALU.mult).then_inc(parts_ready, 1)

                def residual():
                    dve.wait_ge(turned, r + 1)
                    x = k.x[:, bass.ds((r - 1) * TILES, TILES), :]
                    dve.tensor_tensor(x, x, postb[:, :].rearrange("p (c n) -> p c n", c=TILES), ALU.add).then_inc(x_ready, 1)

                if main:
                    for T in range(SLOTS):
                        q = r * SLOTS + T
                        dve.wait_ge(silu_ready, q + 3)
                        dve.wait_ge(down_done, q + (4 if T == 0 else 3 if T < 4 else 1))
                        if T < ET:
                            dve.wait_ge(c_done, r * ET + T + 1)
                            dve.tensor_tensor(hid[:, T % 4, :], act_u[:, T % 2, :], cb[T % 2][:, :], ALU.mult).then_inc(hid_ready, 1)
                        else:
                            dve.tensor_copy(hid[0:EF, T % 4, :], act_u[0:EF, T % 2, :]).then_inc(hid_ready, 1)
                        if post and T == 3:
                            residual()
                        if pre:
                            for at, f in ((2, pre_norm), (9, weights), (21, split)):
                                if T == at:
                                    f()
                elif pre:
                    pre_norm(), weights(), split()
                else:
                    residual()

            rounds(dve, step)


def kernel(**inputs):
    import concourse.bacc as bacc
    from concourse.bass_utils import run_bass_kernel_spmd

    nc = bacc.Bacc("TRN2", target_bir_lowering=False, num_devices=1)
    arrays = {name: np.ascontiguousarray(a) for name, a in inputs.items()}
    d = {name: nc.dram_tensor(name, a.shape, mybir.dt.from_np(a.dtype), kind="ExternalInput").ap() for name, a in arrays.items()}
    out = nc.dram_tensor("out_0_dram", (B, S, D), F32, kind="ExternalOutput").ap()
    build(nc, d, out)
    r = run_bass_kernel_spmd(nc, [arrays], core_ids=[0])
    return r.results[0]["out_0_dram"]
```

```python
import math
from contextlib import ExitStack

import numpy as np
import concourse.bass as bass
from concourse import mybir

F32 = mybir.dt.float32
BF16 = mybir.dt.bfloat16
FP16 = mybir.dt.float16
I32 = mybir.dt.int32
ALU = mybir.AluOpType
ACT = mybir.ActivationFunctionType
AX = mybir.AxisListType.X

B, S, D = 8, 512, 128
P = 128
TILES = S // P
H, HD = 16, 8
VD = 2 * HD
LAM_INIT = 0.8 - 0.6 * math.exp(-0.3 * 11)
EPS = 1e-5
FF = 512
N = 16
RANK = 8
E, EF, TOPK = 64, 64, 8
ET = E * EF // P

NEG = -3.0e38
INV_2PI = 1.0 / (2.0 * math.pi)
ROUND = 1.5 * 2.0 ** 23
TWO_PI_HI = 6.28125
TWO_PI_MID = float(np.float32(np.round((2 * math.pi - TWO_PI_HI) * 2.0 ** 21) / 2.0 ** 21))
TWO_PI_LO = 2 * math.pi - TWO_PI_HI - TWO_PI_MID
PI_BELOW = 3.1415925


class Chain:

    def __init__(self, eng, sem, base=0, passed=None):
        self.eng, self.sem, self.base, self.n, self.passed = eng, sem, base, 0, passed

    def link(self, ins):
        ins.then_inc(self.sem, 1)
        self.n += 1
        self.eng.wait_ge(self.sem, self.base + self.n)
        if self.passed is not None:
            self.eng.sem_inc(self.passed, 1)


def rsqrt_steps(dve, link, v, half, y, t):
    link(dve.tensor_scalar(t.bitcast(I32), v.bitcast(I32), 1, None, ALU.logical_shift_right))
    link(dve.tensor_scalar(y.bitcast(I32), t.bitcast(I32), -1.0, 1597463007.0, ALU.mult, ALU.add))
    link(dve.tensor_scalar(half, v, -0.5, None, ALU.mult))
    for _ in range(3):
        link(dve.tensor_tensor(t, y, y, ALU.mult))
        link(dve.tensor_tensor(t, t, half, ALU.mult))
        link(dve.scalar_tensor_tensor(y, t, 1.5, y, ALU.add, ALU.mult))


RSQRT_LINKS = 3 + 3 * 3


def build(nc, d, out):
    with ExitStack() as top:
        keep = shared_tiles(nc, top)
        setup(nc, d, keep)
        attention(nc, d, keep)
        ffn(nc, d, keep)
        scan(nc, d, keep)
        experts(nc, d, keep, out)


class Keep:
    pass


def shared_tiles(nc, ctx):
    k = Keep()

    def sb(name, shape, dt=F32):
        return ctx.enter_context(nc.sbuf_tensor(name, shape, dt))

    k.x = sb("x_tok", [P, B * TILES, D])
    k.ident = sb("ident", [P, P])
    k.identb = sb("identb", [P, P], BF16)
    k.ones = sb("ones", [P, P])
    k.mod = sb("mod", [P, 2, 6, B])
    k.gate_a0 = sb("gate_a0", [P, B, D])
    k.gate_b0 = sb("gate_b0", [P, B, D])
    k.neg_lam = sb("neg_lam", [P, H])
    k.stats = sb("stats", [P, B * TILES, 2])
    k.rstd = sb("rstd", [P, B * TILES])
    k.half = sb("half", [P, B * TILES])
    k.tmp = sb("rs_tmp", [P, B * TILES])
    k.bn = sb("bn", [P, B * TILES, 6])
    return k


def setup(nc, d, k):
    with ExitStack() as ctx:
        def sb(name, shape, dt=F32):
            return ctx.enter_context(nc.sbuf_tensor(name, shape, dt))

        def sem(name):
            return ctx.enter_context(nc.semaphore(name))

        c = sb("c", [B, 2, D])
        sc = sb("silu_c", [B, 2, D])
        cT = sb("silu_cT", [P, 2, B])
        cTb = sb("silu_cTb", [P, B, P])
        wmod = sb("wmod", [P, 2, 6 * D])
        lq = sb("lq", [1, 4, H * HD])
        lp = sb("lp", [1, 2, H * HD])
        ls = sb("ls", [1, 2, H])
        le = sb("le", [1, 2, H])
        lr = sb("lr", [1, H])
        gs = sb("gs", [P, 2, 2, 2, B])
        gsr = sb("gsr", [P, 2, B, D])
        psum_c = ctx.enter_context(nc.psum_tensor("psum_c", [P, 512], F32))
        psum_m = ctx.enter_context(nc.psum_tensor("psum_m", [P, 512], F32))
        psum_l = ctx.enter_context(nc.psum_tensor("psum_l", [P, 512], F32))
        psum_g = ctx.enter_context(nc.psum_tensor("psum_g", [P, 4, 512], F32))
        x_loaded, w_loaded = sem("x_loaded"), sem("w_loaded")
        consts = sem("setup_consts")
        silu_done, cT_psum, cT_ready, mod_psum, gate_psum = (
            sem("silu_done"), sem("cT_psum"), sem("cT_ready"), sem("mod_psum"), sem("gate_psum"))
        lp_ready, le_ready, lr_ready, lam_psum = sem("lp_ready"), sem("le_ready"), sem("lr_ready"), sem("lam_psum")
        dve_chain = sem("setup_dve")
        block = ctx.enter_context(nc.Block())

        @block.sync
        def _(sp):
            for l, name in enumerate(("L0_c", "L1_c")):
                sp.dma_start(c[:, l, :], d[name]).then_inc(w_loaded, 16)
            for l, name in enumerate(("L0_wmod", "L1_wmod")):
                sp.dma_start(wmod[:, l, :], d[name]).then_inc(w_loaded, 16)
            for j, name in enumerate(("lq1", "lk1", "lq2", "lk2")):
                sp.dma_start(lq[0:1, j, :], d["L0_attn_" + name].rearrange("(a h) d -> a (h d)", a=1)).then_inc(w_loaded, 16)
            sp.dma_start(k.x[:, :, :], d["L0_attn_x"].rearrange("b (i p) d -> p (b i) d", p=P)).then_inc(x_loaded, 16)

        @block.gpsimd
        def _(pool):
            pool.memset(k.ident[:, :], 0.0).then_inc(consts, 1)
            pool.memset(k.identb[:, :], 0.0).then_inc(consts, 1)
            pool.memset(k.ones[:, :], 1.0).then_inc(consts, 1)
            pool.wait_ge(consts, 3)
            for m in (k.ident, k.identb):
                pool.affine_select(out=m[:, :], in_=m[:, :], compare_op=ALU.not_equal, fill=1.0, base=0,
                                   pattern=[[-1, P]], channel_multiplier=1).then_inc(consts, 1)

        @block.scalar
        def _(act):
            act.wait_ge(w_loaded, 16 * 8)
            act.activation(sc[:, :, :], c[:, :, :], ACT.Silu).then_inc(silu_done, 1)
            act.wait_ge(lp_ready, 1)
            act.activation(le[0:1, :, :], ls[0:1, :, :], ACT.Exp).then_inc(le_ready, 1)

        @block.tensor
        def _(pe):
            pe.wait_ge(consts, 5)
            pe.wait_ge(silu_done, 1)
            for l in range(2):
                mm = pe.transpose(psum_c[:, 8 * l:8 * l + B], sc[:, l, :], k.ident[0:B, 0:B])
            mm.then_inc(cT_psum, 1)
            pe.wait_ge(cT_ready, 2)
            for l in range(2):
                for j in range(6):
                    at = (6 * l + j) * B
                    mm = pe.matmul(psum_m[:, at:at + B], wmod[:, l, j * D:(j + 1) * D], cT[:, l, :], start=True, stop=True)
            mm.then_inc(mod_psum, 1)
            for n, j in enumerate((2, 5)):
                for b in range(B):
                    mm = pe.matmul(psum_g[:, 2 * n + b // 4, (b % 4) * D:(b % 4 + 1) * D], cTb[:, b, :],
                                   wmod[:, 0, j * D:(j + 1) * D], start=True, stop=True)
            mm.then_inc(gate_psum, 1)
            pe.wait_ge(lr_ready, 1)
            pe.matmul(psum_l[:, 0:H], k.ones[0:1, :], lr[0:1, :], start=True, stop=True).then_inc(lam_psum, 1)

        @block.vector
        def _(dve):
            link = Chain(dve, dve_chain).link
            dve.wait_ge(w_loaded, 16 * 8)
            for j in range(2):
                link(dve.tensor_tensor(lp[0:1, j, :], lq[0:1, 2 * j, :], lq[0:1, 2 * j + 1, :], ALU.mult))
            dve.tensor_reduce(ls[0:1, :, :], lp[0:1, :, :].rearrange("a j (h d) -> a j h d", d=HD), AX, ALU.add).then_inc(lp_ready, 1)
            dve.wait_ge(cT_psum, 1)
            dve.tensor_copy(cT[:, :, :], psum_c[:, 0:2 * B].rearrange("p (l b) -> p l b", l=2)).then_inc(cT_ready, 1)
            dve.tensor_copy(cTb[:, :, :], psum_c[:, 0:B].unsqueeze(2).broadcast_to([P, B, P])).then_inc(cT_ready, 1)
            dve.wait_ge(le_ready, 1)
            dve.scalar_tensor_tensor(lr[0:1, :], le[0:1, 1, :], -LAM_INIT, le[0:1, 0, :], ALU.add, ALU.subtract).then_inc(lr_ready, 1)
            dve.wait_ge(mod_psum, 1)
            link(dve.tensor_copy(k.mod[:, :, :, :], psum_m[:, 0:12 * B].rearrange("p (l j b) -> p l j b", l=2, j=6)))
            for j in (1, 4):
                link(dve.tensor_scalar(k.mod[:, :, j, :], k.mod[:, :, j, :], 1.0, None, ALU.add))
            for n, j in enumerate((2, 5)):
                g = k.mod[:, :, j, :]
                link(dve.scalar_tensor_tensor(gs[:, 0, n, :, :], g, -1.0, g, ALU.mult, ALU.max))
                link(dve.tensor_scalar(gs[:, 0, n, :, :], gs[:, 0, n, :, :], 0.25, None, ALU.max))
                link(dve.tensor_scalar(gs[:, 1, n, :, :], g, 0.0, 2.0, ALU.is_ge, ALU.mult))
                link(dve.scalar_tensor_tensor(g, gs[:, 1, n, :, :], -1.0, gs[:, 0, n, :, :], ALU.add, ALU.mult))
            dve.wait_ge(gate_psum, 1)
            for n, gate in enumerate((k.gate_a0, k.gate_b0)):
                g = gate[:, :, :].rearrange("p b d -> p (b d)")
                s0, s1 = (gsr[:, j, :, :].rearrange("p b d -> p (b d)") for j in range(2))
                link(dve.tensor_copy(g, psum_g[:, 2 * n:2 * n + 2, :].rearrange("p b d -> p (b d)")))
                link(dve.scalar_tensor_tensor(s0, g, -1.0, g, ALU.mult, ALU.max))
                link(dve.tensor_scalar(s0, s0, 0.25, None, ALU.max))
                link(dve.tensor_scalar(s1, g, 0.0, 2.0, ALU.is_ge, ALU.mult))
                link(dve.scalar_tensor_tensor(g, s1, -1.0, s0, ALU.add, ALU.mult))
            dve.wait_ge(lam_psum, 1)
            link(dve.tensor_copy(k.neg_lam[:, :], psum_l[:, 0:H]))
            dve.wait_ge(x_loaded, 16)
            for t in range(B * TILES):
                last = dve.bn_stats(k.bn[:, t, :], k.x[:, t, :])
            link(last)
            for t in range(B * TILES):
                last = dve.bn_aggr(k.stats[:, t, :], k.bn[:, t, :])
            link(last)
            v = k.stats[:, :, 1]
            link(dve.tensor_scalar(v, v, EPS, None, ALU.add))
            link(dve.tensor_copy(k.half[:, :], v))
            rsqrt_steps(dve, link, k.half[:, :], k.bn[:, :, 0], k.rstd[:, :], k.tmp[:, :])


GROUPS = 8
MAPS = 4
RING = 4
Q_ORDER, K_ORDER = (0, 0, 0, 1, 1, 2), (0, 1, 2, 0, 1, 0)
SROWS = len(Q_ORDER) * HD
NROWS = 3
KROWS = 96
UNITS = 10
SCALE = 1.0 / math.sqrt(HD)


def lagged(r, g, n):
    return (r, g - n) if g >= n else (r - 1, g - n + GROUPS)


def attention(nc, d, k):
    q_dram = nc.dram_tensor("q_stacks", [B, GROUPS, SROWS + NROWS, MAPS, S], BF16).ap()
    k_dram = nc.dram_tensor("k_stacks", [B, GROUPS, SROWS, MAPS, S], BF16).ap()
    with ExitStack() as ctx:
        def sb(name, shape, dt=F32):
            return ctx.enter_context(nc.sbuf_tensor(name, shape, dt))

        def ps(name):
            return ctx.enter_context(nc.psum_tensor(name, [P, 512], F32))

        def sem(name):
            return ctx.enter_context(nc.semaphore(name))

        wraw = sb("wraw", [P, 4, D])
        wqk = sb("wqk", [P, 4, D])
        wv = sb("wv", [P, H * VD])
        wo = sb("wo", [P, 2, D])
        causal = sb("causal", [P, P], BF16)
        zeros = sb("zeros", [B * GROUPS, NROWS, S], BF16)
        xn = sb("xn", [P, TILES, D])
        hT = sb("hT", [P, S])
        parts = sb("parts", [P, 2, 3, S], BF16)
        res = sb("res", [P, S])
        vst = sb("vst", [P, 2, TILES, H, 2 * VD])
        qs, ks = sb("qs", [KROWS, RING, MAPS, S], BF16), sb("ks", [KROWS, RING, MAPS, S], BF16)
        vs = sb("vs", [P, 2, TILES, 2, 2 * VD])
        pT = sb("pT", [P, 2, UNITS, 512])
        bmax = sb("bmax", [P, 2, MAPS, 10])
        qmax = sb("qmax", [P, TILES, MAPS])
        nparts = sb("nparts", [MAPS, 2, NROWS, S], BF16)
        nres = sb("nres", [MAPS, S])
        o_sb = sb("o_sb", [P, 2, S])
        oT = sb("oT", [P, 2, TILES, 2 * H, VD + 1])
        rc = sb("rc", [P, TILES, H, 2])
        og, o2, oc, sq = (sb(n, [P, TILES * H, VD]) for n in ("og", "o2", "oc", "sq"))
        msum, vsum, vhalf, orstd, otmp = (sb(n, [P, TILES * H]) for n in ("msum", "vsum", "vhalf", "orstd", "otmp"))
        merged = sb("merged", [P, TILES, H * VD])
        mT = sb("mT", [P, 2, S])
        gated = sb("gated", [P, TILES, D])
        p1b = [ps(f"p1b{i}") for i in range(2)]
        p2b = [ps(f"p2b{i}") for i in range(2)]
        ob, turnb, prepb, sideb = ps("ob"), ps("turnb"), ps("prepb"), ps("sideb")

        w_loaded, slots_set, zeros_saved, w_ready = sem("attn_w"), sem("slots_set"), sem("zeros_saved"), sem("w_ready")
        xn_ready, xnT_done, hT_ready, qk_done, hi_ready, res_ready, mid_ready, split_ready, v_done, v_ready = (
            sem(n) for n in ("xn_ready", "xnT_done", "hT_ready", "qk_done", "hi_ready", "res_ready", "mid_ready",
                             "split_ready", "v_done", "v_ready"))
        qk_saved = [sem(f"qk_saved{s}") for s in range(2)]
        stack_loaded = [sem(f"stack_loaded{s}") for s in range(RING)]
        neg_loaded = [sem(f"neg_loaded{s}") for s in range(RING)]
        first_unit, first_read, second_unit, exp_done, masked, vs_ready, av_done, o_read, oT_done, oT_read = (
            sem(n) for n in ("first_unit", "first_read", "second_unit", "exp_done", "masked", "vs_ready", "av_done", "o_read",
                             "oT_done", "oT_read"))
        qmax_ready, neg_psum, neg_high, neg_read, neg_mid, neg_ready = (
            sem(n) for n in ("qmax_ready", "neg_psum", "neg_high", "neg_read", "neg_mid", "neg_ready"))
        rc_ready, og_ready, merged_ready, mT_done, mT_ready, wo_done, gated_ready, post_done = (
            sem(n) for n in ("rc_ready", "og_ready", "merged_ready", "mT_done", "mT_ready", "wo_done", "gated_ready", "post_done"))
        pool_own, dve_post, passed = sem("pool_own"), sem("dve_post"), sem("passed")
        block = ctx.enter_context(nc.Block())

        CREDITS = {first_read: 2, second_unit: RING * UNITS, exp_done: 2, vs_ready: GROUPS + 1, av_done: 2, o_read: 1, oT_done: 2,
                   oT_read: 4, neg_psum: 1, neg_ready: 1, xnT_done: 1, res_ready: 1, split_ready: 1, v_done: 1, v_ready: 1,
                   qk_saved[0]: 16, qk_saved[1]: 16, og_ready: 2, merged_ready: 1, mT_done: 1, wo_done: 1, gated_ready: 3}
        W_LOADS = 6 * 16
        SAVES = len(Q_ORDER) * 16
        NEG_LOADS = NROWS * 16
        LOADS = 2 * 16

        def use(r, g):
            return r * (GROUPS // RING) + g // RING

        def rounds(eng, slot):
            def round_(r, first, last):
                for g in range(GROUPS):
                    def on(n):
                        return not (first and g < n) and not (last and g >= n)
                    slot(r, g, on, prep=not last and not (isinstance(r, int) and r == B - 1), post=not first)

            for g in range(GROUPS):
                slot(-1, g, lambda n: False, prep=True, post=False)
            round_(0, True, False)
            with eng.Fori(1, B - 1) as r:
                round_(r, False, False)
            round_(B - 1, False, False)
            round_(B, False, True)

        @block.sync
        def _(sp):
            for j, name in enumerate(("Wq1", "Wq2", "Wk1", "Wk2")):
                sp.dma_start(wraw[:, j, :], d["L0_attn_" + name]).then_inc(w_loaded, 16)
            sp.dma_start(wv[:, :], d["L0_attn_Wv"]).then_inc(w_loaded, 16)
            sp.dma_start(wo[:, :, :], d["L0_attn_Wo"].rearrange("(c p) n -> p c n", p=P)).then_inc(w_loaded, 16)
            sp.wait_ge(slots_set, 6)
            for m in range(MAPS):
                sp.dma_start(q_dram[:, :, SROWS:SROWS + NROWS, m, :].rearrange("b g s t -> (b g) s t"), zeros[:, :, :]).then_inc(zeros_saved, 16)
            sp.wait_ge(zeros_saved, MAPS * 16)

            def load(r, g):
                slot = g % RING
                if g < 2:
                    for s in range(2):
                        sp.wait_ge(qk_saved[s], (r + 1) * 2 * SAVES + 16)
                sp.wait_ge(second_unit, (r * GROUPS + g + 1) * UNITS)
                for tile, rows, dram in ((qs, SROWS + NROWS, q_dram), (ks, SROWS, k_dram)):
                    sp.dma_start(tile[0:rows, slot, :, :].rearrange("p m t -> p (m t)"),
                                 dram[r, g, :, :, :].rearrange("p m t -> p (m t)")).then_inc(stack_loaded[slot], 16)

            def slot(r, g, on, prep, post):
                if on(1):
                    rn, gn = lagged(r, g, 1)
                    sp.wait_ge(neg_ready, rn * GROUPS + gn + 2)
                    for s in range(NROWS):
                        sp.dma_start(qs[SROWS + s:SROWS + s + 1, gn % RING, :, :].rearrange("p m t -> p (m t)"),
                                     nparts[:, gn % 2, s, :]).then_inc(neg_loaded[gn % RING], 16)
                if prep and 1 <= g < 5:
                    b, j = r + 1, g - 1
                    sp.wait_ge(split_ready, b * 4 + j + 2)
                    dram, order = (q_dram, Q_ORDER) if j < 2 else (k_dram, K_ORDER)
                    for n, part in enumerate(order):
                        to = dram[b, :, n * HD:(n + 1) * HD, :, :].rearrange("g r (h j) t -> j g (r h) t", j=2)[j % 2]
                        sp.dma_start(to, parts[:, j % 2, part, :]).then_inc(qk_saved[j % 2], 16)
                rl, gl = (r, g + 2) if g + 2 < GROUPS else (r + 1, g + 2 - GROUPS)
                if g + 2 >= GROUPS and prep or g + 2 < GROUPS and on(0):
                    load(rl, gl)

            rounds(sp, slot)
            sp.wait_ge(post_done, B)

        @block.gpsimd
        def _(pool):
            pool.memset(qs[:, :, :, :], 0.0).then_inc(slots_set, 1)
            pool.memset(ks[:, :, :, :], 1.0).then_inc(slots_set, 1)
            pool.memset(zeros[:, :, :], 0.0).then_inc(slots_set, 1)
            pool.memset(causal[:, :], 0.0).then_inc(slots_set, 1)
            pool.wait_ge(slots_set, 4)
            pool.affine_select(out=causal[:, :], in_=causal[:, :], compare_op=ALU.is_ge, fill=NEG, base=0,
                               pattern=[[-1, P]], channel_multiplier=1).then_inc(slots_set, 1)
            pool.memset(vst[:, :, :, :, :], 1.0).then_inc(slots_set, 1)
            for s, n in CREDITS.items():
                pool.sem_inc(s, n)

            def slot(r, g, on, prep, post):
                if on(1):
                    rn, gn = lagged(r, g, 1)
                    G = rn * GROUPS + gn
                    pool.wait_ge(neg_read, G + 1)
                    pool.sem_inc(passed, 1)
                    pool.tensor_copy(nparts[:, gn % 2, 1, :], nres[:, :]).then_inc(neg_mid, 1)
                    pool.wait_ge(neg_mid, G + 1)
                    pool.tensor_tensor(nparts[:, gn % 2, 2, :], nres[:, :], nparts[:, gn % 2, 1, :], ALU.subtract).then_inc(neg_ready, 1)
                if prep and 1 <= g < 5:
                    j, J = g - 1, (r + 1) * 4 + g - 1
                    pool.wait_ge(res_ready, J + 2)
                    pool.sem_inc(passed, 1)
                    pool.tensor_copy(parts[:, j % 2, 1, :], res[:, :]).then_inc(mid_ready, 1)
                    pool.wait_ge(mid_ready, J + 1)
                    pool.tensor_tensor(parts[:, j % 2, 2, :], res[:, :], parts[:, j % 2, 1, :], ALU.subtract).then_inc(split_ready, 1)
                if post and g == 4:
                    pb = r - 1
                    o = oT[:, pb % 2 if isinstance(pb, int) else (r + 1) % 2, :, :, 0:VD].rearrange("p c (h j) e -> p (c h) j e", j=2)
                    rcv = rc[:, :, :, :].rearrange("p c h j -> p (c h) j")
                    full = [P, TILES * H, VD]
                    pool.wait_ge(rc_ready, pb + 1)
                    pool.wait_ge(merged_ready, pb + 1)
                    pool.tensor_tensor(og[:, :, :], o[:, :, 0, :], rcv[:, :, 0].unsqueeze(2).broadcast_to(full), ALU.mult).then_inc(pool_own, 1)
                    pool.tensor_tensor(o2[:, :, :], o[:, :, 1, :], rcv[:, :, 1].unsqueeze(2).broadcast_to(full), ALU.mult).then_inc(pool_own, 1)
                    pool.wait_ge(pool_own, pb * 2 + 2)
                    pool.tensor_tensor(og[:, :, :], og[:, :, :], o2[:, :, :], ALU.add).then_inc(og_ready, 1)
                if on(2):
                    r2, g2 = lagged(r, g, 2)
                    G = r2 * GROUPS + g2
                    a = g2 % 2
                    pool.wait_ge(v_ready, (r2 + 1) * TILES + 1)
                    pool.wait_ge(av_done, G + 1)
                    pool.sem_inc(passed, 1)
                    pool.tensor_copy(vs[:, a, :, :, :], vst[:, r2 % 2, :, 2 * g2:2 * g2 + 2, :]).then_inc(vs_ready, 1)
                    pool.wait_ge(exp_done, (G + 1) * UNITS + 2)
                    pool.sem_inc(passed, 1)
                    for block_ap, n in ((pT[:, a, :, 0:P], UNITS), (pT[:, a, 1:8:2, 384:512], 4), (pT[:, a, 8:10, 256:384], 2)):
                        pool.affine_select(out=block_ap, in_=block_ap, compare_op=ALU.is_ge, fill=0.0, base=0,
                                           pattern=[[0, n], [1, P]], channel_multiplier=-1).then_inc(masked, 1)

            rounds(pool, slot)

        @block.scalar
        def _(act):
            act.wait_ge(slots_set, 6)

            def slot(r, g, on, prep, post):
                b = r + 1
                if on(2):
                    r2, g2 = lagged(r, g, 2)
                    G2 = r2 * GROUPS + g2
                    act.wait_ge(av_done, G2 + 1)
                for u in range(UNITS):
                    if on(2):
                        act.wait_ge(second_unit, G2 * UNITS + u + 1 + RING * UNITS)
                        act.activation(pT[:, g2 % 2, u, :], p2b[u % 2][:, :], ACT.Exp, scale=SCALE).then_inc(exp_done, 1)
                    if u == 3 and on(1):
                        rn, gn = lagged(r, g, 1)
                        act.wait_ge(neg_psum, rn * GROUPS + gn + 2)
                        if not isinstance(rn, int) or rn * GROUPS + gn >= 2:
                            rp, gp = lagged(rn, gn, 2)
                            act.wait_ge(neg_loaded[gp % RING], (use(rp, gp) + 1) * NEG_LOADS)
                        act.activation(nparts[:, gn % 2, 0, :], turnb[0:MAPS, :], ACT.Copy, scale=-1.0).then_inc(neg_high, 1)
                    if post and g == 7 and u in (2, 6):
                        c, pb = u // 4, r - 1
                        act.wait_ge(mT_done, pb * 2 + c + 2)
                        act.wait_ge(wo_done, pb + 1)
                        act.activation(mT[:, c, :], sideb[:, :], ACT.Copy).then_inc(mT_ready, 1)
                if prep and 1 <= g < 5:
                    j, J = g - 1, b * 4 + g - 1
                    act.wait_ge(qk_done, J + 1)
                    act.wait_ge(qk_saved[j % 2], (b * 2 + j // 2) * SAVES + 16)
                    act.activation(parts[:, j % 2, 0, :], prepb[:, :], ACT.Copy).then_inc(hi_ready, 1)
                if prep and 2 <= g < 6:
                    c, V = g - 2, b * TILES + g - 2
                    act.wait_ge(v_done, V + 2)
                    if c == 0:
                        act.wait_ge(vs_ready, b * GROUPS + 1)
                    act.activation(vst[:, b % 2, c, :, 0:VD], sideb[:, 0:H * VD].rearrange("p (h e) -> p h e", h=H), ACT.Copy).then_inc(v_ready, 1)
                if on(3):
                    r3, g3 = lagged(r, g, 3)
                    G3 = r3 * GROUPS + g3
                    act.wait_ge(av_done, G3 + 3)
                    act.wait_ge(oT_done, G3 + 1)
                    act.activation(o_sb[:, g3 % 2, :], ob[:, :], ACT.Copy).then_inc(o_read, 1)
                if on(4):
                    r4, g4 = lagged(r, g, 4)
                    G4 = r4 * GROUPS + g4
                    act.wait_ge(oT_done, G4 + 3)
                    if g4 == 0:
                        act.wait_ge(og_ready, r4 + 1)
                    act.activation(oT[:, r4 % 2, :, g4 * MAPS:(g4 + 1) * MAPS, :],
                                   turnb[:, :].rearrange("p (c m e) -> p c m e", c=TILES, m=MAPS)[:, :, :, 0:VD + 1],
                                   ACT.Copy).then_inc(oT_read, 1)
                if prep and g == 0:
                    act.wait_ge(xnT_done, b + 2)
                    act.wait_ge(v_done, b * TILES + 1)
                    act.activation(hT[:, :], prepb[:, :], ACT.Identity, scale=k.mod[:, 0, 1, bass.ds(b, 1)],
                                   bias=k.mod[:, 0, 0, bass.ds(b, 1)]).then_inc(hT_ready, 1)

            rounds(act, slot)

        @block.tensor
        def _(pe):
            pe.wait_ge(w_loaded, W_LOADS)
            pe.wait_ge(w_ready, 1)
            pe.wait_ge(slots_set, 6)

            def first_unit_of(G, slot, u):
                bank = p1b[u % 2]
                pe.wait_ge(first_read, G * UNITS + u + 1)
                blocks = {0: [(u, 3, 0)], 1: [(u - 4, 2, 0), (u - 4, 0, 3)],
                          2: [(2 * u - 16, 1, 0), (2 * u - 15, 1, 2)]}[u // 4]
                for m, c, at in blocks:
                    pe.matmul(bank[:, at * P:(at + c + 1) * P], qs[:, slot, m, c * P:(c + 1) * P], ks[:, slot, m, 0:(c + 1) * P],
                              start=True, stop=False, skip_group_check=True)
                    mm = pe.matmul(bank[:, (at + c) * P:(at + c + 1) * P], k.identb[:, :], causal[:, :],
                                   start=False, stop=True, skip_group_check=True)
                mm.then_inc(first_unit, 1)

            def second_unit_of(G, slot, u):
                bank = p2b[u % 2]
                pe.wait_ge(exp_done, G * UNITS + u + 1)
                if u < 8:
                    m = u // 2
                    blocks = [(m, 0, 0)] if u % 2 == 0 else [(m, 1, 0), (m, 3, 384)]
                else:
                    blocks = [(2 * u - 16, 2, 0), (2 * u - 15, 2, 256)]
                for m, c, at in blocks:
                    n = S - c * P
                    mm = pe.matmul(bank[:, at:at + n], ks[:, slot, m, c * P:(c + 1) * P], qs[:, slot, m, c * P:S],
                                   start=True, stop=True, skip_group_check=True)
                mm.then_inc(second_unit, 1)

            def product(G, a):
                pe.wait_ge(masked, 3 * G + 3)
                pe.wait_ge(vs_ready, G + GROUPS + 2)
                pe.wait_ge(o_read, G + 1)
                for c in range(TILES):
                    for m in range(MAPS):
                        u, at = {0: (2 * m, 0), 1: (2 * m + 1, 0), 2: (8 + m // 2, 256 * (m % 2)), 3: (2 * m + 1, 384)}[c]
                        n = S - c * P
                        mm = pe.matmul(ob[32 * m:32 * m + 32, c * P:S], vs[:, a, c, m // 2, :], pT[:, a, u, at:at + n],
                                       start=(c == 0), stop=(c == TILES - 1), skip_group_check=True)
                mm.then_inc(av_done, 1)

            def slot(r, g, on, prep, post):
                b, pb = r + 1, r - 1
                if on(0):
                    pe.wait_ge(stack_loaded[g % RING], (use(r, g) + 1) * LOADS)
                if on(2):
                    r2, g2 = lagged(r, g, 2)
                    pe.wait_ge(neg_loaded[g2 % RING], (use(r2, g2) + 1) * NEG_LOADS)
                for u in range(UNITS):
                    if on(2):
                        second_unit_of(r2 * GROUPS + g2, g2 % RING, u)
                    if on(0):
                        first_unit_of(r * GROUPS + g, g % RING, u)
                    if u == 3 and on(1):
                        rn, gn = lagged(r, g, 1)
                        pe.wait_ge(qmax_ready, rn * GROUPS + gn + 1)
                        pe.wait_ge(oT_read, rn * GROUPS + gn + 1)
                        for c in range(TILES):
                            mm = pe.transpose(turnb[0:MAPS, c * P:(c + 1) * P], qmax[:, c, :], k.ident[:, :])
                        mm.then_inc(neg_psum, 1)
                    if post and g == 7 and u in (1, 5):
                        c = u // 4
                        pe.wait_ge(merged_ready, pb + 2)
                        if c == 0:
                            pe.wait_ge(v_ready, (min(r + 2, B) if isinstance(r, int) else r + 2) * TILES + 1)
                        else:
                            pe.wait_ge(mT_ready, pb * 2 + 1)
                        for i in range(TILES):
                            mm = pe.transpose(sideb[:, i * P:(i + 1) * P], merged[:, i, c * P:(c + 1) * P], k.ident[:, :])
                        mm.then_inc(mT_done, 1)
                if prep and 1 <= g < 5:
                    j, J = g - 1, b * 4 + g - 1
                    pe.wait_ge(hT_ready, b + 1)
                    pe.wait_ge(res_ready, J + 1)
                    pe.matmul(prepb[:, :], wqk[:, j, :], hT[:, :], start=True, stop=True).then_inc(qk_done, 1)
                if prep and 2 <= g < 6:
                    c, V = g - 2, b * TILES + g - 2
                    if c == 0:
                        pe.wait_ge(gated_ready, r + 2)
                    pe.wait_ge(v_ready, V + 1)
                    pe.matmul(sideb[:, 0:H * VD], hT[:, c * P:(c + 1) * P], wv[:, :], start=True, stop=True).then_inc(v_done, 1)
                if on(3):
                    r3, g3 = lagged(r, g, 3)
                    product(r3 * GROUPS + g3, g3 % 2)
                if post and g == 7:
                    pe.wait_ge(mT_ready, pb * 2 + 2)
                    for i in range(TILES):
                        for c in range(2):
                            mm = pe.matmul(sideb[:, i * P:(i + 1) * P], mT[:, c, i * P:(i + 1) * P], wo[:, c, :], start=(c == 0), stop=(c == 1))
                    mm.then_inc(wo_done, 1)
                if on(4):
                    r4, g4 = lagged(r, g, 4)
                    G4 = r4 * GROUPS + g4
                    pe.wait_ge(o_read, G4 + 2)
                    if on(1):
                        rn, gn = lagged(r, g, 1)
                        pe.wait_ge(neg_read, rn * GROUPS + gn + 1)
                    else:
                        pe.wait_ge(oT_read, G4 + 4)
                    for c in range(TILES):
                        mm = pe.transpose(turnb[:, c * P:(c + 1) * P], o_sb[:, g4 % 2, c * P:(c + 1) * P], k.ident[:, :])
                    mm.then_inc(oT_done, 1)
                if prep and g == 0:
                    pe.wait_ge(xn_ready, b + 1)
                    pe.wait_ge(res_ready, b * 4 + 1)
                    for c in range(TILES):
                        mm = pe.transpose(prepb[:, c * P:(c + 1) * P], xn[:, c, :], k.ident[:, :])
                    mm.then_inc(xnT_done, 1)

            rounds(pe, slot)

        @block.vector
        def _(dve):
            dve.wait_ge(w_loaded, W_LOADS)
            for j in range(4):
                ins = dve.tensor_copy(wqk[:, j, :].rearrange("p (g e h) -> p g e h", e=HD, h=2),
                                      wraw[:, j, :].rearrange("p (g h e) -> p g e h", h=2, e=HD))
            ins.then_inc(w_ready, 1)

            def slot(r, g, on, prep, post):
                b, pb = r + 1, r - 1
                G = r * GROUPS + g
                if prep and g == 0:
                    dve.wait_ge(xnT_done, b + 1)
                    for c in range(TILES):
                        ins = normalize(dve, k, xn[:, c, :], b * TILES + c)
                    ins.then_inc(xn_ready, 1)
                for u in range(UNITS):
                    if on(0):
                        dve.wait_ge(first_unit, G * UNITS + u + 1)
                        bank = p1b[u % 2][:, :]
                        if u < 8:
                            to = bmax[:, g % 2, u % 4, 4 * (u // 4):4 * (u // 4) + 4]
                            src = bank.rearrange("p (c t) -> p c t", c=4)
                        else:
                            to = bmax[:, g % 2, 2 * (u - 8):2 * (u - 8) + 2, 8:10]
                            src = bank.rearrange("p (m c t) -> p m c t", m=2, c=2)
                        dve.tensor_reduce(to, src, AX, ALU.max).then_inc(first_read, 1)
                    if u == 4 and on(1):
                        rn, gn = lagged(r, g, 1)
                        Gn = rn * GROUPS + gn
                        dve.wait_ge(neg_high, Gn + 1)
                        dve.wait_ge(neg_ready, Gn + 1)
                        dve.scalar_tensor_tensor(nres[:, :], turnb[0:MAPS, :], -1.0, nparts[:, gn % 2, 0, :], ALU.mult, ALU.subtract).then_inc(neg_read, 1)
                if on(0):
                    dve.wait_ge(neg_psum, G + 1)
                    dve.wait_ge(first_read, (G + 1) * UNITS + 2)
                    for c, lo, n in ((3, 0, 4), (2, 4, 3), (0, 7, 1), (1, 8, 2)):
                        ins = dve.tensor_reduce(qmax[:, c, :], bmax[:, g % 2, :, lo:lo + n], AX, ALU.max)
                    ins.then_inc(qmax_ready, 1)
                if prep and 1 <= g < 5:
                    j, J = g - 1, b * 4 + g - 1
                    dve.wait_ge(hi_ready, J + 1)
                    dve.wait_ge(split_ready, J + 1)
                    dve.tensor_tensor(res[:, :], prepb[:, :], parts[:, j % 2, 0, :], ALU.subtract).then_inc(res_ready, 1)
                full = [P, TILES * H, VD]
                wide = lambda t: t[:, :].unsqueeze(2).broadcast_to(full)
                link = Chain(dve, dve_post, pb * POST_LINKS).link
                if post and g == 4:
                    dve.wait_ge(oT_read, (pb + 1) * GROUPS + 4)
                    dve.wait_ge(og_ready, pb + 2)
                    link(dve.reciprocal(rc[:, :, :, :].rearrange("p c h j -> p c (h j)"), oT[:, (r + 1) % 2, :, :, VD]))
                    dve.tensor_tensor(rc[:, :, :, 1], rc[:, :, :, 1], k.neg_lam[:, :].unsqueeze(1).broadcast_to([P, TILES, H]),
                                      ALU.mult).then_inc(rc_ready, 1)
                if post and g == 5:
                    link = Chain(dve, dve_post, pb * POST_LINKS + 1).link
                    dve.wait_ge(og_ready, pb + 3)
                    link(dve.tensor_reduce(msum[:, :], og[:, :, :], AX, ALU.add))
                    link(dve.scalar_tensor_tensor(oc[:, :, :], wide(msum), -1.0 / VD, og[:, :, :], ALU.mult, ALU.add))
                    link(dve.tensor_tensor(sq[:, :, :], oc[:, :, :], oc[:, :, :], ALU.mult))
                    link(dve.tensor_reduce(vsum[:, :], sq[:, :, :], AX, ALU.add))
                    link(dve.tensor_scalar(vsum[:, :], vsum[:, :], 1.0 / VD, EPS, ALU.mult, ALU.add))
                    rsqrt_steps(dve, link, vsum[:, :], vhalf[:, :], orstd[:, :], otmp[:, :])
                    dve.wait_ge(mT_done, pb * 2 + 1)
                    dve.scalar_tensor_tensor(merged[:, :, :].rearrange("p c (h e) -> p (c h) e", e=VD), oc[:, :, :], 1.0 - LAM_INIT,
                                             wide(orstd), ALU.mult, ALU.mult).then_inc(merged_ready, 1)
                if post and g == 7:
                    dve.wait_ge(wo_done, pb + 2)
                    dve.tensor_tensor(gated[:, :, :], sideb[:, :].rearrange("p (c n) -> p c n", c=TILES),
                                      k.gate_a0[:, bass.ds(pb, 1), :].broadcast_to([P, TILES, D]), ALU.mult).then_inc(gated_ready, 1)
                    dve.wait_ge(gated_ready, pb + 4)
                    x = k.x[:, bass.ds(pb * TILES, TILES), :]
                    dve.tensor_tensor(x, x, gated[:, :, :], ALU.add).then_inc(post_done, 1)

            rounds(dve, slot)


POST_LINKS = 1 + 5 + RSQRT_LINKS


def token_stats(dve, link, k):
    for t in range(B * TILES):
        last = dve.bn_stats(k.bn[:, t, :], k.x[:, t, :])
    link(last)
    for t in range(B * TILES):
        last = dve.bn_aggr(k.stats[:, t, :], k.bn[:, t, :])
    link(last)
    link(dve.tensor_scalar(k.bn[:, :, 1], k.stats[:, :, 1], EPS, None, ALU.add))
    rsqrt_steps(dve, link, k.bn[:, :, 1], k.half[:, :], k.rstd[:, :], k.tmp[:, :])


def normalize(dve, k, xn, tile):
    return dve.tensor_scalar(xn, k.x[:, tile, :], k.stats[:, tile, 0:1], k.rstd[:, bass.ds(tile, 1)], ALU.subtract, ALU.mult)


def ffn(nc, d, k):
    FT = FF // P
    with ExitStack() as ctx:
        def sb(name, shape, dt=F32):
            return ctx.enter_context(nc.sbuf_tensor(name, shape, dt))

        def ps(name):
            return ctx.enter_context(nc.psum_tensor(name, [P, 512], F32))

        def sem(name):
            return ctx.enter_context(nc.semaphore(name))

        w1 = sb("w1", [P, FF])
        w2 = sb("w2", [P, FT, D])
        b2 = sb("b2", [P, D])
        col = sb("col", [P, 4, FT])
        th = sb("th", [P, 8, FT])
        coef = sb("coef", [P, FT])
        xn = sb("f_xn", [P, 2, TILES, D])
        hT = sb("f_hT", [P, 2, S])
        hid = sb("hid", [P, 2, FT, S])
        arg = sb("arg", [P, 2, FT, S])
        turns = sb("turns", [P, 2, FT, S])
        gated = sb("f_gated", [P, 2, TILES, D])
        tpb = [ps(f"tpb{a}") for a in range(2)]
        upb = [ps(f"upb{a}") for a in range(2)]
        outb = [ps(f"outb{a}") for a in range(2)]
        loaded, angle, th_sin, ready = sem("ffn_loaded"), sem("angle"), sem("th_sin"), sem("ffn_credits")
        xn_ready, xT_done, hT_ready, up_done, hid_ready, arg_ready, sin_ready, act_ready, out_done, x_ready = (
            sem(n) for n in ("f_xn_ready", "f_xT_done", "f_hT_ready", "up_done", "hid_ready", "arg_ready", "sin_ready",
                             "act_ready", "out_done", "f_x_ready"))
        dve_setup, dve_chain = sem("ffn_dve_setup"), sem("ffn_dve")
        block = ctx.enter_context(nc.Block())
        CREDITS = {hT_ready: 2, hid_ready: 2, out_done: 2, x_ready: 2}
        LOADS = 7 * 16

        @block.sync
        def _(sp):
            for s, n in CREDITS.items():
                sp.sem_inc(s, n)
            sp.dma_start(w1[:, :], d["L0_ffn_W1"]).then_inc(loaded, 16)
            for n, name in enumerate(("b1", "quantum_phases", "quantum_weights_real", "quantum_weights_imag")):
              with nc.allow_non_contiguous_dma("one value of each hidden unit"):
                sp.dma_start(col[:, n, :], d["L0_ffn_" + name].rearrange("(j p) -> p j", p=P)).then_inc(loaded, 16)
            sp.dma_start(w2[:, :, :], d["L0_ffn_W2"].rearrange("(j p) n -> p j n", p=P)).then_inc(loaded, 16)
            sp.dma_start(b2[:, :], d["L0_ffn_b2"].partition_broadcast(P)).then_inc(loaded, 16)
            sp.wait_ge(x_ready, B + 2)

        def reduce_angle(eng, link, out, angle_, n):
            link(eng.tensor_scalar(n, angle_, INV_2PI, ROUND, ALU.mult, ALU.add))
            link(eng.tensor_scalar(n, n, ROUND, None, ALU.subtract))
            link(eng.scalar_tensor_tensor(out, n, -TWO_PI_HI, angle_, ALU.mult, ALU.add))
            link(eng.scalar_tensor_tensor(out, n, -TWO_PI_MID, out, ALU.mult, ALU.add))
            link(eng.scalar_tensor_tensor(out, n, -TWO_PI_LO, out, ALU.mult, ALU.add))
            return eng.tensor_scalar(out, out, PI_BELOW, -PI_BELOW, ALU.min, ALU.max)

        @block.tensor
        def _(pe):
            pe.wait_ge(loaded, LOADS)
            with pe.Fori(0, B // 2) as it:
                for a in range(2):
                    T = it * 2 + a
                    pe.wait_ge(xn_ready, T + 1)
                    pe.wait_ge(hT_ready, T + 1)
                    for c in range(TILES):
                        mm = pe.transpose(tpb[a][:, c * P:(c + 1) * P], xn[:, a, c, :], k.ident[:, :])
                    mm.then_inc(xT_done, 1)
                for a in range(2):
                    T = it * 2 + a
                    pe.wait_ge(hT_ready, T + 3)
                    for j in range(FT):
                        pe.wait_ge(hid_ready, T * FT + j + 1)
                        pe.matmul(upb[j % 2][:, :], w1[:, j * P:(j + 1) * P], hT[:, a, :], start=True, stop=True).then_inc(up_done, 1)
                for a in range(2):
                    T = it * 2 + a
                    pe.wait_ge(x_ready, T + 1)
                    pe.matmul(outb[a][:, :].rearrange("p (c n) -> p c n", c=TILES), k.ident[:, :],
                              b2[:, :].unsqueeze(1).broadcast_to([P, TILES, D]), start=True, stop=False, skip_group_check=True)
                    pe.wait_ge(act_ready, T + 1)
                    for j in range(FT):
                        for c in range(TILES):
                            mm = pe.matmul(outb[a][:, c * P:(c + 1) * P], hid[:, a, j, c * P:(c + 1) * P], w2[:, j, :],
                                           start=False, stop=(j == FT - 1), skip_group_check=True)
                    mm.then_inc(out_done, 1)

        @block.scalar
        def _(act):
            act.wait_ge(angle, 1)
            act.activation(th[:, 6:8, :], th[:, 4:6, :], ACT.Sin).then_inc(th_sin, 1)
            act.wait_ge(loaded, LOADS)
            with act.Fori(0, B // 2) as it:
                for a in range(2):
                    T = it * 2 + a
                    act.wait_ge(xT_done, T + 1)
                    act.activation(hT[:, a, :], tpb[a][:, :], ACT.Identity, scale=k.mod[:, 0, 4, bass.ds(T, 1)],
                                   bias=k.mod[:, 0, 3, bass.ds(T, 1)]).then_inc(hT_ready, 1)
                for a in range(2):
                    T = it * 2 + a
                    act.wait_ge(out_done, T + 1)
                    for j in range(FT):
                        act.wait_ge(up_done, T * FT + j + 1)
                        act.activation(hid[:, a, j, :], upb[j % 2][:, :], ACT.Identity, bias=col[:, 0, j:j + 1]).then_inc(hid_ready, 1)
                for a in range(2):
                    T = it * 2 + a
                    act.wait_ge(arg_ready, T + 1)
                    act.activation(turns[:, a, :, :], arg[:, a, :, :], ACT.Sin).then_inc(sin_ready, 1)

        @block.vector
        def _(dve):
            link = Chain(dve, dve_setup).link
            token_stats(dve, link, k)
            dve.wait_ge(loaded, LOADS)
            theta = col[:, 1, :]
            link(reduce_angle(dve, link, th[:, 4, :], theta, th[:, 0, :]))
            link(dve.scalar_tensor_tensor(th[:, 1, :], th[:, 4, :], -1.0, th[:, 4, :], ALU.mult, ALU.max))
            dve.tensor_scalar(th[:, 5, :], th[:, 1, :], -1.0, math.pi / 2, ALU.mult, ALU.add).then_inc(angle, 1)
            dve.wait_ge(th_sin, 1)
            link(dve.tensor_tensor(th[:, 2, :], th[:, 7, :], col[:, 2, :], ALU.mult))
            link(dve.tensor_tensor(th[:, 3, :], th[:, 6, :], col[:, 3, :], ALU.mult))
            link(dve.tensor_tensor(th[:, 2, :], th[:, 2, :], th[:, 3, :], ALU.add))
            link(dve.scalar_tensor_tensor(coef[:, :], th[:, 2, :], 0.1, col[:, 3, :], ALU.mult, ALU.mult))
            LINKS = 2 * 8
            with dve.Fori(0, B // 2) as it:
                chain = Chain(dve, dve_chain, it * LINKS)
                link = chain.link
                for a in range(2):
                    T = it * 2 + a
                    for c in range(TILES):
                        ins = normalize(dve, k, xn[:, a, c, :], T * TILES + c)
                    ins.then_inc(xn_ready, 1)
                for a in range(2):
                    T = it * 2 + a
                    for j in range(FT):
                        dve.wait_ge(hid_ready, T * FT + j + 3)
                        ins = dve.tensor_scalar(arg[:, a, j, :], hid[:, a, j, :], 0.1, col[:, 1, j:j + 1], ALU.mult, ALU.add)
                    link(ins)
                    flat = lambda t: t[:, a, :, :].rearrange("p j t -> p (j t)")
                    reduce_angle(dve, link, flat(arg), flat(arg), flat(turns)).then_inc(arg_ready, 1)
                for a in range(2):
                    T = it * 2 + a
                    dve.wait_ge(sin_ready, T + 1)
                    for j in range(FT):
                        ins = dve.scalar_tensor_tensor(hid[:, a, j, :], turns[:, a, j, :], coef[:, j:j + 1], hid[:, a, j, :], ALU.mult, ALU.add)
                    link(ins)
                    dve.tensor_scalar(flat_of(hid, a), flat_of(hid, a), 0.0, None, ALU.max).then_inc(act_ready, 1)
                for a in range(2):
                    T = it * 2 + a
                    dve.wait_ge(out_done, T + 3)
                    link(dve.tensor_tensor(gated[:, a, :, :], outb[a][:, :].rearrange("p (c n) -> p c n", c=TILES),
                                           k.gate_b0[:, bass.ds(T, 1), :].broadcast_to([P, TILES, D]), ALU.mult))
                    x = k.x[:, bass.ds(T * TILES, TILES), :]
                    dve.tensor_tensor(x, x, gated[:, a, :, :], ALU.add).then_inc(x_ready, 1)
                assert chain.n == LINKS, chain.n


def flat_of(t, a):
    return t[:, a, :, :].rearrange("p j t -> p (j t)")


LOG1P = (1.0, -0.49999892711639404, 0.33329710364341736, -0.24951615929603577, 0.1966327428817749, -0.1526966691017151,
         0.10543623566627502, -0.05637361481785774, 0.019542528316378593, -0.0031760570127516985)


def scan(nc, d, k):
    BC = 2 * N
    with ExitStack() as ctx:
        def sb(name, shape, dt=F32):
            return ctx.enter_context(nc.sbuf_tensor(name, shape, dt))

        def ps(name):
            return ctx.enter_context(nc.psum_tensor(name, [P, 512], F32))

        def sem(name):
            return ctx.enter_context(nc.semaphore(name))

        conv_w = sb("conv_w", [P, 3])
        wbc = sb("wbc", [P, 3, BC])
        bbc = sb("bbc", [3 * BC, 1])
        wdt = sb("wdt", [P, RANK])
        bdt = sb("bdt", [RANK, 1])
        wdtp = sb("wdtp", [RANK, D])
        bdtp = sb("bdtp", [P, 1])
        nA = sb("nA", [P, N])
        dco = sb("dco", [P, 1])
        sel = sb("sel", [3 * BC, BC, P], BF16)
        xn = sb("s_xn", [P, TILES, D])
        hT = sb("s_hT", [P, 2, S + 2])
        u = sb("u", [P, S])
        us = sb("us", [P, S])
        bc = sb("bc", [3 * BC, S])
        bcp = sb("bcp", [3 * BC, 2, S], BF16)
        t1 = sb("t1", [RANK, S])
        zb, na, ee, pl = (sb(n, [P, S]) for n in ("zb", "na", "ee", "pl"))
        dt = sb("dt", [P, 2, S])
        dtx = sb("dtx", [P, 2, S])
        dA = sb("dA", [P, 4, S])
        dBx = sb("dBx", [P, 2, S])
        hs = sb("hs", [P, 2, S])
        ch = sb("ch", [P, 4, S])
        yT = sb("yT", [P, S])
        yg = sb("yg", [P, S])
        preb, pre2 = ps("s_preb"), ps("s_pre2")
        bb = [ps(f"bb{i}") for i in range(2)]
        cb = [ps(f"cb{i}") for i in range(2)]
        yb = ps("yb")
        postb = ps("s_postb")
        loaded, sel_ready, consts, nA_ready = sem("s_loaded"), sem("sel_ready"), sem("s_consts"), sem("nA_ready")
        xn_ready, xT_done, hT_ready, u_ready, us_ready, bc_psum, bc_ready, dtr_psum, t1_ready, z_psum, zb_ready, na_ready, ee_ready, log_ready, dt_ready, parts_ready = (
            sem("s_" + n) for n in ("xn_ready", "xT_done", "hT_ready", "u_ready", "us_ready", "bc_psum", "bc_ready", "dtr_psum",
                                    "t1_ready", "z_psum", "zb_ready", "na_ready", "ee_ready", "log_ready", "dt_ready", "parts_ready"))
        state_bc, dA_ready, dBx_ready, scan_done, ch_ready, y_acc, yT_ready, yg_ready, out_done, x_ready = (
            sem("s_" + n) for n in ("state_bc", "dA_ready", "dBx_ready", "scan_done", "ch_ready", "y_acc", "yT_ready", "yg_ready",
                                    "out_done", "x_ready"))
        dve_setup, dve_pre, dve_main, pool_log = sem("s_dve_setup"), sem("s_dve_pre"), sem("s_dve_main"), sem("s_pool_log")
        passed, act_passed = sem("s_passed"), sem("s_act_passed")
        block = ctx.enter_context(nc.Block())
        CREDITS = {x_ready: 1, y_acc: 4, ch_ready: 2, yg_ready: 1, zb_ready: 1, parts_ready: 1, yT_ready: 1,
                   scan_done: 4, dt_ready: 1, log_ready: 1}
        LOADS = (3 + 3 + 6) * 16
        LOG_LINKS = 2 * (len(LOG1P) - 2) + 1

        def rounds(eng, step):
            step(-1, pre=True, main=False)
            with eng.Fori(0, B - 1) as r:
                step(r, pre=True, main=True)
            step(B - 1, pre=False, main=True)

        @block.sync
        def _(sp):
            a = "L1_attn_"
            for j in range(3):
                sp.dma_start(wbc[:, j, :], d[a + "W_bc"]).then_inc(loaded, 16)
                sp.dma_start(bbc[j * BC:(j + 1) * BC, :], d[a + "b_bc"].unsqueeze(1)).then_inc(loaded, 16)
            with nc.allow_non_contiguous_dma("three values of each feature"):
                sp.dma_start(conv_w[:, :], d[a + "conv_w"].rearrange("c p -> p c")).then_inc(loaded, 16)
            sp.dma_start(wdt[:, :], d[a + "W_dt"]).then_inc(loaded, 16)
            sp.dma_start(bdt[:, :], d[a + "b_dt"].unsqueeze(1)).then_inc(loaded, 16)
            sp.dma_start(wdtp[:, :], d[a + "W_dtp"]).then_inc(loaded, 16)
            sp.dma_start(bdtp[:, :], d[a + "b_dtp"].unsqueeze(1)).then_inc(loaded, 16)
            sp.dma_start(dco[:, :], d[a + "Dcoeff"].unsqueeze(1)).then_inc(loaded, 16)
            sp.dma_start(nA[:, :], d[a + "A_log"]).then_inc(nA_ready, 16)
            sp.wait_ge(x_ready, B + 1)

        @block.gpsimd
        def _(pool):
            for s, n in CREDITS.items():
                pool.sem_inc(s, n)
            pool.memset(sel[:, :, :], 0.0).then_inc(consts, 1)
            pool.memset(hT[:, :, :], 0.0).then_inc(consts, 1)
            pool.wait_ge(consts, 2)
            for j in range(3):
                pool.affine_select(out=sel[:, :, :], in_=sel[:, :, :], compare_op=ALU.not_equal, fill=1.0, base=-j * BC,
                                   pattern=[[-1, BC], [0, P]], channel_multiplier=1).then_inc(sel_ready, 1)
                pool.wait_ge(sel_ready, j + 1)

            def step(r, pre, main):
                if pre:
                    b = r + 1
                    pool.wait_ge(ee_ready, b + 1)
                    pool.wait_ge(dt_ready, b + 1)
                    pool.sem_inc(passed, 1)
                    chain = Chain(pool, pool_log, b * LOG_LINKS, passed)
                    link = chain.link
                    p, e = pl[:, :], ee[:, :]
                    link(pool.tensor_scalar(p, e, LOG1P[-1], LOG1P[-2], ALU.mult, ALU.add))
                    for c in LOG1P[-3::-1]:
                        link(pool.tensor_tensor(p, p, e, ALU.mult))
                        link(pool.tensor_scalar(p, p, 1.0, c, ALU.mult, ALU.add))
                    pool.tensor_tensor(p, p, e, ALU.mult).then_inc(log_ready, 1)
                    assert chain.n == LOG_LINKS, chain.n

            rounds(pool, step)

        @block.tensor
        def _(pe):
            pe.wait_ge(loaded, LOADS)
            pe.wait_ge(sel_ready, 3)

            def step(r, pre, main):
                b = r + 1

                def pre_turn():
                    pe.wait_ge(xn_ready, b + 1)
                    pe.wait_ge(zb_ready, b + 1)
                    for c in range(TILES):
                        mm = pe.transpose(preb[:, c * P:(c + 1) * P], xn[:, c, :], k.ident[:, :])
                    mm.then_inc(xT_done, 1)

                def pre_bc():
                    pe.wait_ge(us_ready, b + 1)
                    pe.matmul(preb[0:3 * BC, :], wbc[:, :, :].rearrange("p j n -> p (j n)"), us[:, :], start=True, stop=True).then_inc(bc_psum, 1)
                    pe.matmul(pre2[0:RANK, :], wdt[:, :], us[:, :], start=True, stop=True).then_inc(dtr_psum, 1)

                def pre_z():
                    pe.wait_ge(t1_ready, b + 1)
                    pe.wait_ge(bc_ready, 2 * b + 2)
                    pe.matmul(preb[:, :], wdtp[:, :], t1[:, :], start=True, stop=True).then_inc(z_psum, 1)

                if not main:
                    pre_turn(), pre_bc(), pre_z()
                    return
                par = r % 2
                pe.wait_ge(parts_ready, r + 2)
                for n in range(N + 2):
                    if n < N:
                        pe.wait_ge(ch_ready, r * N + n + 1)
                        pe.matmul(bb[n % 2][:, :], sel[:, n, :], bcp[:, par, :], start=True, stop=True)
                        pe.matmul(cb[n % 2][:, :], sel[:, N + n, :], bcp[:, par, :], start=True, stop=True).then_inc(state_bc, 1)
                    if n >= 2:
                        q = r * N + n - 2
                        pe.wait_ge(ch_ready, q + 3)
                        if n == 2:
                            pe.wait_ge(yT_ready, r + 1)
                        mm = pe.matmul(yb[:, :], k.ident[:, :], ch[:, (n - 2) % 4, :],
                                       start=(n == 2), stop=(n == N + 1), skip_group_check=True)
                        mm.then_inc(y_acc, 1)
                    if pre and n == 2:
                        pre_turn()
                    if pre and n == 6:
                        pre_bc()
                    if pre and n == 8:
                        pre_z()
                pe.wait_ge(yg_ready, r + 2)
                pe.wait_ge(x_ready, r + 1)
                for c in range(TILES):
                    mm = pe.transpose(postb[:, c * P:(c + 1) * P], yg[:, c * P:(c + 1) * P], k.ident[:, :])
                mm.then_inc(out_done, 1)

            rounds(pe, step)

        @block.scalar
        def _(act):
            act.wait_ge(nA_ready, 16)
            act.activation(nA[:, :], nA[:, :], ACT.Exp).then_inc(nA_ready, 1)
            act.wait_ge(nA_ready, 17)
            act.activation(nA[:, :], nA[:, :], ACT.Copy, scale=-1.0).then_inc(nA_ready, 1)
            act.wait_ge(nA_ready, 18)
            act.wait_ge(loaded, LOADS)
            act.wait_ge(consts, 2)

            def step(r, pre, main):
                b = r + 1
                bpar = b % 2

                def pre_h():
                    act.wait_ge(xT_done, b + 1)
                    act.activation(hT[:, bpar, 1:S + 1], preb[:, :], ACT.Identity, scale=k.mod[:, 1, 1, bass.ds(b, 1)],
                                   bias=k.mod[:, 1, 0, bass.ds(b, 1)]).then_inc(hT_ready, 1)

                def pre_silu():
                    act.wait_ge(u_ready, b + 1)
                    act.activation(us[:, :], u[:, :], ACT.Silu).then_inc(us_ready, 1)

                def pre_bc():
                    act.wait_ge(bc_psum, b + 1)
                    act.wait_ge(parts_ready, b + 1)
                    act.activation(bc[:, :], preb[0:3 * BC, :], ACT.Identity, bias=bbc[:, 0:1]).then_inc(bc_ready, 1)
                    act.activation(bcp[:, bpar, :], preb[0:3 * BC, :], ACT.Identity, bias=bbc[:, 0:1]).then_inc(bc_ready, 1)
                    act.wait_ge(dtr_psum, b + 1)
                    act.activation(t1[:, :], pre2[0:RANK, :], ACT.Identity, bias=bdt[:, 0:1]).then_inc(t1_ready, 1)

                def pre_z():
                    act.wait_ge(z_psum, b + 1)
                    act.wait_ge(dt_ready, b + 1)
                    act.activation(zb[:, :], preb[:, :], ACT.Identity, bias=bdtp[:, 0:1]).then_inc(zb_ready, 1)

                def pre_exp():
                    act.wait_ge(na_ready, b + 1)
                    act.wait_ge(log_ready, b + 1)
                    act.activation(ee[:, :], na[:, :], ACT.Exp).then_inc(ee_ready, 1)

                if not main:
                    pre_h(), pre_silu(), pre_bc(), pre_z(), pre_exp()
                    return
                par = r % 2
                act.wait_ge(dt_ready, r + 2)
                for n in range(N):
                    q = r * N + n
                    act.wait_ge(scan_done, q + 1)
                    act.sem_inc(act_passed, 1)
                    act.activation(dA[:, n % 4, :], dt[:, par, :], ACT.Exp, scale=nA[:, n:n + 1]).then_inc(dA_ready, 1)
                    if pre:
                        for at, f in ((2, pre_h), (4, pre_silu), (6, pre_bc), (8, pre_z), (9, pre_exp)):
                            if n == at:
                                f()
                act.wait_ge(yT_ready, r + 2)
                act.wait_ge(x_ready, r + 1)
                act.activation(yg[:, :], yT[:, :], ACT.Copy, scale=k.mod[:, 1, 2, bass.ds(r, 1)]).then_inc(yg_ready, 1)

            rounds(act, step)

        @block.vector
        def _(dve):
            link = Chain(dve, dve_setup).link
            token_stats(dve, link, k)
            dve.wait_ge(loaded, LOADS)
            PRE_LINKS, MAIN_LINKS = 5, 1

            def step(r, pre, main):
                b = r + 1
                bpar = b % 2
                if pre:
                    plink = Chain(dve, dve_pre, b * PRE_LINKS).link

                def pre_norm():
                    for c in range(TILES):
                        ins = normalize(dve, k, xn[:, c, :], b * TILES + c)
                    ins.then_inc(xn_ready, 1)

                def pre_conv():
                    dve.wait_ge(hT_ready, b + 1)
                    plink(dve.tensor_scalar(u[:, :], hT[:, bpar, 0:S], conv_w[:, 0:1], None, ALU.mult))
                    plink(dve.scalar_tensor_tensor(u[:, :], hT[:, bpar, 1:S + 1], conv_w[:, 1:2], u[:, :], ALU.mult, ALU.add))
                    dve.scalar_tensor_tensor(u[:, :], hT[:, bpar, 2:S + 2], conv_w[:, 2:3], u[:, :], ALU.mult, ALU.add).then_inc(u_ready, 1)

                def pre_parts():
                    dve.wait_ge(bc_ready, 2 * b + 2)
                    plink(dve.tensor_tensor(bc[:, :], bc[:, :], bcp[:, bpar, :], ALU.subtract))
                    dve.tensor_copy(bcp[BC:2 * BC, bpar, :], bc[BC:2 * BC, :])
                    plink(dve.tensor_copy(bcp[2 * BC:3 * BC, bpar, :], bc[2 * BC:3 * BC, :]))
                    lo = bcp[2 * BC:3 * BC, bpar, :]
                    dve.tensor_tensor(lo, bc[2 * BC:3 * BC, :], lo, ALU.subtract).then_inc(parts_ready, 1)

                def pre_abs():
                    dve.wait_ge(zb_ready, b + 2)
                    dve.scalar_tensor_tensor(na[:, :], zb[:, :], -1.0, zb[:, :], ALU.mult, ALU.min).then_inc(na_ready, 1)

                def pre_dt():
                    dve.wait_ge(log_ready, b + 2)
                    plink(dve.scalar_tensor_tensor(dt[:, bpar, :], zb[:, :], 0.0, pl[:, :], ALU.max, ALU.add))
                    dve.tensor_tensor(dtx[:, bpar, :], dt[:, bpar, :], hT[:, bpar, 1:S + 1], ALU.mult).then_inc(dt_ready, 1)

                if not main:
                    pre_norm(), pre_conv(), pre_parts(), pre_abs(), pre_dt()
                    return
                par = r % 2
                dve.wait_ge(dt_ready, r + 2)
                for n in range(N):
                    q = r * N + n
                    dve.wait_ge(state_bc, q + 1)
                    dve.tensor_tensor(dBx[:, n % 2, :], dtx[:, par, :], bb[n % 2][:, :], ALU.mult).then_inc(dBx_ready, 1)
                    dve.wait_ge(dA_ready, q + 1)
                    dve.wait_ge(dBx_ready, q + 1)
                    dve.tensor_tensor_scan(hs[:, n % 2, :], dA[:, n % 4, :], dBx[:, n % 2, :], 0.0, ALU.mult, ALU.add).then_inc(scan_done, 1)
                    dve.wait_ge(scan_done, q + 5)
                    dve.wait_ge(y_acc, q + 1)
                    dve.tensor_tensor(ch[:, n % 4, :], hs[:, n % 2, :], cb[n % 2][:, :], ALU.mult).then_inc(ch_ready, 1)
                    if pre:
                        for at, f in ((0, pre_norm), (3, pre_conv), (7, pre_parts), (8, pre_abs), (15, pre_dt)):
                            if n == at:
                                f()
                dve.wait_ge(y_acc, (r + 1) * N + 4)
                dve.wait_ge(yg_ready, r + 1)
                dve.scalar_tensor_tensor(yT[:, :], hT[:, par, 1:S + 1], dco[:, 0:1], yb[:, :], ALU.mult, ALU.add).then_inc(yT_ready, 1)
                dve.wait_ge(out_done, r + 1)
                x = k.x[:, bass.ds(r * TILES, TILES), :]
                dve.tensor_tensor(x, x, postb[:, :].rearrange("p (c n) -> p c n", c=TILES), ALU.add).then_inc(x_ready, 1)

            rounds(dve, step)


def experts(nc, d, k, out):
    SLOTS = ET + 1
    LOW = 2.0 ** 11
    with ExitStack() as ctx:
        def sb(name, shape, dt=F32):
            return ctx.enter_context(nc.sbuf_tensor(name, shape, dt))

        def ps(name):
            return ctx.enter_context(nc.psum_tensor(name, [P, 512], F32))

        def sem(name):
            return ctx.enter_context(nc.semaphore(name))

        w_up = sb("w_up", [P, E, EF])
        w_down = sb("w_down", [P, ET, D])
        ws_up = sb("ws_up", [P, EF])
        ws_down = sb("ws_down", [EF, D])
        cent = sb("cent", [E, D])
        centT = sb("centT", [P, E])
        ebias = sb("ebias", [P, E])
        sel = sb("sel_e", [P, ET, P], FP16)
        xn = sb("e_xn", [P, TILES, D])
        hT = sb("e_hT", [P, 2, S])
        hTr = sb("e_hTr", [P, S])
        biased = sb("biased", [P, TILES, E])
        rest = sb("rest", [P, TILES, E])
        top = sb("top", [P, TILES, TOPK])
        sig = sb("sig", [P, TILES, E])
        wsum = sb("wsum", [P, TILES])
        cw = sb("cw", [P, TILES, 2, E])
        parts = sb("cw_parts", [P, 2, S], FP16)
        low = sb("cw_low", [P, S])
        act_u = sb("act_u", [P, 2, S])
        hid = sb("e_hid", [P, 4, S])
        yg = sb("e_yg", [P, S])
        ub = [ps(f"ub{i}") for i in range(2)]
        cb = [ps(f"e_cb{i}") for i in range(2)]
        yb, preb, routeb, postb = ps("e_yb"), ps("e_preb"), ps("routeb"), ps("e_postb")
        up_loaded, loaded, consts = sem("up_loaded"), sem("e_loaded"), sem("e_consts")
        cent_psum, cent_ready = sem("cent_psum"), sem("cent_ready")
        xn_ready, xT_done, hT_ready, aff_done, sig_ready, cw_ready, cwT_done, high_ready, low_read, parts_ready = (
            sem("e_" + n) for n in ("xn_ready", "xT_done", "hT_ready", "aff_done", "sig_ready", "cw_ready", "cwT_done",
                                    "high_ready", "low_read", "parts_ready"))
        biased_ready, top_ready = sem("biased_ready"), sem("top_ready")
        u_done, c_done, silu_ready, hid_ready, down_done, yg_ready, turned, x_ready = (
            sem("e_" + n) for n in ("u_done", "c_done", "silu_ready", "hid_ready", "down_done", "yg_ready", "turned", "x_ready"))
        stored, passed = sem("stored"), sem("e_passed")
        dve_setup, dve_pre = sem("e_dve_setup"), sem("e_dve_pre")
        block = ctx.enter_context(nc.Block())
        CREDITS = {silu_ready: 2, hid_ready: 2, down_done: 4, yg_ready: 1, turned: 1, x_ready: 1, parts_ready: 2, low_read: 1,
                   biased_ready: 1, top_ready: 1, aff_done: 1, cwT_done: 1}
        LOADS = 5 * 16
        PRE_LINKS = 7

        def rounds(eng, step):
            step(-1, pre=True, main=False, post=False)
            step(0, pre=True, main=True, post=False)
            with eng.Fori(1, B - 1) as r:
                step(r, pre=True, main=True, post=True)
            step(B - 1, pre=False, main=True, post=True)
            step(B, pre=False, main=False, post=True)

        @block.sync
        def _(sp):
            f = "L1_ffn_"
            sp.dma_start(cent[:, :], d[f + "centroids"]).then_inc(loaded, 16)
            sp.dma_start(ebias[:, :], d[f + "expert_biases"].partition_broadcast(P)).then_inc(loaded, 16)
            sp.dma_start(ws_up[:, :], d[f + "Ws_up"]).then_inc(loaded, 16)
            sp.dma_start(ws_down[:, :], d[f + "Ws_down"]).then_inc(loaded, 16)
            sp.dma_start(w_up[:, :, :], d[f + "W_up"].rearrange("e d f -> d e f")).then_inc(up_loaded, 16)
            sp.dma_start(w_down[:, :, :], d[f + "W_down"].rearrange("(t a) f d -> (a f) t d", a=2)).then_inc(loaded, 16)
            with sp.Fori(0, B) as r:
                sp.wait_ge(x_ready, r + 2)
                sp.dma_start(out[r, :, :].rearrange("(i p) d -> p i d", p=P), k.x[:, bass.ds(r * TILES, TILES), :]).then_inc(stored, 16)
            sp.wait_ge(stored, B * 16)

        @block.gpsimd
        def _(pool):
            for s, n in CREDITS.items():
                pool.sem_inc(s, n)
            pool.memset(sel[:, :, :], 0.0).then_inc(consts, 1)
            pool.wait_ge(consts, 1)
            for a in range(2):
                for base, fill in ((0, 1.0), (E, 1.0 / LOW)):
                    view = sel[:, :, a * EF:(a + 1) * EF]
                    pool.affine_select(out=view, in_=view, compare_op=ALU.not_equal, fill=fill, base=-base - a,
                                       pattern=[[-2, ET], [0, EF]], channel_multiplier=1).then_inc(consts, 1)
                    pool.wait_ge(consts, 2 + 2 * a + (1 if base else 0))

        @block.tensor
        def _(pe):
            pe.wait_ge(loaded, LOADS)
            pe.wait_ge(up_loaded, 16)
            pe.wait_ge(consts, 5)
            pe.transpose(preb[:, 0:E], cent[:, :], k.ident[0:E, 0:E]).then_inc(cent_psum, 1)
            pe.wait_ge(cent_ready, 1)

            def step(r, pre, main, post):
                b = r + 1

                def pre_turn():
                    pe.wait_ge(xn_ready, b + 1)
                    pe.wait_ge(low_read, b + 1)
                    for c in range(TILES):
                        mm = pe.transpose(preb[:, c * P:(c + 1) * P], xn[:, c, :], k.ident[:, :])
                    mm.then_inc(xT_done, 1)

                def route():
                    pe.wait_ge(hT_ready, 2 * b + 2)
                    pe.wait_ge(sig_ready, b) if main else None
                    pe.wait_ge(biased_ready, b + 1)
                    for c in range(TILES):
                        mm = pe.matmul(routeb[:, c * E:(c + 1) * E], hTr[:, c * P:(c + 1) * P], centT[:, :], start=True, stop=True)
                    mm.then_inc(aff_done, 1)

                def turn_weights():
                    pe.wait_ge(cw_ready, b + 1)
                    for c in range(TILES):
                        mm = pe.transpose(preb[:, c * P:(c + 1) * P], cw[:, c, :, :].rearrange("p a e -> p (a e)"), k.ident[:, :])
                    mm.then_inc(cwT_done, 1)

                def down(T):
                    q = r * SLOTS + T
                    pe.wait_ge(hid_ready, q + 3)
                    if T == 0:
                        pe.wait_ge(yg_ready, r + 1)
                    rows = P if T < ET else EF
                    w = w_down[:, T, :] if T < ET else ws_down[:, :]
                    pe.matmul(yb[:, :], w, hid[0:rows, T % 4, :], start=(T == 0), stop=(T == ET)).then_inc(down_done, 1)

                def turn_back():
                    pe.wait_ge(yg_ready, r + 1)
                    pe.wait_ge(x_ready, r)
                    for c in range(TILES):
                        mm = pe.transpose(postb[:, c * P:(c + 1) * P], yg[:, c * P:(c + 1) * P], k.ident[:, :])
                    mm.then_inc(turned, 1)

                if main:
                    pe.wait_ge(parts_ready, r + 3)
                    for T in range(SLOTS):
                        q = r * SLOTS + T
                        fresh = 2 if T == 0 else 1
                        pe.wait_ge(silu_ready, q + fresh)
                        pe.sem_inc(passed, 1)
                        if T < ET:
                            pe.matmul(ub[T % 2][:, :], w_up[:, 2 * T:2 * T + 2, :].rearrange("p a f -> p (a f)"), hT[:, r % 2, :],
                                      start=True, stop=True).then_inc(u_done, 1)
                            pe.wait_ge(hid_ready, q + fresh)
                            pe.matmul(cb[T % 2][:, :], sel[:, T, :], parts[:, r % 2, :], start=True, stop=True).then_inc(c_done, 1)
                        else:
                            pe.matmul(ub[T % 2][0:EF, :], ws_up[:, :], hT[:, r % 2, :], start=True, stop=True).then_inc(u_done, 1)
                        if T >= 2:
                            down(T - 2)
                        if post and T == 2:
                            turn_back()
                        if pre:
                            for at, f in ((4, pre_turn), (8, route), (20, turn_weights)):
                                if T == at:
                                    f()
                    down(SLOTS - 2)
                    down(SLOTS - 1)
                elif pre:
                    pre_turn(), route(), turn_weights()
                else:
                    turn_back()

            rounds(pe, step)

        @block.scalar
        def _(act):
            act.wait_ge(cent_psum, 1)
            act.activation(centT[:, :], preb[:, 0:E], ACT.Copy).then_inc(cent_ready, 1)
            act.wait_ge(cent_ready, 1)

            def step(r, pre, main, post):
                b = r + 1

                def pre_h():
                    act.wait_ge(xT_done, b + 1)
                    act.wait_ge(aff_done, b + 1)
                    for to in (hT[:, b % 2, :], hTr[:, :]):
                        act.activation(to, preb[:, :], ACT.Identity, scale=k.mod[:, 1, 4, bass.ds(b, 1)],
                                       bias=k.mod[:, 1, 3, bass.ds(b, 1)]).then_inc(hT_ready, 1)

                def sigmoid():
                    act.wait_ge(cw_ready, b) if main else None
                    act.wait_ge(biased_ready, b + 2)
                    act.activation(sig[:, :, :].rearrange("p c e -> p (c e)"), routeb[:, 0:TILES * E], ACT.Sigmoid).then_inc(sig_ready, 1)

                def high():
                    act.wait_ge(cwT_done, b + 2)
                    act.wait_ge(parts_ready, b + 2)
                    act.activation(parts[:, b % 2, :], preb[:, :], ACT.Copy).then_inc(high_ready, 1)

                if main:
                    for T in range(SLOTS):
                        q = r * SLOTS + T
                        act.wait_ge(u_done, q + 1)
                        act.wait_ge(hid_ready, q + (2 if T == 0 else 1))
                        rows = P if T < ET else EF
                        act.activation(act_u[0:rows, T % 2, :], ub[T % 2][0:rows, :], ACT.Silu).then_inc(silu_ready, 1)
                        if pre:
                            for at, f in ((5, pre_h), (9, sigmoid), (21, high)):
                                if T == at:
                                    f()
                    act.wait_ge(down_done, (r + 1) * SLOTS + 4)
                    act.wait_ge(turned, r + 1)
                    act.activation(yg[:, :], yb[:, :], ACT.Copy, scale=k.mod[:, 1, 5, bass.ds(r, 1)]).then_inc(yg_ready, 1)
                elif pre:
                    pre_h(), sigmoid(), high()

            rounds(act, step)

        @block.vector
        def _(dve):
            link = Chain(dve, dve_setup).link
            token_stats(dve, link, k)
            dve.wait_ge(loaded, LOADS)

            def step(r, pre, main, post):
                b = r + 1

                def pre_norm():
                    for c in range(TILES):
                        ins = normalize(dve, k, xn[:, c, :], b * TILES + c)
                    ins.then_inc(xn_ready, 1)

                def weights():
                    dve.wait_ge(aff_done, b + 2)
                    dve.wait_ge(cwT_done, b + 1)
                    chain = Chain(dve, dve_pre, b * PRE_LINKS)
                    link = chain.link
                    dve.tensor_tensor(biased[:, :, :], routeb[:, 0:TILES * E].rearrange("p (c e) -> p c e", c=TILES),
                                      ebias[:, :].unsqueeze(1).broadcast_to([P, TILES, E]), ALU.add).then_inc(biased_ready, 1)
                    dve.wait_ge(loaded, LOADS)
                    dve.wait_ge(biased_ready, b + 2)
                    for c in range(TILES):
                        ins = dve.max(top[:, c, :], biased[:, c, :])
                    ins.then_inc(top_ready, 1)
                    dve.wait_ge(loaded, LOADS)
                    dve.wait_ge(top_ready, b + 2)
                    for c in range(TILES):
                        ins = dve.match_replace(rest[:, c, :], top[:, c, :], biased[:, c, :], NEG)
                    link(ins)
                    link(dve.tensor_tensor(rest[:, :, :], rest[:, :, :], biased[:, :, :], ALU.not_equal))
                    dve.wait_ge(sig_ready, b + 1)
                    link(dve.tensor_tensor(rest[:, :, :], rest[:, :, :], sig[:, :, :], ALU.mult))
                    link(dve.tensor_reduce(wsum[:, :], rest[:, :, :], AX, ALU.add))
                    link(dve.tensor_scalar(wsum[:, :], wsum[:, :], 1e-8, None, ALU.add))
                    link(dve.reciprocal(wsum[:, :], wsum[:, :]))
                    link(dve.tensor_tensor(rest[:, :, :], rest[:, :, :], wsum[:, :].unsqueeze(2).broadcast_to([P, TILES, E]), ALU.mult))
                    dve.tensor_copy(cw[:, :, :, :], rest[:, :, :].unsqueeze(2).broadcast_to([P, TILES, 2, E])).then_inc(cw_ready, 1)
                    assert chain.n == PRE_LINKS

                def split():
                    dve.wait_ge(high_ready, b + 1)
                    lo = parts[E:2 * E, b % 2, :]
                    dve.tensor_tensor(low[E:2 * E, :], preb[E:2 * E, :], lo, ALU.subtract).then_inc(low_read, 1)
                    dve.wait_ge(low_read, b + 2)
                    dve.tensor_scalar(lo, low[E:2 * E, :], LOW, None, ALU.mult).then_inc(parts_ready, 1)

                def residual():
                    dve.wait_ge(turned, r + 1)
                    x = k.x[:, bass.ds((r - 1) * TILES, TILES), :]
                    dve.tensor_tensor(x, x, postb[:, :].rearrange("p (c n) -> p c n", c=TILES), ALU.add).then_inc(x_ready, 1)

                if main:
                    for T in range(SLOTS):
                        q = r * SLOTS + T
                        dve.wait_ge(silu_ready, q + 3)
                        dve.wait_ge(down_done, q + (4 if T == 0 else 3 if T < 4 else 1))
                        if T < ET:
                            dve.wait_ge(c_done, r * ET + T + 1)
                            dve.tensor_tensor(hid[:, T % 4, :], act_u[:, T % 2, :], cb[T % 2][:, :], ALU.mult).then_inc(hid_ready, 1)
                        else:
                            dve.tensor_copy(hid[0:EF, T % 4, :], act_u[0:EF, T % 2, :]).then_inc(hid_ready, 1)
                        if post and T == 3:
                            residual()
                        if pre:
                            for at, f in ((2, pre_norm), (9, weights), (21, split)):
                                if T == at:
                                    f()
                elif pre:
                    pre_norm(), weights(), split()
                else:
                    residual()

            rounds(dve, step)


def kernel(**inputs):
    import concourse.bacc as bacc
    from concourse.bass_utils import run_bass_kernel_spmd

    nc = bacc.Bacc("TRN2", target_bir_lowering=False, num_devices=1)
    arrays = {name: np.ascontiguousarray(a) for name, a in inputs.items()}
    d = {name: nc.dram_tensor(name, a.shape, mybir.dt.from_np(a.dtype), kind="ExternalInput").ap() for name, a in arrays.items()}
    out = nc.dram_tensor("out_0_dram", (B, S, D), F32, kind="ExternalOutput").ap()
    build(nc, d, out)
    r = run_bass_kernel_spmd(nc, [arrays], core_ids=[0])
    return r.results[0]["out_0_dram"]
```

```python
import math
from contextlib import ExitStack

import numpy as np
import concourse.bass as bass
from concourse import mybir

F32 = mybir.dt.float32
BF16 = mybir.dt.bfloat16
FP16 = mybir.dt.float16
I32 = mybir.dt.int32
ALU = mybir.AluOpType
ACT = mybir.ActivationFunctionType
AX = mybir.AxisListType.X

B, S, D = 8, 512, 128
P = 128
TILES = S // P
H, HD = 16, 8
VD = 2 * HD
LAM_INIT = 0.8 - 0.6 * math.exp(-0.3 * 11)
EPS = 1e-5
FF = 512
N = 16
BC = 2 * N
RANK = 8
E, EF, TOPK = 64, 64, 8
ET = E * EF // P

NEG = -3.0e38
INV_2PI = 1.0 / (2.0 * math.pi)
ROUND = 1.5 * 2.0 ** 23
TWO_PI_HI = 6.28125
TWO_PI_LO = 2 * math.pi - TWO_PI_HI
PI_BELOW = 3.1415925


class Chain:

    def __init__(self, eng, sem, base=0, passed=None):
        self.eng, self.sem, self.base, self.n, self.passed = eng, sem, base, 0, passed

    def link(self, ins):
        ins.then_inc(self.sem, 1)
        self.n += 1
        self.eng.wait_ge(self.sem, self.base + self.n)
        if self.passed is not None:
            self.eng.sem_inc(self.passed, 1)


def rsqrt_start(dve, link, v, half, y, t):
    link(dve.tensor_scalar(t.bitcast(I32), v.bitcast(I32), 1, None, ALU.logical_shift_right))
    link(dve.tensor_scalar(y.bitcast(I32), t.bitcast(I32), -1.0, 1597463007.0, ALU.mult, ALU.add))
    link(dve.tensor_scalar(half, v, -0.5, None, ALU.mult))


def rsqrt_newton(dve, link, half, y, t):
    link(dve.tensor_tensor(t, y, y, ALU.mult))
    link(dve.tensor_tensor(t, t, half, ALU.mult))
    link(dve.scalar_tensor_tensor(y, t, 1.5, y, ALU.add, ALU.mult))


def rsqrt_steps(dve, link, v, half, y, t):
    rsqrt_start(dve, link, v, half, y, t)
    for _ in range(3):
        rsqrt_newton(dve, link, half, y, t)


RSQRT_LINKS = 3 + 3 * 3


def build(nc, d, out):
    with ExitStack() as top:
        keep = shared_tiles(nc, top)
        setup(nc, d, keep)
        attention(nc, d, keep)
        ffn(nc, d, keep)
        expert_tiles(nc, top, keep)
        scan(nc, d, keep)
        experts(nc, d, keep, out)


class Keep:
    pass


def shared_tiles(nc, ctx):
    k = Keep()

    def sb(name, shape, dt=F32):
        return ctx.enter_context(nc.sbuf_tensor(name, shape, dt))

    k.x = sb("x_tok", [P, B * TILES, D])
    k.ident = sb("ident", [P, P])
    k.identb = sb("identb", [P, P], BF16)
    k.ones = sb("ones", [P, P])
    k.mod = sb("mod", [P, 2, 6, B])
    k.gate_a0 = sb("gate_a0", [P, B, D])
    k.gate_b0 = sb("gate_b0", [P, B, D])
    k.neg_lam = sb("neg_lam", [P, H])
    k.stats = sb("stats", [P, B * TILES, 2])
    k.rstd = sb("rstd", [P, B * TILES])
    k.half = sb("half", [P, B * TILES])
    k.tmp = sb("rs_tmp", [P, B * TILES])
    k.bn = sb("bn", [P, B * TILES, 6])
    k.wraw = sb("wraw", [P, 4, D])
    k.wv = sb("wv", [P, H * VD])
    k.wo = sb("wo", [P, 2, D])
    k.w1 = sb("w1", [P, FF])
    k.w2 = sb("w2", [P, FF // P, D])
    k.b2 = sb("b2", [P, D])
    k.col = sb("col", [P, 4, FF // P])
    k.conv_w = sb("conv_w", [P, 3])
    k.wbc = sb("wbc", [P, 3, BC])
    k.bbc = sb("bbc", [3 * BC, 1])
    k.wdt = sb("wdt", [P, RANK])
    k.bdt = sb("bdt", [RANK, 1])
    k.wdtp = sb("wdtp", [RANK, D])
    k.bdtp = sb("bdtp", [P, 1])
    k.nA = sb("nA", [P, N])
    k.dco = sb("dco", [P, 1])
    k.cent = sb("cent", [E, D])
    k.ebias = sb("ebias", [P, E])
    k.x_loaded, k.attn_loaded, k.ffn_loaded, k.scan_loaded, k.moe_loaded = (
        ctx.enter_context(nc.semaphore(n)) for n in ("x_loaded", "attn_loaded", "ffn_loaded", "scan_loaded", "moe_loaded"))
    return k


def load_weights(nc, sp, d, k):
    a = "L0_attn_"
    for j, name in enumerate(("Wq1", "Wq2", "Wk1", "Wk2")):
        sp.dma_start(k.wraw[:, j, :], d[a + name]).then_inc(k.attn_loaded, 16)
    sp.dma_start(k.wv[:, :], d[a + "Wv"]).then_inc(k.attn_loaded, 16)
    sp.dma_start(k.wo[:, :, :], d[a + "Wo"].rearrange("(c p) n -> p c n", p=P)).then_inc(k.attn_loaded, 16)
    a = "L0_ffn_"
    sp.dma_start(k.w1[:, :], d[a + "W1"]).then_inc(k.ffn_loaded, 16)
    with nc.allow_non_contiguous_dma("one value of each hidden unit"):
        for n, name in enumerate(("b1", "quantum_phases", "quantum_weights_real", "quantum_weights_imag")):
            sp.dma_start(k.col[:, n, :], d[a + name].rearrange("(j p) -> p j", p=P)).then_inc(k.ffn_loaded, 16)
    sp.dma_start(k.w2[:, :, :], d[a + "W2"].rearrange("(j p) n -> p j n", p=P)).then_inc(k.ffn_loaded, 16)
    sp.dma_start(k.b2[:, :], d[a + "b2"].partition_broadcast(P)).then_inc(k.ffn_loaded, 16)
    a = "L1_attn_"
    for j in range(3):
        sp.dma_start(k.wbc[:, j, :], d[a + "W_bc"]).then_inc(k.scan_loaded, 16)
        sp.dma_start(k.bbc[j * BC:(j + 1) * BC, :], d[a + "b_bc"].unsqueeze(1)).then_inc(k.scan_loaded, 16)
    with nc.allow_non_contiguous_dma("three values of each feature"):
        sp.dma_start(k.conv_w[:, :], d[a + "conv_w"].rearrange("c p -> p c")).then_inc(k.scan_loaded, 16)
    sp.dma_start(k.wdt[:, :], d[a + "W_dt"]).then_inc(k.scan_loaded, 16)
    sp.dma_start(k.bdt[:, :], d[a + "b_dt"].unsqueeze(1)).then_inc(k.scan_loaded, 16)
    sp.dma_start(k.wdtp[:, :], d[a + "W_dtp"]).then_inc(k.scan_loaded, 16)
    sp.dma_start(k.bdtp[:, :], d[a + "b_dtp"].unsqueeze(1)).then_inc(k.scan_loaded, 16)
    sp.dma_start(k.dco[:, :], d[a + "Dcoeff"].unsqueeze(1)).then_inc(k.scan_loaded, 16)
    sp.dma_start(k.nA[:, :], d[a + "A_log"]).then_inc(k.scan_loaded, 16)
    a = "L1_ffn_"
    sp.dma_start(k.cent[:, :], d[a + "centroids"]).then_inc(k.moe_loaded, 16)
    sp.dma_start(k.ebias[:, :], d[a + "expert_biases"].partition_broadcast(P)).then_inc(k.moe_loaded, 16)


W_SCALE = 2.0 ** 6
W_CHUNKS = B
W_COLS = E * EF + P


def expert_tiles(nc, ctx, k):
    k.w = ctx.enter_context(nc.sbuf_tensor("w_experts", [P, 2, W_COLS], F32))
    k.w_high = ctx.enter_context(nc.sbuf_tensor("w_high", [P, 2, W_COLS], FP16))
    k.w_low = ctx.enter_context(nc.sbuf_tensor("w_low", [P, 2, W_COLS], FP16))
    k.w_filled, k.w_loaded, k.w_scaled, k.w_rounded, k.w_ready = (
        ctx.enter_context(nc.semaphore(n)) for n in ("w_filled", "we_loaded", "w_scaled", "w_rounded", "we_ready"))


def chunk(t, c):
    n = W_COLS // W_CHUNKS
    return t[:, :, bass.ds(c * n, n)]


def setup(nc, d, k):
    with ExitStack() as ctx:
        def sb(name, shape, dt=F32):
            return ctx.enter_context(nc.sbuf_tensor(name, shape, dt))

        used = []

        def sem(name):
            used.append(ctx.enter_context(nc.semaphore(name)))
            return used[-1]

        def clear():
            for s in used:
                nc.gpsimd.sem_clear(s)

        ctx.callback(clear)

        c = sb("c", [B, 2, D])
        sc = sb("silu_c", [B, 2, D])
        cT = sb("silu_cT", [P, 2, B])
        cTb = sb("silu_cTb", [P, B, P])
        wmod = sb("wmod", [P, 2, 6 * D])
        lq = sb("lq", [1, 4, H * HD])
        lp = sb("lp", [1, 2, H * HD])
        ls = sb("ls", [1, 2, H])
        le = sb("le", [1, 2, H])
        lr = sb("lr", [1, H])
        gs = sb("gs", [P, 2, 2, 2, B])
        psum_c = ctx.enter_context(nc.psum_tensor("psum_c", [P, 512], F32))
        psum_m = ctx.enter_context(nc.psum_tensor("psum_m", [P, 512], F32))
        psum_l = ctx.enter_context(nc.psum_tensor("psum_l", [P, 512], F32))
        psum_g = ctx.enter_context(nc.psum_tensor("psum_g", [P, 4, 512], F32))
        c_loaded, lq_loaded, w_loaded, x_first = sem("c_loaded"), sem("lq_loaded"), sem("wmod_loaded"), sem("x_first")
        consts = sem("setup_consts")
        silu_done, cT_psum, cT_ready, mod_psum, gate_psum = (
            sem("silu_done"), sem("cT_psum"), sem("cT_ready"), sem("mod_psum"), sem("gate_psum"))
        lp_ready, le_ready, lr_ready, lam_psum = sem("lp_ready"), sem("le_ready"), sem("lr_ready"), sem("lam_psum")
        dve_chain = sem("setup_dve")
        block = ctx.enter_context(nc.Block())

        @block.sync
        def _(sp):
            for l, name in enumerate(("L0_c", "L1_c")):
                sp.dma_start(c[:, l, :], d[name]).then_inc(c_loaded, 16)
            for l, name in enumerate(("L0_wmod", "L1_wmod")):
                sp.dma_start(wmod[:, l, :], d[name]).then_inc(w_loaded, 16)
            for j, name in enumerate(("lq1", "lk1", "lq2", "lk2")):
                sp.dma_start(lq[0:1, j, :], d["L0_attn_" + name].rearrange("(a h) d -> a (h d)", a=1)).then_inc(lq_loaded, 16)
            load_weights(nc, sp, d, k)

        @block.gpsimd
        def _(pool):
            pool.memset(k.ident[:, :], 0.0).then_inc(consts, 1)
            pool.memset(k.identb[:, :], 0.0).then_inc(consts, 1)
            pool.memset(k.ones[:, :], 1.0).then_inc(consts, 1)
            pool.wait_ge(consts, 3)
            for m in (k.ident, k.identb):
                pool.affine_select(out=m[:, :], in_=m[:, :], compare_op=ALU.not_equal, fill=1.0, base=0,
                                   pattern=[[-1, P]], channel_multiplier=1).then_inc(consts, 1)

        @block.scalar
        def _(act):
            x_in = d["L0_attn_x"].rearrange("b (i p) d -> p (b i) d", p=P)
            act.dma_start(k.x[:, 0:TILES, :], x_in[:, 0:TILES, :]).then_inc(x_first, 16)
            act.dma_start(k.x[:, TILES:, :], x_in[:, TILES:, :]).then_inc(k.x_loaded, 16)
            act.wait_ge(c_loaded, 16 * 2)
            act.activation(sc[:, :, :], c[:, :, :], ACT.Silu).then_inc(silu_done, 1)
            act.wait_ge(lp_ready, 1)
            act.activation(le[0:1, :, :], ls[0:1, :, :], ACT.Exp).then_inc(le_ready, 1)
            act.wait_ge(gate_psum, 1)
            for n, gate in enumerate((k.gate_a0, k.gate_b0)):
                act.activation(gate[:, :, :].rearrange("p b d -> p (b d)"), psum_g[:, 2 * n:2 * n + 2, :].rearrange("p b d -> p (b d)"), ACT.Copy)

        @block.tensor
        def _(pe):
            pe.wait_ge(consts, 5)
            pe.wait_ge(silu_done, 1)
            for l in range(2):
                mm = pe.transpose(psum_c[:, 8 * l:8 * l + B], sc[:, l, :], k.ident[0:B, 0:B])
            mm.then_inc(cT_psum, 1)
            pe.wait_ge(cT_ready, 2)
            pe.wait_ge(w_loaded, 16 * 2)
            for l in range(2):
                for j in range(6):
                    at = (6 * l + j) * B
                    mm = pe.matmul(psum_m[:, at:at + B], wmod[:, l, j * D:(j + 1) * D], cT[:, l, :], start=True, stop=True)
            mm.then_inc(mod_psum, 1)
            for n, j in enumerate((2, 5)):
                for b in range(B):
                    mm = pe.matmul(psum_g[:, 2 * n + b // 4, (b % 4) * D:(b % 4 + 1) * D], cTb[:, b, :],
                                   wmod[:, 0, j * D:(j + 1) * D], start=True, stop=True)
            mm.then_inc(gate_psum, 1)
            pe.wait_ge(lr_ready, 1)
            pe.matmul(psum_l[:, 0:H], k.ones[0:1, :], lr[0:1, :], start=True, stop=True).then_inc(lam_psum, 1)

        @block.vector
        def _(dve):
            link = Chain(dve, dve_chain).link
            dve.wait_ge(cT_psum, 1)
            dve.tensor_copy(cT[:, :, :], psum_c[:, 0:2 * B].rearrange("p (l b) -> p l b", l=2)).then_inc(cT_ready, 1)
            dve.tensor_copy(cTb[:, :, :], psum_c[:, 0:B].unsqueeze(2).broadcast_to([P, B, P])).then_inc(cT_ready, 1)
            dve.wait_ge(lq_loaded, 16 * 4)
            for j in range(2):
                link(dve.tensor_tensor(lp[0:1, j, :], lq[0:1, 2 * j, :], lq[0:1, 2 * j + 1, :], ALU.mult))
            dve.tensor_reduce(ls[0:1, :, :], lp[0:1, :, :].rearrange("a j (h d) -> a j h d", d=HD), AX, ALU.add).then_inc(lp_ready, 1)
            dve.wait_ge(x_first, 16)
            token_stats(dve, link, k, range(1))
            dve.wait_ge(le_ready, 1)
            dve.scalar_tensor_tensor(lr[0:1, :], le[0:1, 1, :], -LAM_INIT, le[0:1, 0, :], ALU.add, ALU.subtract).then_inc(lr_ready, 1)
            dve.wait_ge(mod_psum, 1)
            link(dve.tensor_copy(k.mod[:, :, :, :], psum_m[:, 0:12 * B].rearrange("p (l j b) -> p l j b", l=2, j=6)))
            for j in (1, 4):
                link(dve.tensor_scalar(k.mod[:, :, j, :], k.mod[:, :, j, :], 1.0, None, ALU.add))
            for n, j in enumerate((2, 5)):
                g = k.mod[:, :, j, :]
                link(dve.scalar_tensor_tensor(gs[:, 0, n, :, :], g, -1.0, g, ALU.mult, ALU.max))
                link(dve.tensor_scalar(gs[:, 0, n, :, :], gs[:, 0, n, :, :], 0.25, None, ALU.max))
                link(dve.tensor_scalar(gs[:, 1, n, :, :], g, 0.0, 2.0, ALU.is_ge, ALU.mult))
                link(dve.scalar_tensor_tensor(g, gs[:, 1, n, :, :], -1.0, gs[:, 0, n, :, :], ALU.add, ALU.mult))
            dve.wait_ge(lam_psum, 1)
            link(dve.tensor_copy(k.neg_lam[:, :], psum_l[:, 0:H]))


GROUPS = 8
MAPS = 4
RING = 4
Q_ORDER, K_ORDER = (0, 0, 0, 1, 1, 2), (0, 1, 2, 0, 1, 0)
SROWS = len(Q_ORDER) * HD
NROWS = 3
KROWS = 96
UNITS = 10
FIRST_BANKS = 3
FIRST_CREDITS = FIRST_BANKS + (GROUPS * UNITS) % FIRST_BANKS
SCALE = 1.0 / math.sqrt(HD)
PRODUCT_AT = (6, 9, 10, 11)
LEAD = 2
GATES_AT, STATS_AT = 2, 7
LAG = 2


def first_since(g, u):
    at, length = g * UNITS + u, GROUPS * UNITS
    before = [n for n in range(at - 2 * FIRST_BANKS, at) if n % length % FIRST_BANKS == at % FIRST_BANKS]
    return at - before[-1]


def lagged(r, g, n):
    return (r, g - n) if g >= n else (r - 1, g - n + GROUPS)


def attention(nc, d, k):
    q_dram = nc.dram_tensor("q_stacks", [B, GROUPS, SROWS + NROWS, MAPS, S], BF16).ap()
    k_dram = nc.dram_tensor("k_stacks", [B, GROUPS, SROWS, MAPS, S], BF16).ap()
    with ExitStack() as ctx:
        def sb(name, shape, dt=F32):
            return ctx.enter_context(nc.sbuf_tensor(name, shape, dt))

        def ps(name):
            return ctx.enter_context(nc.psum_tensor(name, [P, 512], F32))

        def sem(name):
            return ctx.enter_context(nc.semaphore(name))

        wqk = sb("wqk", [P, 4, D])
        causal = sb("causal", [P, P], BF16)
        zeros = sb("zeros", [B * GROUPS, NROWS, S], BF16)
        xn = sb("xn", [P, TILES, D])
        hT = sb("hT", [P, S])
        parts = sb("parts", [P, 2, 3, S], BF16)
        res = sb("res", [P, S])
        vst = sb("vst", [P, 2, TILES, H, 2 * VD])
        qs, ks = sb("qs", [KROWS, RING, MAPS, S], BF16), sb("ks", [KROWS, RING, MAPS, S], BF16)
        vs = sb("vs", [P, 2, TILES, 2, 2 * VD])
        pT = sb("pT", [P, 2, UNITS, 512])
        bmax = sb("bmax", [P, 2, MAPS, 10])
        qmax = sb("qmax", [P, TILES, MAPS])
        nparts = sb("nparts", [MAPS, 2, NROWS, S], BF16)
        nres = sb("nres", [MAPS, S])
        o_sb = sb("o_sb", [P, 2, S])
        oT = sb("oT", [P, 2, TILES, 2 * H, VD + 1])
        rc = sb("rc", [P, TILES, H, 2])
        og, o2, oc, sq = (sb(n, [P, TILES * H, VD]) for n in ("og", "o2", "oc", "sq"))
        msum, vsum, vhalf, orstd, otmp = (sb(n, [P, TILES * H]) for n in ("msum", "vsum", "vhalf", "orstd", "otmp"))
        merged = sb("merged", [P, TILES, H * VD])
        mT = sb("mT", [P, 2, S])
        gated = sb("gated", [P, TILES, D])
        p1b = [ps(f"p1b{i}") for i in range(FIRST_BANKS)]
        p2b = [ps(f"p2b{i}") for i in range(2)]
        ob, turnb = ps("ob"), ps("turnb")
        sideb = ps("sideb")

        slots_set, zeros_saved, w_ready, dve_fill = sem("slots_set"), sem("zeros_saved"), sem("w_ready"), sem("dve_fill")
        xn_ready, xnT_done, hT_ready, qk_done, hi_ready, res_ready, mid_ready, split_ready, v_done, v_ready = (
            sem(n) for n in ("xn_ready", "xnT_done", "hT_ready", "qk_done", "hi_ready", "res_ready", "mid_ready",
                             "split_ready", "v_done", "v_ready"))
        qk_saved = [sem(f"qk_saved{s}") for s in range(2)]
        stack_loaded = [sem(f"stack_loaded{s}") for s in range(RING)]
        neg_loaded = [sem(f"neg_loaded{s}") for s in range(RING)]
        first_unit, first_read, second_unit, exp_done, masked, vs_ready, av_done, o_read, oT_done, oT_read = (
            sem(n) for n in ("first_unit", "first_read", "second_unit", "exp_done", "masked", "vs_ready", "av_done", "o_read",
                             "oT_done", "oT_read"))
        qmax_ready, neg_psum, neg_high, neg_read, neg_mid, neg_ready = (
            sem(n) for n in ("qmax_ready", "neg_psum", "neg_high", "neg_read", "neg_mid", "neg_ready"))
        rc_ready, og_ready, merged_ready, mT_done, mT_ready, wo_done, gated_ready, post_done = (
            sem(n) for n in ("rc_ready", "og_ready", "merged_ready", "mT_done", "mT_ready", "wo_done", "gated_ready", "post_done"))
        pool_own, dve_post, passed = sem("pool_own"), sem("dve_post"), sem("passed")
        block = ctx.enter_context(nc.Block())

        CREDITS = {first_read: FIRST_CREDITS, second_unit: RING * UNITS, exp_done: 2, vs_ready: GROUPS + 1, av_done: 2, o_read: 1, oT_done: 2,
                   oT_read: 4, neg_psum: 1, neg_ready: 1, xnT_done: 1, res_ready: 1, split_ready: 1, v_done: 1, v_ready: 1,
                   qk_saved[0]: 16, qk_saved[1]: 16, og_ready: 2, merged_ready: 1, mT_done: 1, wo_done: 1, gated_ready: 3}
        W_LOADS = 6 * 16
        SAVES = len(Q_ORDER) * 16
        NEG_LOADS = NROWS * 16
        LOADS = 2 * 16

        def use(r, g):
            return r * (GROUPS // RING) + g // RING

        def rounds(eng, slot):
            def round_(r, first, last):
                for g in range(GROUPS):
                    def on(n):
                        return not (first and g < n) and not (last and g >= n)
                    slot(r, g, on, prep=not last and not (isinstance(r, int) and r == B - 1), post=not first)

            for g in range(GROUPS):
                slot(-1, g, lambda n: False, prep=True, post=False)
            round_(0, True, False)
            with eng.Fori(1, B - 1) as r:
                round_(r, False, False)
            round_(B - 1, False, False)
            round_(B, False, True)

        @block.sync
        def _(sp):
            sp.wait_ge(slots_set, 2)
            for m in range(MAPS):
                sp.dma_start(q_dram[:, :, SROWS:SROWS + NROWS, m, :].rearrange("b g s t -> (b g) s t"), zeros[:, :, :]).then_inc(zeros_saved, 16)
            sp.wait_ge(zeros_saved, MAPS * 16)

            def load(r, g):
                slot = g % RING
                if g < 2:
                    sp.wait_ge(slots_set, 6)
                    for s in range(2):
                        sp.wait_ge(qk_saved[s], (r + 1) * 2 * SAVES + 16)
                sp.wait_ge(second_unit, (r * GROUPS + g + 1) * UNITS)
                for tile, rows, dram in ((qs, SROWS + NROWS, q_dram), (ks, SROWS, k_dram)):
                    sp.dma_start(tile[0:rows, slot, :, :].rearrange("p m t -> p (m t)"),
                                 dram[r, g, :, :, :].rearrange("p m t -> p (m t)")).then_inc(stack_loaded[slot], 16)

            def slot(r, g, on, prep, post):
                if on(1):
                    rn, gn = lagged(r, g, 1)
                    sp.wait_ge(neg_ready, rn * GROUPS + gn + 2)
                    for s in range(NROWS):
                        sp.dma_start(qs[SROWS + s:SROWS + s + 1, gn % RING, :, :].rearrange("p m t -> p (m t)"),
                                     nparts[:, gn % 2, s, :]).then_inc(neg_loaded[gn % RING], 16)
                if prep and 2 <= g < 6:
                    b, j = r + 1, g - 2
                    sp.wait_ge(split_ready, b * 4 + j + 2)
                    dram, order = (q_dram, Q_ORDER) if j < 2 else (k_dram, K_ORDER)
                    for n, part in enumerate(order):
                        to = dram[b, :, n * HD:(n + 1) * HD, :, :].rearrange("g r (h j) t -> j g (r h) t", j=2)[j % 2]
                        sp.dma_start(to, parts[:, j % 2, part, :]).then_inc(qk_saved[j % 2], 16)
                rl, gl = (r, g + 2) if g + 2 < GROUPS else (r + 1, g + 2 - GROUPS)
                if g + 2 >= GROUPS and prep or g + 2 < GROUPS and on(0):
                    load(rl, gl)

            rounds(sp, slot)
            sp.wait_ge(post_done, B)

        @block.gpsimd
        def _(pool):
            for s, n in CREDITS.items():
                pool.sem_inc(s, n)
            pool.memset(vst[:, :, :, :, :], 1.0).then_inc(slots_set, 1)
            pool.memset(zeros[:, :, :], 0.0).then_inc(slots_set, 1)
            pool.memset(causal[:, :], 0.0).then_inc(slots_set, 1)
            pool.wait_ge(slots_set, 3)
            pool.affine_select(out=causal[:, :], in_=causal[:, :], compare_op=ALU.is_ge, fill=NEG, base=0,
                               pattern=[[-1, P]], channel_multiplier=1).then_inc(slots_set, 1)
            pool.memset(qs[:, :, :, :], 0.0).then_inc(slots_set, 1)
            pool.memset(ks[:, :, :, :], 1.0).then_inc(slots_set, 1)

            def slot(r, g, on, prep, post):
                pb = r - 1
                o = oT[:, (r + 1) % 2, :, :, 0:VD].rearrange("p c (h j) e -> p (c h) j e", j=2)
                rcv = rc[:, :, :, :].rearrange("p c h j -> p (c h) j")
                full = [P, TILES * H, VD]
                if post and g == 4:
                    pool.wait_ge(rc_ready, pb + 1)
                    pool.wait_ge(merged_ready, pb + 1)
                    pool.tensor_tensor(og[:, :, :], o[:, :, 0, :], rcv[:, :, 0].unsqueeze(2).broadcast_to(full), ALU.mult).then_inc(pool_own, 1)
                if post and g == 5:
                    pool.wait_ge(pool_own, pb * 2 + 2)
                    pool.tensor_tensor(og[:, :, :], og[:, :, :], o2[:, :, :], ALU.add).then_inc(og_ready, 1)
                if on(1):
                    rn, gn = lagged(r, g, 1)
                    G = rn * GROUPS + gn
                    pool.wait_ge(neg_mid, G + 1)
                    pool.tensor_tensor(nparts[:, gn % 2, 2, :], nres[:, :], nparts[:, gn % 2, 1, :], ALU.subtract).then_inc(neg_ready, 1)
                if post and g == 4:
                    pool.tensor_tensor(o2[:, :, :], o[:, :, 1, :], rcv[:, :, 1].unsqueeze(2).broadcast_to(full), ALU.mult).then_inc(pool_own, 1)
                if on(2):
                    r2, g2 = lagged(r, g, 2)
                    G = r2 * GROUPS + g2
                    a = g2 % 2
                    pool.wait_ge(v_ready, (r2 + 1) * TILES + 1)
                    pool.wait_ge(av_done, G + 1)
                    pool.sem_inc(passed, 1)
                    pool.tensor_copy(vs[:, a, :, :, :], vst[:, r2 % 2, :, 2 * g2:2 * g2 + 2, :]).then_inc(vs_ready, 1)
                    pool.wait_ge(exp_done, (G + 1) * UNITS + 2)
                    pool.sem_inc(passed, 1)
                    for block_ap, n in ((pT[:, a, :, 0:P], UNITS), (pT[:, a, 1:8:2, 384:512], 4), (pT[:, a, 8:10, 256:384], 2)):
                        pool.affine_select(out=block_ap, in_=block_ap, compare_op=ALU.is_ge, fill=0.0, base=0,
                                           pattern=[[0, n], [1, P]], channel_multiplier=-1).then_inc(masked, 1)
                if prep and 1 <= g < 5:
                    j, J = g - 1, (r + 1) * 4 + g - 1
                    pool.wait_ge(mid_ready, J + 1)
                    pool.tensor_tensor(parts[:, j % 2, 2, :], res[:, :], parts[:, j % 2, 1, :], ALU.subtract).then_inc(split_ready, 1)

            rounds(pool, slot)

        @block.scalar
        def _(act):
            act.wait_ge(slots_set, 1)

            def slot(r, g, on, prep, post):
                b = r + 1
                if on(2):
                    r2, g2 = lagged(r, g, 2)
                    G2 = r2 * GROUPS + g2
                    act.wait_ge(av_done, G2 + 1)
                for u in range(UNITS + LAG):
                    if on(2) and u >= LAG:
                        v = u - LAG
                        act.wait_ge(second_unit, G2 * UNITS + v + 1 + RING * UNITS)
                        act.activation(pT[:, g2 % 2, v, :], p2b[v % 2][:, :], ACT.Exp, scale=SCALE).then_inc(exp_done, 1)
                    if u == 2 and on(1):
                        rn, gn = lagged(r, g, 1)
                        act.wait_ge(neg_psum, rn * GROUPS + gn + 2)
                        if not isinstance(rn, int) or rn * GROUPS + gn >= 2:
                            rp, gp = lagged(rn, gn, 2)
                            act.wait_ge(neg_loaded[gp % RING], (use(rp, gp) + 1) * NEG_LOADS)
                        act.activation(nparts[:, gn % 2, 0, :], turnb[0:MAPS, :], ACT.Copy, scale=-1.0).then_inc(neg_high, 1)
                    if u == 5 and on(1):
                        act.wait_ge(neg_read, rn * GROUPS + gn + 1)
                        act.activation(nparts[:, gn % 2, 1, :], nres[:, :], ACT.Copy).then_inc(neg_mid, 1)
                    if prep and u == 5 and 1 <= g < 5:
                        j, J = g - 1, b * 4 + g - 1
                        act.wait_ge(qk_done, J + 1)
                        act.wait_ge(qk_saved[j % 2], (b * 2 + j // 2) * SAVES + 16)
                        act.activation(parts[:, j % 2, 0, :], sideb[:, :], ACT.Copy).then_inc(hi_ready, 1)
                    if prep and u == 9 and 1 <= g < 5:
                        act.wait_ge(res_ready, J + 2)
                        act.activation(parts[:, j % 2, 1, :], res[:, :], ACT.Copy).then_inc(mid_ready, 1)
                    if post and g == 7 and u in (5, 8):
                        c, pb = u // 8, r - 1
                        act.wait_ge(mT_done, pb * 2 + c + 2)
                        act.wait_ge(wo_done, pb + 1)
                        act.activation(mT[:, c, :], sideb[:, :], ACT.Copy).then_inc(mT_ready, 1)
                if prep and 2 <= g < 6:
                    c, V = g - 2, b * TILES + g - 2
                    act.wait_ge(v_done, V + 2)
                    if c == 0:
                        act.wait_ge(vs_ready, b * GROUPS + 1)
                    act.activation(vst[:, b % 2, c, :, 0:VD], sideb[:, 0:H * VD].rearrange("p (h e) -> p h e", h=H), ACT.Copy).then_inc(v_ready, 1)
                if on(3):
                    r3, g3 = lagged(r, g, 3)
                    G3 = r3 * GROUPS + g3
                    act.wait_ge(av_done, G3 + 3)
                    act.wait_ge(oT_done, G3 + 1)
                    act.activation(o_sb[:, g3 % 2, :], ob[:, :], ACT.Copy).then_inc(o_read, 1)
                if on(4):
                    r4, g4 = lagged(r, g, 4)
                    G4 = r4 * GROUPS + g4
                    act.wait_ge(oT_done, G4 + 3)
                    if g4 == 0:
                        act.wait_ge(og_ready, r4 + 1)
                    act.activation(oT[:, r4 % 2, :, g4 * MAPS:(g4 + 1) * MAPS, :],
                                   turnb[:, :].rearrange("p (c m e) -> p c m e", c=TILES, m=MAPS)[:, :, :, 0:VD + 1],
                                   ACT.Copy).then_inc(oT_read, 1)
                if prep and g == 0:
                    act.wait_ge(xnT_done, b + 2)
                    act.wait_ge(v_done, b * TILES + 1)
                    act.activation(hT[:, :], sideb[:, :], ACT.Identity, scale=k.mod[:, 0, 1, bass.ds(b, 1)],
                                   bias=k.mod[:, 0, 0, bass.ds(b, 1)]).then_inc(hT_ready, 1)

            rounds(act, slot)

        @block.tensor
        def _(pe):
            pe.wait_ge(k.attn_loaded, W_LOADS)
            pe.wait_ge(w_ready, 1)

            def first_unit_of(r, g, u):
                G, slot = r * GROUPS + g, g % RING
                bank = p1b[(g * UNITS + u) % FIRST_BANKS]
                pe.wait_ge(first_read, G * UNITS + u + 1 - first_since(g, u) + FIRST_CREDITS)
                blocks = {0: [(u, 3, 0)], 1: [(u - 4, 2, 0), (u - 4, 0, 3)],
                          2: [(2 * u - 16, 1, 0), (2 * u - 15, 1, 2)]}[u // 4]
                for m, c, at in blocks:
                    pe.matmul(bank[:, at * P:(at + c + 1) * P], qs[:, slot, m, c * P:(c + 1) * P], ks[:, slot, m, 0:(c + 1) * P],
                              start=True, stop=False, skip_group_check=True)
                    mm = pe.matmul(bank[:, (at + c) * P:(at + c + 1) * P], k.identb[:, :], causal[:, :],
                                   start=False, stop=True, skip_group_check=True)
                mm.then_inc(first_unit, 1)

            def second_unit_of(G, slot, u):
                bank = p2b[u % 2]
                pe.wait_ge(exp_done, G * UNITS + u + 1)
                if u < 8:
                    m = u // 2
                    blocks = [(m, 0, 0)] if u % 2 == 0 else [(m, 1, 0), (m, 3, 384)]
                else:
                    blocks = [(2 * u - 16, 2, 0), (2 * u - 15, 2, 256)]
                for m, c, at in blocks:
                    n = S - c * P
                    mm = pe.matmul(bank[:, at:at + n], ks[:, slot, m, c * P:(c + 1) * P], qs[:, slot, m, c * P:S],
                                   start=True, stop=True, skip_group_check=True)
                mm.then_inc(second_unit, 1)

            def product(G, a, c):
                if c == 0:
                    pe.wait_ge(masked, 3 * G + 3)
                    pe.wait_ge(vs_ready, G + GROUPS + 2)
                    pe.wait_ge(o_read, G + 1)
                for m in range(MAPS):
                    u, at = {0: (2 * m, 0), 1: (2 * m + 1, 0), 2: (8 + m // 2, 256 * (m % 2)), 3: (2 * m + 1, 384)}[c]
                    n = S - c * P
                    mm = pe.matmul(ob[32 * m:32 * m + 32, c * P:S], vs[:, a, c, m // 2, :], pT[:, a, u, at:at + n],
                                   start=(c == 0), stop=(c == TILES - 1), skip_group_check=True)
                if c == TILES - 1:
                    mm.then_inc(av_done, 1)

            def slot(r, g, on, prep, post):
                b, pb = r + 1, r - 1
                if on(2):
                    r2, g2 = lagged(r, g, 2)
                for u in range(UNITS + LAG):
                    if on(0) and LEAD <= u < UNITS:
                        first_unit_of(r, g, u)
                    if on(2) and u >= LAG:
                        if u == LAG:
                            pe.wait_ge(neg_loaded[g2 % RING], (use(r2, g2) + 1) * NEG_LOADS)
                        second_unit_of(r2 * GROUPS + g2, g2 % RING, u - LAG)
                    if on(3) and u in PRODUCT_AT:
                        r3, g3 = lagged(r, g, 3)
                        product(r3 * GROUPS + g3, g3 % 2, PRODUCT_AT.index(u))
                    if u == 2 and on(1):
                        rn, gn = lagged(r, g, 1)
                        pe.wait_ge(qmax_ready, rn * GROUPS + gn + 1)
                        pe.wait_ge(oT_read, rn * GROUPS + gn + 1)
                        for c in range(TILES):
                            mm = pe.transpose(turnb[0:MAPS, c * P:(c + 1) * P], qmax[:, c, :], k.ident[:, :])
                        mm.then_inc(neg_psum, 1)
                    if prep and u == 3 and 1 <= g < 5:
                        j, J = g - 1, b * 4 + g - 1
                        pe.wait_ge(hT_ready, b + 1)
                        if g == 2:
                            pe.wait_ge(res_ready, J + 1)
                        if g > 2:
                            pe.wait_ge(v_ready, b * TILES + g - 1)
                        pe.matmul(sideb[:, :], wqk[:, j, :], hT[:, :], start=True, stop=True).then_inc(qk_done, 1)
                    if post and g == 7 and u in (4, 7):
                        c = u // 7
                        pe.wait_ge(merged_ready, pb + 2)
                        if c == 0:
                            pe.wait_ge(v_ready, (min(r + 2, B) if isinstance(r, int) else r + 2) * TILES + 1)
                        else:
                            pe.wait_ge(mT_ready, pb * 2 + 1)
                        for i in range(TILES):
                            mm = pe.transpose(sideb[:, i * P:(i + 1) * P], merged[:, i, c * P:(c + 1) * P], k.ident[:, :])
                        mm.then_inc(mT_done, 1)
                    if post and g == 7 and u == 10:
                        pe.wait_ge(mT_ready, pb * 2 + 2)
                        for i in range(TILES):
                            for c in range(2):
                                mm = pe.matmul(sideb[:, i * P:(i + 1) * P], mT[:, c, i * P:(i + 1) * P], k.wo[:, c, :], start=(c == 0), stop=(c == 1))
                        mm.then_inc(wo_done, 1)
                if g + 1 < GROUPS and on(0) or g + 1 == GROUPS and prep:
                    rl, gl = (r, g + 1) if g + 1 < GROUPS else (r + 1, 0)
                    pe.wait_ge(stack_loaded[gl % RING], (use(rl, gl) + 1) * LOADS)
                    for u in range(LEAD):
                        first_unit_of(rl, gl, u)
                if prep and 2 <= g < 6:
                    c, V = g - 2, b * TILES + g - 2
                    pe.wait_ge(v_ready, V + 1)
                    pe.wait_ge(res_ready, b * 4 + min(g, 4) + 1)
                    pe.matmul(sideb[:, 0:H * VD], hT[:, c * P:(c + 1) * P], k.wv[:, :], start=True, stop=True).then_inc(v_done, 1)
                if on(4):
                    r4, g4 = lagged(r, g, 4)
                    G4 = r4 * GROUPS + g4
                    pe.wait_ge(o_read, G4 + 2)
                    if on(1):
                        rn, gn = lagged(r, g, 1)
                        pe.wait_ge(neg_read, rn * GROUPS + gn + 1)
                    else:
                        pe.wait_ge(oT_read, G4 + 4)
                    for c in range(TILES):
                        mm = pe.transpose(turnb[:, c * P:(c + 1) * P], o_sb[:, g4 % 2, c * P:(c + 1) * P], k.ident[:, :])
                    mm.then_inc(oT_done, 1)
                if prep and g == 0:
                    pe.wait_ge(xn_ready, b + 1)
                    pe.wait_ge(gated_ready, r + 2)
                    pe.wait_ge(v_ready, b * TILES + 1)
                    for c in range(TILES):
                        mm = pe.transpose(sideb[:, c * P:(c + 1) * P], xn[:, c, :], k.ident[:, :])
                    mm.then_inc(xnT_done, 1)

            rounds(pe, slot)

        @block.vector
        def _(dve):
            dve.wait_ge(k.attn_loaded, W_LOADS)
            for j in range(4):
                ins = dve.tensor_copy(wqk[:, j, :].rearrange("p (g e h) -> p g e h", e=HD, h=2),
                                      k.wraw[:, j, :].rearrange("p (g h e) -> p g e h", h=2, e=HD))
            ins.then_inc(w_ready, 1)
            fill = Chain(dve, dve_fill).link

            def slot(r, g, on, prep, post):
                b, pb = r + 1, r - 1
                G = r * GROUPS + g
                if prep and g == 0:
                    dve.wait_ge(xnT_done, b + 1)
                    for c in range(TILES):
                        ins = normalize(dve, k, xn[:, c, :], b * TILES + c)
                    ins.then_inc(xn_ready, 1)
                if prep and not on(0):
                    if g == GATES_AT:
                        for gate in (k.gate_a0, k.gate_b0):
                            v, size, sign = (t.rearrange("p b d -> p (b d)") for t in (gate[:, :, :], og[:, :, :], o2[:, :, :]))
                            fill(dve.scalar_tensor_tensor(size, v, -1.0, v, ALU.mult, ALU.max))
                            fill(dve.tensor_scalar(size, size, 0.25, None, ALU.max))
                            fill(dve.tensor_scalar(sign, v, 0.0, 2.0, ALU.is_ge, ALU.mult))
                            fill(dve.scalar_tensor_tensor(v, sign, -1.0, size, ALU.add, ALU.mult))
                    if g == STATS_AT:
                        dve.wait_ge(k.x_loaded, 16)
                        token_stats(dve, fill, k, range(1, B))
                full = [P, TILES * H, VD]
                wide = lambda t: t[:, :].unsqueeze(2).broadcast_to(full)
                at = {(4, 2): 0, (5, 7): 1, (5, 9): 2, (6, 0): 3, (6, 2): 4, (6, 4): 5, (6, 6): 9, (6, 8): 12, (7, 0): 15}
                for u in range(UNITS):
                    if post and (g, u) in at:
                        link = Chain(dve, dve_post, pb * POST_LINKS + at[g, u]).link
                    if post and (g, u) == (4, 2):
                        dve.wait_ge(oT_read, (pb + 1) * GROUPS + 4)
                        dve.wait_ge(og_ready, pb + 2)
                        link(dve.reciprocal(rc[:, :, :, :].rearrange("p c h j -> p c (h j)"), oT[:, (r + 1) % 2, :, :, VD]))
                        dve.tensor_tensor(rc[:, :, :, 1], rc[:, :, :, 1], k.neg_lam[:, :].unsqueeze(1).broadcast_to([P, TILES, H]),
                                          ALU.mult).then_inc(rc_ready, 1)
                    if post and (g, u) == (5, 7):
                        dve.wait_ge(og_ready, pb + 3)
                        link(dve.tensor_reduce(msum[:, :], og[:, :, :], AX, ALU.add))
                    if post and (g, u) == (5, 9):
                        link(dve.scalar_tensor_tensor(oc[:, :, :], wide(msum), -1.0 / VD, og[:, :, :], ALU.mult, ALU.add))
                    if post and (g, u) == (6, 0):
                        link(dve.tensor_tensor(sq[:, :, :], oc[:, :, :], oc[:, :, :], ALU.mult))
                    if post and (g, u) == (6, 2):
                        link(dve.tensor_reduce(vsum[:, :], sq[:, :, :], AX, ALU.add))
                    if post and (g, u) == (6, 4):
                        link(dve.tensor_scalar(vsum[:, :], vsum[:, :], 1.0 / VD, EPS, ALU.mult, ALU.add))
                        rsqrt_start(dve, link, vsum[:, :], vhalf[:, :], orstd[:, :], otmp[:, :])
                    if post and (g, u) in ((6, 6), (6, 8), (7, 0)):
                        rsqrt_newton(dve, link, vhalf[:, :], orstd[:, :], otmp[:, :])
                    if post and (g, u) == (7, 1):
                        dve.wait_ge(mT_done, pb * 2 + 1)
                        dve.scalar_tensor_tensor(merged[:, :, :].rearrange("p c (h e) -> p (c h) e", e=VD), oc[:, :, :], 1.0 - LAM_INIT,
                                                 wide(orstd), ALU.mult, ALU.mult).then_inc(merged_ready, 1)
                    if prep and u == 7 and 1 <= g < 5:
                        j, J = g - 1, b * 4 + g - 1
                        dve.wait_ge(hi_ready, J + 1)
                        dve.wait_ge(split_ready, J + 1)
                        dve.tensor_tensor(res[:, :], sideb[:, :], parts[:, j % 2, 0, :], ALU.subtract).then_inc(res_ready, 1)
                    if on(0):
                        dve.wait_ge(first_unit, G * UNITS + u + 1)
                        bank = p1b[(g * UNITS + u) % FIRST_BANKS][:, :]
                        if u < 8:
                            to = bmax[:, g % 2, u % 4, 4 * (u // 4):4 * (u // 4) + 4]
                            src = bank.rearrange("p (c t) -> p c t", c=4)
                        else:
                            to = bmax[:, g % 2, 2 * (u - 8):2 * (u - 8) + 2, 8:10]
                            src = bank.rearrange("p (m c t) -> p m c t", m=2, c=2)
                        dve.tensor_reduce(to, src, AX, ALU.max).then_inc(first_read, 1)
                    if u == 3 and on(1):
                        rn, gn = lagged(r, g, 1)
                        Gn = rn * GROUPS + gn
                        dve.wait_ge(neg_high, Gn + 1)
                        dve.wait_ge(neg_ready, Gn + 1)
                        dve.scalar_tensor_tensor(nres[:, :], turnb[0:MAPS, :], -1.0, nparts[:, gn % 2, 0, :], ALU.mult, ALU.subtract).then_inc(neg_read, 1)
                if on(0):
                    dve.wait_ge(neg_psum, G + 1)
                    dve.wait_ge(first_read, (G + 1) * UNITS + FIRST_CREDITS)
                    for c, lo, n in ((3, 0, 4), (2, 4, 3), (0, 7, 1), (1, 8, 2)):
                        ins = dve.tensor_reduce(qmax[:, c, :], bmax[:, g % 2, :, lo:lo + n], AX, ALU.max)
                    ins.then_inc(qmax_ready, 1)
                if post and g == 7:
                    dve.wait_ge(wo_done, pb + 2)
                    dve.tensor_tensor(gated[:, :, :], sideb[:, :].rearrange("p (c n) -> p c n", c=TILES),
                                      k.gate_a0[:, bass.ds(pb, 1), :].broadcast_to([P, TILES, D]), ALU.mult).then_inc(gated_ready, 1)
                    dve.wait_ge(gated_ready, pb + 4)
                    x = k.x[:, bass.ds(pb * TILES, TILES), :]
                    dve.tensor_tensor(x, x, gated[:, :, :], ALU.add).then_inc(post_done, 1)

            rounds(dve, slot)


POST_LINKS = 1 + 5 + RSQRT_LINKS


def token_stats(dve, link, k, batches):
    tiles = range(batches[0] * TILES, (batches[-1] + 1) * TILES)
    part = slice(tiles[0], tiles[-1] + 1)
    for t in tiles:
        last = dve.bn_stats(k.bn[:, t, :], k.x[:, t, :])
    link(last)
    for t in tiles:
        last = dve.bn_aggr(k.stats[:, t, :], k.bn[:, t, :])
    link(last)
    link(dve.tensor_scalar(k.bn[:, part, 1], k.stats[:, part, 1], EPS, None, ALU.add))
    rsqrt_steps(dve, link, k.bn[:, part, 1], k.half[:, part], k.rstd[:, part], k.tmp[:, part])


def normalize(dve, k, xn, tile):
    return dve.tensor_scalar(xn, k.x[:, tile, :], k.stats[:, tile, 0:1], k.rstd[:, bass.ds(tile, 1)], ALU.subtract, ALU.mult)


def ffn(nc, d, k):
    FT = FF // P
    HID_RING = 4
    with ExitStack() as ctx:
        def sb(name, shape, dt=F32):
            return ctx.enter_context(nc.sbuf_tensor(name, shape, dt))

        def ps(name):
            return ctx.enter_context(nc.psum_tensor(name, [P, 512], F32))

        def sem(name):
            return ctx.enter_context(nc.semaphore(name))

        w1, w2, b2, col, loaded = k.w1, k.w2, k.b2, k.col, k.ffn_loaded
        th = sb("th", [P, 8, FT])
        coef = sb("coef", [P, FT])
        xn = sb("f_xn", [P, TILES, D])
        hT = sb("f_hT", [P, S])
        hid = sb("hid", [P, HID_RING, FT, S])
        arg = sb("arg", [P, 2, FT, S])
        turns = sb("turns", [P, 2, FT, S])
        red = sb("red", [P, 2, FT, S])
        sine = sb("sine", [P, 2, FT, S])
        relu = sb("relu", [P, 2, FT, S])
        gated = sb("f_gated", [P, TILES, D])
        tpb = ps("tpb")
        upb = [ps(f"upb{a}") for a in range(2)]
        outb = [ps(f"outb{a}") for a in range(2)]
        angle, th_sin = sem("angle"), sem("th_sin")
        xn_ready, xT_done, hT_ready, up_done, hid_ready, arg_ready, turns_ready, red_ready, clamped, sin_ready, gate_done, act_ready, out_done, gated_ready, x_ready = (
            sem(n) for n in ("f_xn_ready", "f_xT_done", "f_hT_ready", "up_done", "hid_ready", "arg_ready", "turns_ready", "red_ready", "clamped",
                             "sin_ready", "gate_done", "act_ready", "out_done", "f_gated_ready", "f_x_ready"))
        dve_setup, pool_own, passed = (
            sem("ffn_dve_setup"), sem("ffn_pool"), sem("ffn_passed"))
        block = ctx.enter_context(nc.Block())
        CREDITS = {xT_done: 1, hT_ready: 1, up_done: FT, hid_ready: 2, red_ready: 2, sin_ready: 2, gate_done: 2 * FT, out_done: 2,
                   gated_ready: 2, x_ready: 1}
        LOADS = 7 * 16

        def rounds(eng, step):
            def one(r, at):
                step(r, at % 2, norm=at + 2 < B, up=0 <= at + 1 < B, reduce=0 <= at < B, sines=0 <= at - 1 < B, down=0 <= at - 2 < B)

            for at in range(-2, 2):
                one(at, at)
            with eng.Fori(1, B // 2 - 1) as it:
                for a in range(2):
                    one(it * 2 + a, 2 + a)
            for at in range(B - 2, B + 2):
                one(at, at)

        @block.sync
        def _(sp):
            sp.wait_ge(x_ready, B + 1)

        @block.tensor
        def _(pe):
            pe.wait_ge(loaded, LOADS)

            def step(r, a, norm, up, reduce, sines, down):
                if up:
                    b = r + 1
                    pe.wait_ge(xn_ready, b + 1)
                    pe.wait_ge(hT_ready, b + 1)
                    for c in range(TILES):
                        mm = pe.transpose(tpb[:, c * P:(c + 1) * P], xn[:, c, :], k.ident[:, :])
                    mm.then_inc(xT_done, 1)
                if up:
                    b = r + 1
                    pe.wait_ge(hT_ready, b + 2)
                    for j in range(FT):
                        pe.wait_ge(hid_ready, b * FT + j + 1)
                        pe.matmul(upb[j % 2][:, :], w1[:, j * P:(j + 1) * P], hT[:, :], start=True, stop=True).then_inc(up_done, 1)
                if down:
                    b = r - 2
                    pe.wait_ge(gated_ready, b + 1)
                    pe.matmul(outb[a][:, :].rearrange("p (c n) -> p c n", c=TILES), k.ident[:, :],
                              b2[:, :].unsqueeze(1).broadcast_to([P, TILES, D]), start=True, stop=False, skip_group_check=True)
                    pe.wait_ge(act_ready, b + 1)
                    for j in range(FT):
                        for c in range(TILES):
                            mm = pe.matmul(outb[a][:, c * P:(c + 1) * P], relu[:, a, j, c * P:(c + 1) * P], w2[:, j, :],
                                           start=False, stop=(j == FT - 1), skip_group_check=True)
                    mm.then_inc(out_done, 1)

            rounds(pe, step)

        @block.scalar
        def _(act):
            act.wait_ge(angle, 1)
            act.activation(th[:, 6:8, :], th[:, 4:6, :], ACT.Sin).then_inc(th_sin, 1)
            act.wait_ge(loaded, LOADS)

            def step(r, a, norm, up, reduce, sines, down):
                if up:
                    b = r + 1
                    act.wait_ge(xT_done, b + 2)
                    act.wait_ge(up_done, (b + 1) * FT)
                    act.activation(hT[:, :], tpb[:, :], ACT.Identity, scale=k.mod[:, 0, 4, bass.ds(b, 1)],
                                   bias=k.mod[:, 0, 3, bass.ds(b, 1)]).then_inc(hT_ready, 1)
                if sines:
                    b = r - 1
                    act.wait_ge(clamped, b + 1)
                    act.wait_ge(gate_done, (b + 1) * FT)
                    act.activation(sine[:, 1 - a, :, :], red[:, 1 - a, :, :], ACT.Sin).then_inc(sin_ready, 1)
                if up:
                    b = r + 1
                    act.wait_ge(red_ready, b + 1)
                    for j in range(FT):
                        act.wait_ge(up_done, (b + 1) * FT + j + 1)
                        act.sem_inc(passed, 1)
                        act.activation(hid[:, b % HID_RING, j, :], upb[j % 2][:, :], ACT.Identity, bias=col[:, 0, j:j + 1]).then_inc(hid_ready, 1)
                    for j in range(FT):
                        act.wait_ge(hid_ready, b * FT + j + 3)
                        act.sem_inc(passed, 1)
                        act.activation(arg[:, 1 - a, j, :], hid[:, b % HID_RING, j, :], ACT.Identity, scale=0.1, bias=col[:, 1, j:j + 1]).then_inc(arg_ready, 1)
                if sines:
                    b = r - 1
                    act.wait_ge(gate_done, (b + 3) * FT)
                    act.wait_ge(out_done, b + 1)
                    act.sem_inc(passed, 1)
                    act.activation(flat(relu[:, 1 - a, :, :]), flat(hid[:, (r + HID_RING - 1) % HID_RING, :, :]), ACT.Relu).then_inc(act_ready, 1)

            rounds(act, step)

        @block.gpsimd
        def _(pool):
            for s, n in CREDITS.items():
                pool.sem_inc(s, n)

            def step(r, a, norm, up, reduce, sines, down):
                if reduce:
                    chain = Chain(pool, pool_own, r * 2 * FT, passed)
                    pool.wait_ge(red_ready, r + 1)
                    pool.sem_inc(passed, 1)
                    for j in range(FT):
                        pool.wait_ge(arg_ready, r * FT + j + 1)
                        pool.sem_inc(passed, 1)
                        chain.link(pool.tensor_scalar(turns[:, a, j, :], arg[:, a, j, :], INV_2PI, ROUND, ALU.mult, ALU.add))
                        chain.link(pool.tensor_scalar(turns[:, a, j, :], turns[:, a, j, :], -ROUND, -TWO_PI_HI, ALU.add, ALU.mult))
                        pool.tensor_tensor(arg[:, a, j, :], arg[:, a, j, :], turns[:, a, j, :], ALU.add).then_inc(turns_ready, 1)

            rounds(pool, step)

        @block.vector
        def _(dve):
            link = Chain(dve, dve_setup).link
            token_stats(dve, link, k, range(1))
            dve.wait_ge(loaded, LOADS)
            theta = col[:, 1, :]
            link(dve.tensor_scalar(th[:, 0, :], theta, INV_2PI, ROUND, ALU.mult, ALU.add))
            link(dve.tensor_scalar(th[:, 0, :], th[:, 0, :], ROUND, None, ALU.subtract))
            link(dve.scalar_tensor_tensor(th[:, 4, :], th[:, 0, :], -TWO_PI_HI, theta, ALU.mult, ALU.add))
            link(dve.scalar_tensor_tensor(th[:, 4, :], th[:, 0, :], -TWO_PI_LO, th[:, 4, :], ALU.mult, ALU.add))
            link(dve.tensor_scalar(th[:, 4, :], th[:, 4, :], PI_BELOW, -PI_BELOW, ALU.min, ALU.max))
            link(dve.scalar_tensor_tensor(th[:, 1, :], th[:, 4, :], -1.0, th[:, 4, :], ALU.mult, ALU.max))
            dve.tensor_scalar(th[:, 5, :], th[:, 1, :], -1.0, math.pi / 2, ALU.mult, ALU.add).then_inc(angle, 1)
            dve.wait_ge(th_sin, 1)
            link(dve.tensor_tensor(th[:, 2, :], th[:, 7, :], col[:, 2, :], ALU.mult))
            link(dve.tensor_tensor(th[:, 3, :], th[:, 6, :], col[:, 3, :], ALU.mult))
            link(dve.tensor_tensor(th[:, 2, :], th[:, 2, :], th[:, 3, :], ALU.add))
            link(dve.scalar_tensor_tensor(coef[:, :], th[:, 2, :], 0.1, col[:, 3, :], ALU.mult, ALU.mult))

            def step(r, a, norm, up, reduce, sines, down):
                if norm:
                    b = r + 2
                    dve.wait_ge(xT_done, b + 1)
                    for c in range(TILES):
                        ins = normalize(dve, k, xn[:, c, :], b * TILES + c)
                    ins.then_inc(xn_ready, 1)
                    if not up:
                        token_stats(dve, link, k, range(1, B))
                if sines:
                    b = r - 1
                    dve.wait_ge(sin_ready, b + 3)
                    for j in range(FT):
                        h = hid[:, (r + HID_RING - 1) % HID_RING, j, :]
                        dve.scalar_tensor_tensor(h, sine[:, 1 - a, j, :], coef[:, j:j + 1], h, ALU.mult, ALU.add).then_inc(gate_done, 1)
                if reduce:
                    dve.wait_ge(turns_ready, (r + 1) * FT)
                    dve.wait_ge(sin_ready, r + 1)
                    dve.sem_inc(passed, 1)
                    dve.scalar_tensor_tensor(flat(red[:, a, :, :]), flat(turns[:, a, :, :]), TWO_PI_LO / TWO_PI_HI, flat(arg[:, a, :, :]),
                                             ALU.mult, ALU.add).then_inc(red_ready, 1)
                    dve.wait_ge(red_ready, r + 3)
                    dve.tensor_scalar(flat(red[:, a, :, :]), flat(red[:, a, :, :]), PI_BELOW, -PI_BELOW, ALU.min, ALU.max).then_inc(clamped, 1)
                if down:
                    b = r - 2
                    dve.wait_ge(out_done, b + 3)
                    dve.wait_ge(x_ready, b + 1)
                    dve.sem_inc(passed, 1)
                    dve.tensor_tensor(gated[:, :, :], outb[a][:, :].rearrange("p (c n) -> p c n", c=TILES),
                                      k.gate_b0[:, bass.ds(b, 1), :].broadcast_to([P, TILES, D]), ALU.mult).then_inc(gated_ready, 1)
                    dve.wait_ge(gated_ready, b + 3)
                    x = k.x[:, bass.ds(b * TILES, TILES), :]
                    dve.tensor_tensor(x, x, gated[:, :, :], ALU.add).then_inc(x_ready, 1)

            rounds(dve, step)


def flat(t):
    return t.rearrange("p j t -> p (j t)")


LOG1P = (1.0, -0.49999892711639404, 0.33329710364341736, -0.24951615929603577, 0.1966327428817749, -0.1526966691017151,
         0.10543623566627502, -0.05637361481785774, 0.019542528316378593, -0.0031760570127516985)
LOG_DVE = 4
LOG_AT = (9, 10, 11, 12)
Y_LAG = 6
CH_RING = 8


def scan(nc, d, k):
    with ExitStack() as ctx:
        def sb(name, shape, dt=F32):
            return ctx.enter_context(nc.sbuf_tensor(name, shape, dt))

        def ps(name):
            return ctx.enter_context(nc.psum_tensor(name, [P, 512], F32))

        def sem(name):
            return ctx.enter_context(nc.semaphore(name))

        conv_w, wbc, bbc, wdt, bdt, wdtp, bdtp, nA, dco, loaded = (
            k.conv_w, k.wbc, k.bbc, k.wdt, k.bdt, k.wdtp, k.bdtp, k.nA, k.dco, k.scan_loaded)
        diag = sb("diag", [P, 4, P])
        sel = sb("sel", [3 * BC, BC, P], BF16)
        pick = sb("s_pick", [3 * BC, BC], BF16)
        xn = sb("s_xn", [P, TILES, D])
        hT = sb("s_hT", [P, 3, S + 2])
        us = sb("us", [P, S])
        bc = sb("bc", [3 * BC, S])
        bcp = sb("bcp", [3 * BC, 2, S], BF16)
        t1 = sb("t1", [RANK, S])
        zb, na, ee, pl = (sb(n, [P, S]) for n in ("zb", "na", "ee", "pl"))
        dt = sb("dt", [P, 2, S])
        dtx = sb("dtx", [P, 2, S])
        dA = sb("dA", [P, 4, S])
        dBx = sb("dBx", [P, 2, S])
        hs = sb("hs", [P, CH_RING, S])
        csb = sb("csb", [P, 2, S])
        ch = sb("ch", [P, CH_RING, S])
        yg = sb("yg", [P, S])
        preb, pre2 = ps("s_preb"), ps("s_pre2")
        bb = [ps(f"bb{i}") for i in range(2)]
        cb = [ps(f"cb{i}") for i in range(2)]
        yb = ps("yb")
        postb = ps("s_postb")
        sel_ready, consts, nA_ready = sem("sel_ready"), sem("s_consts"), sem("nA_ready")
        xn_ready, xT_done, hT_ready, u_ready, us_ready, bc_psum, bc_ready, dtr_psum, t1_ready, z_psum, zb_ready, na_ready, ee_ready, dt_ready, parts_ready = (
            sem("s_" + n) for n in ("xn_ready", "xT_done", "hT_ready", "u_ready", "us_ready", "bc_psum", "bc_ready", "dtr_psum",
                                    "t1_ready", "z_psum", "zb_ready", "na_ready", "ee_ready", "dt_ready", "parts_ready"))
        b_done, c_done, dA_ready, dBx_ready, scan_done, ch_ready, y_acc, yg_ready, out_done, x_ready = (
            sem("s_" + n) for n in ("b_done", "c_done", "dA_ready", "dBx_ready", "scan_done", "ch_ready", "y_acc", "yg_ready",
                                    "out_done", "x_ready"))
        dve_setup, dve_pre, pool_log = sem("s_dve_setup"), sem("s_dve_pre"), sem("s_pool_log")
        high_ready, poly_ready, diag_ready, c_copied, pool_ch_ready = sem("s_high_ready"), sem("s_poly_ready"), sem("diag_ready"), sem("c_copied"), sem("pool_ch_ready")
        passed, act_passed = sem("s_passed"), sem("s_act_passed")
        block = ctx.enter_context(nc.Block())
        CREDITS = {x_ready: 1, y_acc: CH_RING, ch_ready: 1, c_copied: 1, pool_ch_ready: CH_RING // 2, dBx_ready: 2, yg_ready: 1, zb_ready: 1,
                   parts_ready: 1, t1_ready: 1, scan_done: 4, dt_ready: 1}
        HALF = N // 2
        LOADS = (3 + 3 + 7) * 16
        LOG_LINKS = 2 * (len(LOG1P) - 2 - LOG_DVE) + 1

        def rounds(eng, step):
            for r0, r1 in ((-2, -1), (-1, 0), (0, 1), (1, B - 2), (B - 2, B - 1), (B - 1, B), (B, B + 1)):
                on = dict(front=r0 + 2 < B, back=-1 <= r0 < B - 1, main=0 <= r0 < B, post=r0 >= 1)
                if r1 - r0 > 1:
                    with eng.Fori(r0, r1) as r:
                        step(r, **on)
                else:
                    step(r0, **on)

        @block.sync
        def _(sp):
            sp.wait_ge(k.w_filled, 2)
            f = "L1_ffn_"
            sp.dma_start(k.w[:, 0, 0:E * EF].rearrange("p (e f) -> p e f", e=E), d[f + "W_up"].rearrange("e d f -> d e f")).then_inc(k.w_loaded, 16)
            sp.dma_start(k.w[:, 1, 0:E * EF].rearrange("p (t n) -> p t n", t=ET), d[f + "W_down"].rearrange("(t a) f n -> (a f) t n", a=2)).then_inc(k.w_loaded, 16)
            sp.dma_start(k.w[:, 0, E * EF:E * EF + EF], d[f + "Ws_up"]).then_inc(k.w_loaded, 16)
            sp.dma_start(k.w[0:EF, 1, E * EF:E * EF + D], d[f + "Ws_down"]).then_inc(k.w_loaded, 16)
            sp.wait_ge(x_ready, B + 1)

        @block.gpsimd
        def _(pool):
            for s, n in CREDITS.items():
                pool.sem_inc(s, n)
            pool.memset(k.w[:, 0, E * EF + EF:W_COLS], 0.0).then_inc(k.w_filled, 1)
            pool.wait_ge(k.w_filled, 1)
            pool.memset(k.w[EF:P, 1, E * EF:W_COLS], 0.0).then_inc(k.w_filled, 1)
            pool.wait_ge(k.w_filled, 2)
            pool.memset(hT[:, :, :], 0.0).then_inc(consts, 1)
            pool.memset(pick[:, :], 0.0).then_inc(consts, 1)
            for j in range(3):
                pool.wait_ge(consts, 2 + j)
                pool.affine_select(out=pick[:, :], in_=pick[:, :], compare_op=ALU.not_equal, fill=1.0, base=-j * BC,
                                   pattern=[[-1, BC]], channel_multiplier=1).then_inc(consts, 1)

            def step(r, front, back, main, post):
                b = r + 1
                chain = Chain(pool, pool_log, b * LOG_LINKS, passed)
                link = chain.link
                p, e = pl[:, :], ee[:, :]

                def log_start():
                    pool.wait_ge(ee_ready, b + 1)
                    pool.wait_ge(dt_ready, b + 1)
                    pool.sem_inc(passed, 1)
                    link(pool.tensor_scalar(p, e, LOG1P[-1], LOG1P[-2], ALU.mult, ALU.add))

                def log_more(*coefficients):
                    for c in coefficients:
                        link(pool.tensor_tensor(p, p, e, ALU.mult))
                        link(pool.tensor_scalar(p, p, 1.0, c, ALU.mult, ALU.add))

                def log_end():
                    pool.tensor_tensor(p, p, e, ALU.mult).then_inc(poly_ready, 1)
                    assert chain.n == LOG_LINKS, chain.n

                def split_weights():
                    pool.wait_ge(k.w_rounded, b + 1)
                    pool.tensor_tensor(chunk(k.w_low, b), chunk(k.w, b), chunk(k.w_high, b), ALU.subtract).then_inc(k.w_ready, 1)

                if main:
                    for n in range(1, N, 2):
                        q, m = r * N + n, r * HALF + n // 2
                        pool.wait_ge(c_copied, m + 2)
                        pool.wait_ge(scan_done, q + 5)
                        pool.wait_ge(y_acc, q + 1)
                        pool.tensor_tensor(ch[:, n % CH_RING, :], hs[:, n % CH_RING, :], csb[:, n // 2 % 2, :], ALU.mult).then_inc(pool_ch_ready, 1)
                        if back and n == 1:
                            log_start()
                        if back and n == 3:
                            log_more(LOG1P[-3])
                        if back and n == 5:
                            log_more(*LOG1P[-4:LOG_DVE - 1:-1])
                        if back and n == 7:
                            log_end()
                        if back and n == 15:
                            split_weights()
                elif back:
                    log_start(), log_more(*LOG1P[-3:LOG_DVE - 1:-1]), log_end(), split_weights()

            rounds(pool, step)

        @block.tensor
        def _(pe):
            pe.wait_ge(loaded, LOADS)
            pe.wait_ge(sel_ready, 1)
            pe.wait_ge(diag_ready, 1)

            def step(r, front, back, main, post):
                b = r + 2

                def front_turn():
                    pe.wait_ge(xn_ready, b + 1)
                    pe.wait_ge(zb_ready, b + 1)
                    for c in range(TILES):
                        mm = pe.transpose(preb[:, c * P:(c + 1) * P], xn[:, c, :], k.ident[:, :])
                    mm.then_inc(xT_done, 1)

                def conv():
                    pe.wait_ge(hT_ready, b + 1)
                    pe.wait_ge(t1_ready, b + 1)
                    for j in range(3):
                        mm = pe.matmul(pre2[:, :], diag[:, j, :], hT[:, b % 3, j:j + S], start=(j == 0), stop=(j == 2))
                    mm.then_inc(u_ready, 1)

                def front_bc():
                    pe.wait_ge(us_ready, b + 1)
                    pe.matmul(preb[0:3 * BC, :], wbc[:, :, :].rearrange("p j n -> p (j n)"), us[:, :], start=True, stop=True).then_inc(bc_psum, 1)
                    pe.matmul(pre2[0:RANK, :], wdt[:, :], us[:, :], start=True, stop=True).then_inc(dtr_psum, 1)

                def front_z():
                    pe.wait_ge(t1_ready, b + 2)
                    pe.wait_ge(bc_ready, b + 1)
                    pe.matmul(preb[:, :], wdtp[:, :], t1[:, :], start=True, stop=True).then_inc(z_psum, 1)

                def add_state(r, n):
                    if n % 2:
                        pe.wait_ge(pool_ch_ready, r * HALF + n // 2 + 1 + CH_RING // 2)
                    else:
                        pe.wait_ge(ch_ready, r * HALF + n // 2 + 2)
                    pe.matmul(yb[:, :], k.ident[:, :], ch[:, n % CH_RING, :], start=False, stop=(n == N - 1), skip_group_check=True).then_inc(y_acc, 1)

                def turn_back():
                    pe.wait_ge(yg_ready, r + 1)
                    pe.wait_ge(x_ready, r)
                    for c in range(TILES):
                        mm = pe.transpose(postb[:, c * P:(c + 1) * P], yg[:, c * P:(c + 1) * P], k.ident[:, :])
                    mm.then_inc(out_done, 1)

                if not main:
                    if front:
                        front_turn(), conv(), front_bc(), front_z()
                    if post:
                        for n in range(N - Y_LAG, N):
                            add_state(r - 1, n)
                        turn_back()
                    return
                par = r % 2
                pe.wait_ge(parts_ready, r + 2)

                def spread_b(n):
                    pe.wait_ge(dBx_ready, r * N + n + 1)
                    pe.matmul(bb[n % 2][:, :], sel[:, n, :], bcp[:, par, :], start=True, stop=True).then_inc(b_done, 1)

                spread_b(0)
                for n in range(N):
                    m = r * HALF + n // 2
                    if n + 1 < N:
                        spread_b(n + 1)
                    pe.wait_ge((ch_ready, c_copied)[n % 2], m + 1)
                    pe.matmul(cb[n % 2][:, :], sel[:, N + n, :], bcp[:, par, :], start=True, stop=True).then_inc(c_done, 1)
                    if n == Y_LAG:
                        pe.wait_ge(yg_ready, r + 1)
                        pe.matmul(yb[:, :], diag[:, 3, :], hT[:, (r + 3) % 3, 1:S + 1], start=True, stop=False, skip_group_check=True)
                    if n >= Y_LAG:
                        add_state(r, n - Y_LAG)
                    elif post and n < Y_LAG // 2:
                        add_state(r - 1, N - Y_LAG + 2 * n)
                        add_state(r - 1, N - Y_LAG + 2 * n + 1)
                    if front:
                        for at, f in ((2, front_turn), (5, conv), (8, front_bc), (11, front_z)):
                            if n == at:
                                f()
                    if post and n == Y_LAG:
                        turn_back()

            rounds(pe, step)

        @block.scalar
        def _(act):
            act.wait_ge(loaded, LOADS)
            act.activation(nA[:, :], nA[:, :], ACT.Exp).then_inc(nA_ready, 1)
            act.wait_ge(nA_ready, 1)
            act.activation(nA[:, :], nA[:, :], ACT.Copy, scale=-1.0).then_inc(nA_ready, 1)
            act.wait_ge(nA_ready, 2)
            act.wait_ge(consts, 5)
            act.activation(sel[:, :, :], pick[:, :].unsqueeze(2).broadcast_to([3 * BC, BC, P]), ACT.Copy).then_inc(sel_ready, 1)

            def step(r, front, back, main, post):
                b = r + 2

                def front_h():
                    act.wait_ge(xT_done, b + 1)
                    act.activation(hT[:, b % 3, 1:S + 1], preb[:, :], ACT.Identity, scale=k.mod[:, 1, 1, bass.ds(b, 1)],
                                   bias=k.mod[:, 1, 0, bass.ds(b, 1)]).then_inc(hT_ready, 1)

                def front_silu():
                    act.wait_ge(u_ready, b + 1)
                    act.activation(us[:, :], pre2[:, :], ACT.Silu).then_inc(us_ready, 1)

                def front_bc():
                    act.wait_ge(bc_psum, b + 1)
                    act.wait_ge(parts_ready, b + 1)
                    act.activation(bc[:, :], preb[0:3 * BC, :], ACT.Identity, bias=bbc[:, 0:1]).then_inc(bc_ready, 1)
                    act.wait_ge(dtr_psum, b + 1)
                    act.activation(t1[:, :], pre2[0:RANK, :], ACT.Identity, bias=bdt[:, 0:1]).then_inc(t1_ready, 1)

                def front_z():
                    act.wait_ge(z_psum, b + 1)
                    act.wait_ge(dt_ready, b + 1)
                    act.activation(zb[:, :], preb[:, :], ACT.Identity, bias=bdtp[:, 0:1]).then_inc(zb_ready, 1)

                def front_exp():
                    act.wait_ge(na_ready, b + 1)
                    act.wait_ge(dt_ready, b + 1)
                    act.activation(ee[:, :], na[:, :], ACT.Exp).then_inc(ee_ready, 1)

                def back_parts():
                    b = r + 1
                    act.wait_ge(bc_ready, b + 1)
                    act.activation(bcp[:, b % 2, :], bc[:, :], ACT.Copy).then_inc(high_ready, 1)

                def gate():
                    act.wait_ge(y_acc, r * N + CH_RING)
                    act.wait_ge(x_ready, r)
                    act.activation(yg[:, :], yb[:, :], ACT.Copy, scale=k.mod[:, 1, 2, bass.ds(r - 1, 1)]).then_inc(yg_ready, 1)

                def split_weights():
                    b = r + 1
                    if not main:
                        act.wait_ge(k.w_loaded, 4 * 16)
                    act.activation(chunk(k.w, b), chunk(k.w, b), ACT.Copy, scale=W_SCALE).then_inc(k.w_scaled, 1)
                    act.wait_ge(k.w_scaled, b + 1)
                    act.sem_inc(act_passed, 1)
                    act.activation(chunk(k.w_high, b), chunk(k.w, b), ACT.Copy).then_inc(k.w_rounded, 1)

                if not main:
                    if back:
                        back_parts()
                    if front:
                        front_h(), front_silu(), front_bc(), front_z(), front_exp()
                    if back:
                        split_weights()
                    if post:
                        gate()
                    return
                par = r % 2
                act.wait_ge(dt_ready, r + 2)

                def copy_c(n):
                    m = r * HALF + n // 2
                    act.wait_ge(c_done, r * N + n + 1)
                    act.wait_ge(pool_ch_ready, m - 1 + CH_RING // 2)
                    act.activation(csb[:, n // 2 % 2, :], cb[n % 2][:, :], ACT.Copy).then_inc(c_copied, 1)

                for n in range(N):
                    q = r * N + n
                    act.wait_ge(scan_done, q + 1)
                    act.sem_inc(act_passed, 1)
                    act.activation(dA[:, n % 4, :], dt[:, par, :], ACT.Exp, scale=nA[:, n:n + 1]).then_inc(dA_ready, 1)
                    if n and n % 2 == 0:
                        copy_c(n - 1)
                    if post and n == Y_LAG // 2 + 1:
                        gate()
                    if back and n == 1:
                        back_parts()
                    if back and n == 10:
                        split_weights()
                    if front:
                        for at, f in ((3, front_h), (6, front_silu), (9, front_bc), (14, front_z), (15, front_exp)):
                            if n == at:
                                f()
                copy_c(N - 1)

            rounds(act, step)

        @block.vector
        def _(dve):
            setup_link = Chain(dve, dve_setup).link
            token_stats(dve, setup_link, k, range(1))
            dve.wait_ge(loaded, LOADS)
            for j in range(4):
                ins = dve.tensor_scalar(diag[:, j, :], k.ident[:, :], conv_w[:, j:j + 1] if j < 3 else dco[:, 0:1], None, ALU.mult)
            ins.then_inc(diag_ready, 1)
            PRE_LINKS = 3 + LOG_DVE

            def step(r, front, back, main, post):
                b = r + 1
                plink = Chain(dve, dve_pre, b * PRE_LINKS).link

                def front_norm():
                    b = r + 2
                    for c in range(TILES):
                        ins = normalize(dve, k, xn[:, c, :], b * TILES + c)
                    ins.then_inc(xn_ready, 1)

                def front_abs():
                    b = r + 2
                    dve.wait_ge(zb_ready, b + 2)
                    dve.scalar_tensor_tensor(na[:, :], zb[:, :], -1.0, zb[:, :], ALU.mult, ALU.min).then_inc(na_ready, 1)

                def back_parts():
                    dve.wait_ge(high_ready, b + 1)
                    plink(dve.tensor_tensor(bc[:, :], bc[:, :], bcp[:, b % 2, :], ALU.subtract))
                    dve.tensor_copy(bcp[BC:2 * BC, b % 2, :], bc[BC:2 * BC, :])
                    plink(dve.tensor_copy(bcp[2 * BC:3 * BC, b % 2, :], bc[2 * BC:3 * BC, :]))
                    lo = bcp[2 * BC:3 * BC, b % 2, :]
                    dve.tensor_tensor(lo, bc[2 * BC:3 * BC, :], lo, ALU.subtract).then_inc(parts_ready, 1)

                def log_end(c):
                    plink(dve.scalar_tensor_tensor(pl[:, :], pl[:, :], c, ee[:, :], ALU.add, ALU.mult))

                def softplus():
                    plink(dve.scalar_tensor_tensor(dt[:, b % 2, :], zb[:, :], 0.0, pl[:, :], ALU.max, ALU.add))

                def weigh():
                    dve.tensor_tensor(dtx[:, b % 2, :], dt[:, b % 2, :], hT[:, b % 3, 1:S + 1], ALU.mult).then_inc(dt_ready, 1)

                def residual():
                    dve.wait_ge(out_done, r)
                    x = k.x[:, bass.ds((r - 1) * TILES, TILES), :]
                    dve.tensor_tensor(x, x, postb[:, :].rearrange("p (c n) -> p c n", c=TILES), ALU.add).then_inc(x_ready, 1)

                if not main:
                    if front:
                        front_norm()
                    if back:
                        back_parts(), dve.wait_ge(poly_ready, b + 1)
                        for c in LOG1P[LOG_DVE - 1::-1]:
                            log_end(c)
                        softplus(), weigh()
                    if front:
                        if not back:
                            token_stats(dve, setup_link, k, range(1, B))
                        front_abs()
                    if post:
                        residual()
                    return
                par = r % 2
                dve.wait_ge(dt_ready, r + 2)

                def enter(n):
                    q = r * N + n
                    dve.wait_ge(b_done, q + 1)
                    dve.tensor_tensor(dBx[:, n % 2, :], dtx[:, par, :], bb[n % 2][:, :], ALU.mult).then_inc(dBx_ready, 1)

                enter(0)
                for n in range(N):
                    q = r * N + n
                    dve.wait_ge(dA_ready, q + 1)
                    dve.wait_ge(dBx_ready, q + 3)
                    if n % 2:
                        dve.wait_ge(pool_ch_ready, r * HALF + n // 2 + 1)
                    dve.tensor_tensor_scan(hs[:, n % CH_RING, :], dA[:, n % 4, :], dBx[:, n % 2, :], 0.0, ALU.mult, ALU.add).then_inc(scan_done, 1)
                    if n + 1 < N:
                        enter(n + 1)
                    if n % 2 == 0:
                        dve.wait_ge(scan_done, q + 5)
                        dve.wait_ge(c_done, q + 1)
                        dve.wait_ge(y_acc, q + 1)
                        dve.tensor_tensor(ch[:, n % CH_RING, :], hs[:, n % CH_RING, :], cb[n % 2][:, :], ALU.mult).then_inc(ch_ready, 1)
                    if front and n == 0:
                        front_norm()
                    if front and n == 15:
                        front_abs()
                    if back:
                        if n == 3:
                            back_parts()
                        if n == LOG_AT[0]:
                            dve.wait_ge(poly_ready, b + 1)
                        for c, at in zip(LOG1P[LOG_DVE - 1::-1], LOG_AT):
                            if n == at:
                                log_end(c)
                        if n == LOG_AT[-1]:
                            softplus()
                        if n == LOG_AT[-1] + 1:
                            weigh()
                    if post and n == Y_LAG + 2:
                        residual()

            rounds(dve, step)


def experts(nc, d, k, out):
    SLOTS = ET + 1
    RING = 5
    DOWN_LAG = 3
    LOW = 2.0 ** 11
    with ExitStack() as ctx:
        def sb(name, shape, dt=F32):
            return ctx.enter_context(nc.sbuf_tensor(name, shape, dt))

        def ps(name):
            return ctx.enter_context(nc.psum_tensor(name, [P, 512], F32))

        def sem(name):
            return ctx.enter_context(nc.semaphore(name))

        cent, ebias, loaded = k.cent, k.ebias, k.moe_loaded
        centT = sb("centT", [P, E])
        pick = sb("e_pick", [P, ET, 2], FP16)
        sel = sb("sel_e", [P, ET, P], FP16)
        xn = sb("e_xn", [P, TILES, D])
        hT = sb("e_hT", [P, S])
        hTh, hTl = sb("e_hTh", [P, 2, S], FP16), sb("e_hTl", [P, 2, S], FP16)
        biased = sb("biased", [P, TILES, E])
        rest = sb("rest", [P, TILES, E])
        top = sb("top", [P, TILES, TOPK])
        sig = sb("sig", [P, TILES, E])
        wsum = sb("wsum", [P, TILES])
        cw = sb("cw", [P, TILES, 2, E])
        parts = sb("cw_parts", [P, 2, S], FP16)
        low = sb("cw_low", [P, S])
        act_u = sb("act_u", [P, 2, S])
        hid = sb("e_hid", [P, RING, S])
        hid_h, hid_l = sb("hid_h", [P, RING, S], FP16), sb("hid_l", [P, RING, S], FP16)
        gate = sb("e_gate", [P, B])
        yg = sb("e_yg", [P, S])
        ub = [ps(f"ub{i}") for i in range(2)]
        cb = [ps(f"e_cb{i}") for i in range(2)]
        yb, preb, routeb, postb = ps("e_yb"), ps("e_preb"), ps("routeb"), ps("e_postb")
        consts, sel_ready = sem("e_consts"), sem("e_sel_ready")
        cent_psum, cent_ready = sem("cent_psum"), sem("cent_ready")
        xn_ready, xT_done, hT_ready, aff_done, sig_ready, cw_ready, cwT_done, high_ready, low_read, parts_ready = (
            sem("e_" + n) for n in ("xn_ready", "xT_done", "hT_ready", "aff_done", "sig_ready", "cw_ready", "cwT_done",
                                    "high_ready", "low_read", "parts_ready"))
        biased_ready, top_ready, gate_ready = sem("biased_ready"), sem("top_ready"), sem("gate_ready")
        u_done, c_done, silu_ready, hid_ready, hid_rounded, split_ready, down_done, yg_ready, turned, x_ready, hT_split = (
            sem("e_" + n) for n in ("u_done", "c_done", "silu_ready", "hid_ready", "hid_rounded", "split_ready", "down_done", "yg_ready",
                                    "turned", "x_ready", "hT_split"))
        stored, passed = sem("stored"), sem("e_passed")
        dve_setup, dve_pre = sem("e_dve_setup"), sem("e_dve_pre")
        block = ctx.enter_context(nc.Block())
        CREDITS = {silu_ready: RING, hid_ready: RING, split_ready: RING, down_done: RING, yg_ready: 1, turned: 1, x_ready: 1, parts_ready: 2, low_read: 1,
                   biased_ready: 1, top_ready: 1, aff_done: 1, cwT_done: 1}
        LOADS = 2 * 16

        def place(T):
            return T % (RING - 1) if T < ET else RING - 1

        def bank(T):
            return T % 2

        def free(q, T, where):
            before = min(n for n in range(1, SLOTS + 1) if where((T - n) % SLOTS) == where(T))
            return q - before + 1 + RING

        PRE_LINKS = 7

        def rounds(eng, step):
            step(-1, pre=True, main=False, post=False)
            step(0, pre=True, main=True, post=False)
            with eng.Fori(1, B - 1) as r:
                step(r, pre=True, main=True, post=True)
            step(B - 1, pre=False, main=True, post=True)
            step(B, pre=False, main=False, post=True)

        @block.sync
        def _(sp):
            with sp.Fori(0, B) as r:
                sp.wait_ge(x_ready, r + 2)
                sp.dma_start(out[r, :, :].rearrange("(i p) d -> p i d", p=P), k.x[:, bass.ds(r * TILES, TILES), :]).then_inc(stored, 16)
            sp.wait_ge(stored, B * 16)

        @block.gpsimd
        def _(pool):
            for s, n in CREDITS.items():
                pool.sem_inc(s, n)
            pool.memset(pick[:, :, :], 0.0).then_inc(consts, 1)
            pool.wait_ge(consts, 1)
            for a in range(2):
                for base, fill in ((0, W_SCALE), (E, W_SCALE / LOW)):
                    view = pick[:, :, a]
                    pool.affine_select(out=view, in_=view, compare_op=ALU.not_equal, fill=fill, base=-base - a,
                                       pattern=[[-2, ET]], channel_multiplier=1).then_inc(consts, 1)
                    pool.wait_ge(consts, 2 + 2 * a + (1 if base else 0))

            def step(r, pre, main, post):
                def split_h():
                    b = r + 1
                    pool.wait_ge(hT_ready, 2 * b + 2)
                    pool.tensor_tensor(hTl[:, b % 2, :], hT[:, :], hTh[:, b % 2, :], ALU.subtract).then_inc(hT_split, 1)

                def split_hidden(r, T):
                    pool.wait_ge(hid_rounded, r * SLOTS + T + 1)
                    pool.tensor_tensor(hid_l[:, place(T), :], hid[:, place(T), :], hid_h[:, place(T), :], ALU.subtract).then_inc(split_ready, 1)

                if main:
                    for T in range(SLOTS):
                        if T:
                            split_hidden(r, T - 1)
                        elif post:
                            split_hidden(r - 1, SLOTS - 1)
                        if pre and T == 10:
                            split_h()
                elif pre:
                    split_h()
                else:
                    split_hidden(r - 1, SLOTS - 1)

            rounds(pool, step)

        @block.tensor
        def _(pe):
            pe.wait_ge(loaded, LOADS)
            pe.wait_ge(k.w_rounded, W_CHUNKS)
            pe.wait_ge(k.w_ready, W_CHUNKS)
            pe.transpose(preb[:, 0:E], cent[:, :], k.ident[0:E, 0:E]).then_inc(cent_psum, 1)
            pe.wait_ge(cent_ready, 1)

            def step(r, pre, main, post):
                b = r + 1

                def pre_turn():
                    pe.wait_ge(xn_ready, b + 1)
                    pe.wait_ge(low_read, b + 1)
                    for c in range(TILES):
                        mm = pe.transpose(preb[:, c * P:(c + 1) * P], xn[:, c, :], k.ident[:, :])
                    mm.then_inc(xT_done, 1)

                def route():
                    pe.wait_ge(hT_ready, 2 * b + 2)
                    if main:
                        pe.wait_ge(sig_ready, b)
                    pe.wait_ge(biased_ready, b + 1)
                    for c in range(TILES):
                        mm = pe.matmul(routeb[:, c * E:(c + 1) * E], hT[:, c * P:(c + 1) * P], centT[:, :], start=True, stop=True)
                    mm.then_inc(aff_done, 1)

                def turn_weights():
                    pe.wait_ge(cw_ready, b + 1)
                    for c in range(TILES):
                        mm = pe.transpose(preb[:, c * P:(c + 1) * P], cw[:, c, :, :].rearrange("p a e -> p (a e)"), k.ident[:, :])
                    mm.then_inc(cwT_done, 1)

                def product(to, w, high, low, start, stop):
                    pe.matmul(to, w[0], high, start=start, stop=False, skip_group_check=True)
                    pe.matmul(to, w[0], low, start=False, stop=False, skip_group_check=True)
                    return pe.matmul(to, w[1], high, start=False, stop=stop, skip_group_check=True)

                def weights(j, T):
                    return k.w_high[:, j, T * P:(T + 1) * P], k.w_low[:, j, T * P:(T + 1) * P]

                def down(r, T):
                    pe.wait_ge(split_ready, r * SLOTS + T + 1 + RING)
                    if T == 0:
                        pe.wait_ge(yg_ready, r + 1)
                    product(yb[:, :], weights(1, T), hid_h[:, place(T), :], hid_l[:, place(T), :], T == 0, T == ET).then_inc(down_done, 1)

                def turn_back():
                    pe.wait_ge(yg_ready, r + 1)
                    pe.wait_ge(x_ready, r)
                    for c in range(TILES):
                        mm = pe.transpose(postb[:, c * P:(c + 1) * P], yg[:, c * P:(c + 1) * P], k.ident[:, :])
                    mm.then_inc(turned, 1)

                if main and not post:
                    pe.wait_ge(sel_ready, 1)
                if main:
                    pe.wait_ge(parts_ready, r + 3)
                    pe.wait_ge(hT_split, r + 1)
                    for T in range(SLOTS):
                        q = r * SLOTS + T
                        pe.wait_ge(silu_ready, free(q, T, bank))
                        product(ub[bank(T)][:, :], weights(0, T), hTh[:, r % 2, :], hTl[:, r % 2, :], True, True).then_inc(u_done, 1)
                        if T < ET:
                            pe.wait_ge(hid_ready, free(q, T, bank))
                            pe.matmul(cb[bank(T)][:, :], sel[:, T, :], parts[:, r % 2, :], start=True, stop=True).then_inc(c_done, 1)
                        if pre:
                            for at, f in ((3, pre_turn), (7, route), (20, turn_weights)):
                                if T == at:
                                    f()
                        if T >= DOWN_LAG:
                            down(r, T - DOWN_LAG)
                        elif post:
                            down(r - 1, T - DOWN_LAG + SLOTS)
                        if post and T == DOWN_LAG + 2:
                            turn_back()
                elif pre:
                    pre_turn(), route(), turn_weights()
                else:
                    for T in range(SLOTS - DOWN_LAG, SLOTS):
                        down(r - 1, T)
                    turn_back()

            rounds(pe, step)

        @block.scalar
        def _(act):
            act.wait_ge(gate_ready, 1)
            act.wait_ge(cent_psum, 1)
            act.activation(centT[:, :], preb[:, 0:E], ACT.Copy).then_inc(cent_ready, 1)
            act.wait_ge(cent_ready, 1)
            act.wait_ge(consts, 5)
            act.activation(sel[:, :, :].rearrange("p t (a f) -> p t a f", a=2), pick[:, :, :].unsqueeze(3).broadcast_to([P, ET, 2, EF]),
                           ACT.Copy).then_inc(sel_ready, 1)

            def step(r, pre, main, post):
                b = r + 1

                def pre_h():
                    act.wait_ge(xT_done, b + 1)
                    if main:
                        act.wait_ge(hT_split, b)
                    act.wait_ge(aff_done, b + 1)
                    for to in (hT[:, :], hTh[:, b % 2, :]):
                        act.activation(to, preb[:, :], ACT.Identity, scale=k.mod[:, 1, 4, bass.ds(b, 1)],
                                       bias=k.mod[:, 1, 3, bass.ds(b, 1)]).then_inc(hT_ready, 1)

                def sigmoid():
                    if main:
                        act.wait_ge(cw_ready, b)
                    act.wait_ge(biased_ready, b + 2)
                    act.activation(sig[:, :, :].rearrange("p c e -> p (c e)"), routeb[:, 0:TILES * E], ACT.Sigmoid).then_inc(sig_ready, 1)

                def high():
                    act.wait_ge(cwT_done, b + 2)
                    act.wait_ge(parts_ready, b + 2)
                    act.activation(parts[:, b % 2, :], preb[:, :], ACT.Copy).then_inc(high_ready, 1)

                def round_hidden(r, T):
                    q = r * SLOTS + T
                    act.wait_ge(hid_ready, q + 1 + RING)
                    act.wait_ge(down_done, free(q, T, place))
                    act.activation(hid_h[:, place(T), :], hid[:, place(T), :], ACT.Copy).then_inc(hid_rounded, 1)

                def gate_result():
                    act.wait_ge(down_done, r * SLOTS + RING)
                    act.wait_ge(turned, r)
                    act.activation(yg[:, :], yb[:, :], ACT.Copy, scale=gate[:, bass.ds(r - 1, 1)]).then_inc(yg_ready, 1)

                if main:
                    for T in range(SLOTS):
                        q = r * SLOTS + T
                        if post and T == DOWN_LAG:
                            gate_result()
                        act.wait_ge(u_done, q + 1)
                        act.wait_ge(hid_ready, free(q, T, bank))
                        act.activation(act_u[:, bank(T), :], ub[bank(T)][:, :], ACT.Silu, scale=1.0 / W_SCALE).then_inc(silu_ready, 1)
                        if T:
                            round_hidden(r, T - 1)
                        elif post:
                            round_hidden(r - 1, SLOTS - 1)
                        if pre:
                            for at, f in ((4, pre_h), (10, sigmoid), (21, high)):
                                if T == at:
                                    f()
                elif pre:
                    pre_h(), sigmoid(), high()
                else:
                    round_hidden(r - 1, SLOTS - 1)
                    gate_result()

            rounds(act, step)

        @block.vector
        def _(dve):
            setup_link = Chain(dve, dve_setup).link
            token_stats(dve, setup_link, k, range(1))
            dve.tensor_scalar(gate[:, :], k.mod[:, 1, 5, :], W_SCALE ** -2, None, ALU.mult).then_inc(gate_ready, 1)
            dve.wait_ge(loaded, LOADS)

            def step(r, pre, main, post):
                b = r + 1
                link = Chain(dve, dve_pre, b * PRE_LINKS).link

                def pre_norm():
                    for c in range(TILES):
                        ins = normalize(dve, k, xn[:, c, :], b * TILES + c)
                    ins.then_inc(xn_ready, 1)

                def bias():
                    dve.wait_ge(aff_done, b + 2)
                    dve.tensor_tensor(biased[:, :, :], routeb[:, 0:TILES * E].rearrange("p (c e) -> p c e", c=TILES),
                                      ebias[:, :].unsqueeze(1).broadcast_to([P, TILES, E]), ALU.add).then_inc(biased_ready, 1)

                def largest():
                    dve.wait_ge(loaded, LOADS)
                    dve.wait_ge(biased_ready, b + 2)
                    for c in range(TILES):
                        ins = dve.max(top[:, c, :], biased[:, c, :])
                    ins.then_inc(top_ready, 1)

                def strike():
                    dve.wait_ge(loaded, LOADS)
                    dve.wait_ge(top_ready, b + 2)
                    for c in range(TILES):
                        ins = dve.match_replace(rest[:, c, :], top[:, c, :], biased[:, c, :], NEG)
                    link(ins)

                def mask():
                    link(dve.tensor_tensor(rest[:, :, :], rest[:, :, :], biased[:, :, :], ALU.not_equal))

                def chosen():
                    dve.wait_ge(sig_ready, b + 1)
                    link(dve.tensor_tensor(rest[:, :, :], rest[:, :, :], sig[:, :, :], ALU.mult))

                def total():
                    link(dve.tensor_reduce(wsum[:, :], rest[:, :, :], AX, ALU.add))
                    link(dve.tensor_scalar(wsum[:, :], wsum[:, :], 1e-8, None, ALU.add))
                    link(dve.reciprocal(wsum[:, :], wsum[:, :]))

                def share():
                    link(dve.tensor_tensor(rest[:, :, :], rest[:, :, :], wsum[:, :].unsqueeze(2).broadcast_to([P, TILES, E]), ALU.mult))

                def double():
                    dve.wait_ge(cwT_done, b + 1)
                    dve.tensor_copy(cw[:, :, :, :], rest[:, :, :].unsqueeze(2).broadcast_to([P, TILES, 2, E])).then_inc(cw_ready, 1)

                steps = ((0, pre_norm), (9, bias), (10, largest), (11, strike), (12, mask), (13, chosen), (14, total), (15, share), (16, double))
                def split():
                    dve.wait_ge(high_ready, b + 1)
                    lo = parts[E:2 * E, b % 2, :]
                    dve.tensor_tensor(low[E:2 * E, :], preb[E:2 * E, :], lo, ALU.subtract).then_inc(low_read, 1)
                    dve.wait_ge(low_read, b + 2)
                    dve.tensor_scalar(lo, low[E:2 * E, :], LOW, None, ALU.mult).then_inc(parts_ready, 1)

                def residual():
                    dve.wait_ge(turned, r + 1)
                    x = k.x[:, bass.ds((r - 1) * TILES, TILES), :]
                    dve.tensor_tensor(x, x, postb[:, :].rearrange("p (c n) -> p c n", c=TILES), ALU.add).then_inc(x_ready, 1)

                if main:
                    for T in range(SLOTS):
                        q = r * SLOTS + T
                        dve.wait_ge(silu_ready, q + 1 + RING)
                        dve.wait_ge(split_ready, free(q, T, place))
                        if T < ET:
                            dve.wait_ge(c_done, r * ET + T + 1)
                            dve.tensor_tensor(hid[:, place(T), :], act_u[:, bank(T), :], cb[bank(T)][:, :], ALU.mult).then_inc(hid_ready, 1)
                        else:
                            dve.tensor_scalar(hid[:, place(T), :], act_u[:, bank(T), :], W_SCALE, None, ALU.mult).then_inc(hid_ready, 1)
                        if post and T == DOWN_LAG + 4:
                            residual()
                        if pre:
                            for at, f in (*steps, (21, split)):
                                if T == at:
                                    f()
                elif pre:
                    for n, (_, f) in enumerate(steps):
                        f()
                        if n == 0:
                            token_stats(dve, setup_link, k, range(1, B))
                    split()
                else:
                    residual()

            rounds(dve, step)


def kernel(**inputs):
    import concourse.bacc as bacc
    from concourse.bass_utils import run_bass_kernel_spmd

    nc = bacc.Bacc("TRN2", target_bir_lowering=False, num_devices=1)
    arrays = {name: np.ascontiguousarray(a) for name, a in inputs.items()}
    d = {name: nc.dram_tensor(name, a.shape, mybir.dt.from_np(a.dtype), kind="ExternalInput").ap() for name, a in arrays.items()}
    out = nc.dram_tensor("out_0_dram", (B, S, D), F32, kind="ExternalOutput").ap()
    build(nc, d, out)
    r = run_bass_kernel_spmd(nc, [arrays], core_ids=[0])
    return r.results[0]["out_0_dram"]
```
